# Optimizing a Trainium2 kernel written in Bass

```python
import numpy as np
import jax
import jax.numpy as jnp

def _softmax(x, axis=-1):
    return jax.nn.softmax(x, axis=axis)

def _gelu(x):
    return jax.nn.gelu(x, approximate=True)

def _silu(x):
    return jax.nn.silu(x)

def _sigmoid(x):
    return jax.nn.sigmoid(x)

def _layernorm(x, axis=-1, eps=1e-05):
    m = jnp.mean(x, axis=axis, keepdims=True)
    v = jnp.var(x, axis=axis, keepdims=True)
    return (x - m) / jnp.sqrt(v + eps)

def _scatter_add(tgt, idx, src, axis=0):
    return tgt.at[idx].add(src)

def _segment_sum(src, seg, n):
    return jax.ops.segment_sum(src, seg, n)
kernel_name = 'mk_hybrid_d2_jaxref_r8_2f08df'

def setup_inputs(seed: int=0):
    np.random.seed(seed)
    _w = jnp.asarray

    def _L0_attn_a_setup():
        import jax, jax.numpy as jnp
        import numpy as np
        import math
        HIDDEN = 256
        HEADS = 16
        HEAD_DIM = HIDDEN // HEADS
        SEQ = 256
        BATCH = 1
        THRESH = 0.7
        key = jax.random.key(seed)
        ks = jax.random.split(key, 9)
        init = lambda k, shape: jax.random.normal(k, shape, dtype=jnp.float32) * 0.02
        return {'hidden_states': jax.random.normal(ks[0], (BATCH, SEQ, HIDDEN), dtype=jnp.float32), 'Wq': init(ks[1], (HIDDEN, HIDDEN)), 'bq': jnp.zeros((HIDDEN,), jnp.float32), 'Wk': init(ks[2], (HIDDEN, HIDDEN)), 'bk': jnp.zeros((HIDDEN,), jnp.float32), 'Wv': init(ks[3], (HIDDEN, HIDDEN)), 'bv': jnp.zeros((HIDDEN,), jnp.float32), 'Wo': init(ks[4], (HIDDEN, HIDDEN)), 'bo': jnp.zeros((HIDDEN,), jnp.float32), 'truth_gate': jnp.full((1,), THRESH, jnp.float32), 'balance_gate': jnp.full((1,), THRESH, jnp.float32), 'order_gate': jnp.full((1,), THRESH, jnp.float32), 'justice_gate': jnp.full((1,), THRESH, jnp.float32), 'harmony_gate': jnp.full((1,), THRESH, jnp.float32)}
    _L0_attn_a_in = _L0_attn_a_setup()

    def _L0_attn_b_setup():
        import jax, jax.numpy as jnp
        import numpy as np
        B, T, HIDDEN = (2, 512, 256)
        NUM_HEADS, HEAD_K, HEAD_V = (6, 32, 64)
        KEY_DIM, VALUE_DIM = (NUM_HEADS * HEAD_K, NUM_HEADS * HEAD_V)
        CONV_K, CHUNK, EPS = (4, 64, 1e-05)

        def short_conv(x, w):
            K = w.shape[1]
            xp = jnp.pad(x, ((0, 0), (K - 1, 0), (0, 0)))
            y = sum((xp[:, i:i + x.shape[1], :] * w[:, i] for i in range(K)))
            return jax.nn.silu(y)

        def l2norm(x):
            return x * jax.lax.rsqrt(jnp.sum(x * x, -1, keepdims=True))

        def _step(S, xs):
            qt, kt, vt, gt, bt = xs
            S = S * jnp.exp(gt)[..., None, None]
            pred = jnp.einsum('bhk,bhkv->bhv', kt, S)
            delta = (vt - pred) * bt[..., None]
            S = S + jnp.einsum('bhk,bhv->bhkv', kt, delta)
            return (S, jnp.einsum('bhk,bhkv->bhv', qt, S))

        def _chunk(S, xs):
            return jax.lax.scan(_step, S, xs)
        _chunk_ckpt = jax.checkpoint(_chunk)

        def gated_delta_rule(q, k, v, g, beta):
            b, t, h, dk = q.shape
            dv = v.shape[-1]
            q = l2norm(q) * dk ** (-0.5)
            k = l2norm(k)
            nc = t // CHUNK

            def to_scan(x):
                x = x.reshape(b, nc, CHUNK, *x.shape[2:])
                return jnp.moveaxis(x, 0, 2)
            xs = tuple(map(to_scan, (q, k, v, g, beta)))
            S0 = jnp.zeros((b, h, dk, dv), q.dtype)
            _, o = jax.lax.scan(_chunk_ckpt, S0, xs)
            return jnp.moveaxis(o, 2, 0).reshape(b, t, h, dv)
        key = jax.random.key(seed)
        ks = jax.random.split(key, 14)

        def lin(k, fi, fo):
            return jax.random.normal(k, (fi, fo), jnp.float32) / np.sqrt(fi)
        A = jax.random.uniform(ks[11], (NUM_HEADS,), minval=0.001, maxval=16.0)
        dt = jnp.exp(jax.random.uniform(ks[12], (NUM_HEADS,)) * (np.log(0.1) - np.log(0.001)) + np.log(0.001))
        dt = jnp.clip(dt, 0.0001)
        return {'hidden_states': jax.random.normal(ks[0], (B, T, HIDDEN), jnp.float32), 'Wq': lin(ks[1], HIDDEN, KEY_DIM), 'Wk': lin(ks[2], HIDDEN, KEY_DIM), 'Wv': lin(ks[3], HIDDEN, VALUE_DIM), 'Wa': lin(ks[4], HIDDEN, NUM_HEADS), 'Wb': lin(ks[5], HIDDEN, NUM_HEADS), 'Wg': lin(ks[6], HIDDEN, VALUE_DIM), 'Wo': lin(ks[7], VALUE_DIM, HIDDEN), 'conv_wq': jax.random.normal(ks[8], (KEY_DIM, CONV_K), jnp.float32) / np.sqrt(CONV_K), 'conv_wk': jax.random.normal(ks[9], (KEY_DIM, CONV_K), jnp.float32) / np.sqrt(CONV_K), 'conv_wv': jax.random.normal(ks[10], (VALUE_DIM, CONV_K), jnp.float32) / np.sqrt(CONV_K), 'A_log': jnp.log(A), 'dt_bias': dt + jnp.log(-jnp.expm1(-dt)), 'norm_weight': jnp.ones((HEAD_V,), jnp.float32)}
    _L0_attn_b_in = _L0_attn_b_setup()

    def _L0_ffn_setup():
        import jax, jax.numpy as jnp
        import numpy as np
        D_MODEL = 256
        D_EXPERT = 1024
        EPS = 1e-08

        def ternary_quant(w):
            scale = jnp.mean(jnp.abs(w)) + EPS
            q = jnp.clip(jnp.round(w / scale), -1.0, 1.0) * scale
            return w + jax.lax.stop_gradient(q - w)
        key = jax.random.key(seed)
        k_x, k_up, k_gate, k_down = jax.random.split(key, 4)
        std_in = 1.0 / np.sqrt(D_MODEL)
        std_exp = 1.0 / np.sqrt(D_EXPERT)
        return {'x': jax.random.normal(k_x, (4, 256, D_MODEL), dtype=jnp.float32), 'W_up': jax.random.normal(k_up, (D_EXPERT, D_MODEL), dtype=jnp.float32) * std_in, 'W_gate': jax.random.normal(k_gate, (D_EXPERT, D_MODEL), dtype=jnp.float32) * std_in, 'W_down': jax.random.normal(k_down, (D_MODEL, D_EXPERT), dtype=jnp.float32) * std_exp}
    _L0_ffn_in = _L0_ffn_setup()

    def _L1_attn_a_setup():
        import jax, jax.numpy as jnp
        import numpy as np
        B, SQ, H = (2, 256, 256)
        NH = 16
        HN = H // NH
        key = jax.random.key(seed)
        ks = jax.random.split(key, 6)
        query = jax.random.normal(ks[0], (B, SQ, H), dtype=jnp.float32)
        k_in = jax.random.normal(ks[1], (B, SQ, H), dtype=jnp.float32)
        v_in = jax.random.normal(ks[2], (B, SQ, H), dtype=jnp.float32)
        Wqkv = jax.random.normal(ks[3], (3 * H, H), dtype=jnp.float32) * (1.0 / np.sqrt(H))
        Wproj = jax.random.normal(ks[4], (H, H), dtype=jnp.float32) * (1.0 / np.sqrt(H))
        bproj = jnp.zeros((H,), dtype=jnp.float32)
        return {'query': query, 'key': k_in, 'value': v_in, 'Wqkv': Wqkv, 'Wproj': Wproj, 'bproj': bproj}
    _L1_attn_a_in = _L1_attn_a_setup()

    def _L1_attn_b_setup():
        import jax, jax.numpy as jnp
        import numpy as np
        B, T, D = (2, 256, 256)
        H, LAT, RD = (16, 64, 64)
        HD = D // H

        def _rope_tables(rd, max_t, theta=10000.0):
            freqs = 1.0 / theta ** (np.arange(0, rd, 2, dtype=np.float32) / rd)
            t = np.arange(max_t, dtype=np.float32)
            ang = np.outer(t, freqs)
            cos = np.tile(np.cos(ang), (1, 2))
            sin = np.tile(np.sin(ang), (1, 2))
            return (jnp.asarray(cos), jnp.asarray(sin))

        def _rotate_half(x):
            d = x.shape[-1] // 2
            return jnp.concatenate([-x[..., d:], x[..., :d]], axis=-1)

        def _apply_rope(x, cos, sin):
            t = x.shape[2]
            return x * cos[:t][None, None] + _rotate_half(x) * sin[:t][None, None]
        key = jax.random.key(seed)
        ks = jax.random.split(key, 9)
        s = 0.02
        return {'x': jax.random.normal(ks[0], (B, T, D), jnp.float32), 'Wqd': jax.random.normal(ks[1], (D, LAT), jnp.float32) * s, 'Wqu': jax.random.normal(ks[2], (LAT, D), jnp.float32) * s, 'Wqr': jax.random.normal(ks[3], (LAT, H * RD), jnp.float32) * s, 'Wkvd': jax.random.normal(ks[4], (D, LAT), jnp.float32) * s, 'Wku': jax.random.normal(ks[5], (LAT, D), jnp.float32) * s, 'Wvu': jax.random.normal(ks[6], (LAT, D), jnp.float32) * s, 'Wkr': jax.random.normal(ks[7], (D, RD), jnp.float32) * s, 'Wo': jax.random.normal(ks[8], (D, D), jnp.float32) * s}
    _L1_attn_b_in = _L1_attn_b_setup()

    def _L1_ffn_setup():
        import jax, jax.numpy as jnp
        import numpy as np
        NUM_EXPERTS = 8
        TOP_K = 2
        LORA_ALPHA = 2.0
        LORA_RANK = 16
        D_MODEL = 256
        D_HIDDEN = 704
        key = jax.random.key(seed)
        ks = jax.random.split(key, 11)
        B, S, D, H, E, R = (2, 128, D_MODEL, D_HIDDEN, NUM_EXPERTS, LORA_RANK)
        sd = 1.0 / np.sqrt(D)
        sh = 1.0 / np.sqrt(H)
        x = jax.random.normal(ks[0], (B, S, D), jnp.float32)
        gate_w = jax.random.normal(ks[1], (E, D), jnp.float32) * sd
        w_up = jax.random.normal(ks[2], (H, D), jnp.float32) * sd
        w_gate = jax.random.normal(ks[3], (H, D), jnp.float32) * sd
        w_down = jax.random.normal(ks[4], (D, H), jnp.float32) * sh
        up_A = jax.random.normal(ks[5], (E, R, D), jnp.float32) * sd
        up_B = jax.random.normal(ks[6], (E, H, R), jnp.float32) * 0.02
        gate_A = jax.random.normal(ks[7], (E, R, D), jnp.float32) * sd
        gate_B = jax.random.normal(ks[8], (E, H, R), jnp.float32) * 0.02
        down_A = jax.random.normal(ks[9], (E, R, H), jnp.float32) * sh
        down_B = jax.random.normal(ks[10], (E, D, R), jnp.float32) * 0.02
        return {'x': x, 'gate_w': gate_w, 'w_up': w_up, 'w_gate': w_gate, 'w_down': w_down, 'up_A': up_A, 'up_B': up_B, 'gate_A': gate_A, 'gate_B': gate_B, 'down_A': down_A, 'down_B': down_B}
    _L1_ffn_in = _L1_ffn_setup()
    _d = {'L0_attn_a_hidden_states': _L0_attn_a_in['hidden_states'], 'L0_attn_a_Wq': _L0_attn_a_in['Wq'], 'L0_attn_a_bq': _L0_attn_a_in['bq'], 'L0_attn_a_Wk': _L0_attn_a_in['Wk'], 'L0_attn_a_bk': _L0_attn_a_in['bk'], 'L0_attn_a_Wv': _L0_attn_a_in['Wv'], 'L0_attn_a_bv': _L0_attn_a_in['bv'], 'L0_attn_a_Wo': _L0_attn_a_in['Wo'], 'L0_attn_a_bo': _L0_attn_a_in['bo'], 'L0_attn_a_truth_gate': _L0_attn_a_in['truth_gate'], 'L0_attn_a_balance_gate': _L0_attn_a_in['balance_gate'], 'L0_attn_a_order_gate': _L0_attn_a_in['order_gate'], 'L0_attn_a_justice_gate': _L0_attn_a_in['justice_gate'], 'L0_attn_a_harmony_gate': _L0_attn_a_in['harmony_gate'], 'L0_attn_b_Wq': _L0_attn_b_in['Wq'], 'L0_attn_b_Wk': _L0_attn_b_in['Wk'], 'L0_attn_b_Wv': _L0_attn_b_in['Wv'], 'L0_attn_b_Wa': _L0_attn_b_in['Wa'], 'L0_attn_b_Wb': _L0_attn_b_in['Wb'], 'L0_attn_b_Wg': _L0_attn_b_in['Wg'], 'L0_attn_b_Wo': _L0_attn_b_in['Wo'], 'L0_attn_b_conv_wq': _L0_attn_b_in['conv_wq'], 'L0_attn_b_conv_wk': _L0_attn_b_in['conv_wk'], 'L0_attn_b_conv_wv': _L0_attn_b_in['conv_wv'], 'L0_attn_b_A_log': _L0_attn_b_in['A_log'], 'L0_attn_b_dt_bias': _L0_attn_b_in['dt_bias'], 'L0_attn_b_norm_weight': _L0_attn_b_in['norm_weight'], 'L0_ffn_W_up': _L0_ffn_in['W_up'], 'L0_ffn_W_gate': _L0_ffn_in['W_gate'], 'L0_ffn_W_down': _L0_ffn_in['W_down'], 'L1_attn_a_key': _L1_attn_a_in['key'], 'L1_attn_a_value': _L1_attn_a_in['value'], 'L1_attn_a_Wqkv': _L1_attn_a_in['Wqkv'], 'L1_attn_a_Wproj': _L1_attn_a_in['Wproj'], 'L1_attn_a_bproj': _L1_attn_a_in['bproj'], 'L1_attn_b_Wqd': _L1_attn_b_in['Wqd'], 'L1_attn_b_Wqu': _L1_attn_b_in['Wqu'], 'L1_attn_b_Wqr': _L1_attn_b_in['Wqr'], 'L1_attn_b_Wkvd': _L1_attn_b_in['Wkvd'], 'L1_attn_b_Wku': _L1_attn_b_in['Wku'], 'L1_attn_b_Wvu': _L1_attn_b_in['Wvu'], 'L1_attn_b_Wkr': _L1_attn_b_in['Wkr'], 'L1_attn_b_Wo': _L1_attn_b_in['Wo'], 'L1_ffn_gate_w': _L1_ffn_in['gate_w'], 'L1_ffn_w_up': _L1_ffn_in['w_up'], 'L1_ffn_w_gate': _L1_ffn_in['w_gate'], 'L1_ffn_w_down': _L1_ffn_in['w_down'], 'L1_ffn_up_A': _L1_ffn_in['up_A'], 'L1_ffn_up_B': _L1_ffn_in['up_B'], 'L1_ffn_gate_A': _L1_ffn_in['gate_A'], 'L1_ffn_gate_B': _L1_ffn_in['gate_B'], 'L1_ffn_down_A': _L1_ffn_in['down_A'], 'L1_ffn_down_B': _L1_ffn_in['down_B']}
    _x0 = _d['L0_attn_a_hidden_states']
    _d['L0_attn_a_hidden_states'] = jax.random.normal(jax.random.fold_in(jax.random.key(seed), 1), (1, 1024, 256), dtype=_x0.dtype)
    del _x0
    return _d

def reference(L0_attn_a_hidden_states, L0_attn_a_Wq, L0_attn_a_bq, L0_attn_a_Wk, L0_attn_a_bk, L0_attn_a_Wv, L0_attn_a_bv, L0_attn_a_Wo, L0_attn_a_bo, L0_attn_a_truth_gate, L0_attn_a_balance_gate, L0_attn_a_order_gate, L0_attn_a_justice_gate, L0_attn_a_harmony_gate, L0_attn_b_Wq, L0_attn_b_Wk, L0_attn_b_Wv, L0_attn_b_Wa, L0_attn_b_Wb, L0_attn_b_Wg, L0_attn_b_Wo, L0_attn_b_conv_wq, L0_attn_b_conv_wk, L0_attn_b_conv_wv, L0_attn_b_A_log, L0_attn_b_dt_bias, L0_attn_b_norm_weight, L0_ffn_W_up, L0_ffn_W_gate, L0_ffn_W_down, L1_attn_a_key, L1_attn_a_value, L1_attn_a_Wqkv, L1_attn_a_Wproj, L1_attn_a_bproj, L1_attn_b_Wqd, L1_attn_b_Wqu, L1_attn_b_Wqr, L1_attn_b_Wkvd, L1_attn_b_Wku, L1_attn_b_Wvu, L1_attn_b_Wkr, L1_attn_b_Wo, L1_ffn_gate_w, L1_ffn_w_up, L1_ffn_w_gate, L1_ffn_w_down, L1_ffn_up_A, L1_ffn_up_B, L1_ffn_gate_A, L1_ffn_gate_B, L1_ffn_down_A, L1_ffn_down_B):

    def _L0_attn_a_ref(hidden_states, Wq, bq, Wk, bk, Wv, bv, Wo, bo, truth_gate, balance_gate, order_gate, justice_gate, harmony_gate):
        import jax, jax.numpy as jnp
        import numpy as np
        import math
        HIDDEN = 256
        HEADS = 16
        HEAD_DIM = HIDDEN // HEADS
        SEQ = 256
        BATCH = 1
        THRESH = 0.7
        B, S, D = hidden_states.shape
        H, hd = (HEADS, HEAD_DIM)

        def proj(W, b):
            return (hidden_states @ W.T + b).reshape(B, S, H, hd).transpose(0, 2, 1, 3)
        q, k, v = (proj(Wq, bq), proj(Wk, bk), proj(Wv, bv))
        scores = jnp.einsum('bhqd,bhkd->bhqk', q, k) / math.sqrt(hd)
        truth_penalty = jax.nn.sigmoid(truth_gate) * (jnp.linalg.norm(k, axis=-1, keepdims=True) * 0.01)
        logp = jax.nn.log_softmax(scores, axis=-1)
        entropy = -jnp.sum(jnp.exp(logp) * logp, axis=-1, keepdims=True)
        balance_adjustment = jax.nn.sigmoid(balance_gate) * (entropy / math.log(S) * 0.1)
        position_bias = jnp.arange(S, dtype=jnp.float32) / S
        order_bonus = jax.nn.sigmoid(order_gate) * (position_bias * 0.05)
        mean_score = scores.mean(axis=-1, keepdims=True)
        justice_adjustment = jax.nn.sigmoid(justice_gate) * ((mean_score - scores) * 0.1)
        smoothness = -jnp.abs(scores[..., 1:] - scores[..., :-1]).mean(axis=-1, keepdims=True)
        harmony_smooth = jax.nn.sigmoid(harmony_gate) * (smoothness * 0.1)
        scores = scores - truth_penalty + balance_adjustment + order_bonus + justice_adjustment + harmony_smooth
        attn = jax.nn.softmax(scores, axis=-1)
        out = jnp.einsum('bhqk,bhkd->bhqd', attn, v)
        out = out.transpose(0, 2, 1, 3).reshape(B, S, D)
        return out @ Wo.T + bo

    def _L0_attn_b_ref(hidden_states, Wq, Wk, Wv, Wa, Wb, Wg, Wo, conv_wq, conv_wk, conv_wv, A_log, dt_bias, norm_weight):
        import jax, jax.numpy as jnp
        import numpy as np
        B, T, HIDDEN = (2, 512, 256)
        NUM_HEADS, HEAD_K, HEAD_V = (6, 32, 64)
        KEY_DIM, VALUE_DIM = (NUM_HEADS * HEAD_K, NUM_HEADS * HEAD_V)
        CONV_K, CHUNK, EPS = (4, 64, 1e-05)

        def short_conv(x, w):
            K = w.shape[1]
            xp = jnp.pad(x, ((0, 0), (K - 1, 0), (0, 0)))
            y = sum((xp[:, i:i + x.shape[1], :] * w[:, i] for i in range(K)))
            return jax.nn.silu(y)

        def l2norm(x):
            return x * jax.lax.rsqrt(jnp.sum(x * x, -1, keepdims=True))

        def _step(S, xs):
            qt, kt, vt, gt, bt = xs
            S = S * jnp.exp(gt)[..., None, None]
            pred = jnp.einsum('bhk,bhkv->bhv', kt, S)
            delta = (vt - pred) * bt[..., None]
            S = S + jnp.einsum('bhk,bhv->bhkv', kt, delta)
            return (S, jnp.einsum('bhk,bhkv->bhv', qt, S))

        def _chunk(S, xs):
            return jax.lax.scan(_step, S, xs)
        _chunk_ckpt = jax.checkpoint(_chunk)

        def gated_delta_rule(q, k, v, g, beta):
            b, t, h, dk = q.shape
            dv = v.shape[-1]
            q = l2norm(q) * dk ** (-0.5)
            k = l2norm(k)
            nc = t // CHUNK

            def to_scan(x):
                x = x.reshape(b, nc, CHUNK, *x.shape[2:])
                return jnp.moveaxis(x, 0, 2)
            xs = tuple(map(to_scan, (q, k, v, g, beta)))
            S0 = jnp.zeros((b, h, dk, dv), q.dtype)
            _, o = jax.lax.scan(_chunk_ckpt, S0, xs)
            return jnp.moveaxis(o, 2, 0).reshape(b, t, h, dv)
        b, t, _ = hidden_states.shape
        q = short_conv(hidden_states @ Wq, conv_wq).reshape(b, t, NUM_HEADS, HEAD_K)
        k = short_conv(hidden_states @ Wk, conv_wk).reshape(b, t, NUM_HEADS, HEAD_K)
        v = short_conv(hidden_states @ Wv, conv_wv).reshape(b, t, NUM_HEADS, HEAD_V)
        beta = jax.nn.sigmoid(hidden_states @ Wb)
        g = -jnp.exp(A_log) * jax.nn.softplus(hidden_states @ Wa + dt_bias)
        o = gated_delta_rule(q, k, v, g, beta)
        gate = (hidden_states @ Wg).reshape(b, t, NUM_HEADS, HEAD_V)
        o = o * jax.lax.rsqrt(jnp.mean(o * o, -1, keepdims=True) + EPS) * norm_weight
        o = o * jax.nn.silu(gate)
        return o.reshape(b, t, VALUE_DIM) @ Wo

    def _L0_ffn_ref(x, W_up, W_gate, W_down):
        import jax, jax.numpy as jnp
        import numpy as np
        D_MODEL = 256
        D_EXPERT = 1024
        EPS = 1e-08

        def ternary_quant(w):
            scale = jnp.mean(jnp.abs(w)) + EPS
            q = jnp.clip(jnp.round(w / scale), -1.0, 1.0) * scale
            return w + jax.lax.stop_gradient(q - w)
        wu = ternary_quant(W_up)
        wg = ternary_quant(W_gate)
        wd = ternary_quant(W_down)
        up = jnp.einsum('bsd,ed->bse', x, wu)
        gate = jnp.einsum('bsd,ed->bse', x, wg)
        hidden = jax.nn.silu(up) * gate
        return jnp.einsum('bse,de->bsd', hidden, wd)

    def _L1_attn_a_ref(query, key, value, Wqkv, Wproj, bproj):
        import jax, jax.numpy as jnp
        import numpy as np
        B, SQ, H = (2, 256, 256)
        NH = 16
        HN = H // NH
        b, sq, h = query.shape
        nh, hn = (NH, HN)
        norm = 1.0 / jnp.sqrt(jnp.asarray(hn, query.dtype))
        x = jnp.transpose(query, (1, 0, 2)).reshape(sq * b, h)
        mixed = x @ Wqkv.T
        mixed = mixed.reshape(sq, b, nh, 3, hn)
        q = mixed[..., 0, :]
        k = mixed[..., 1, :]
        v = mixed[..., 2, :]
        q = q.reshape(sq, b * nh, hn).transpose(1, 0, 2)
        k = k.reshape(sq, b * nh, hn).transpose(1, 0, 2)
        v = v.reshape(sq, b * nh, hn).transpose(1, 0, 2)
        attn = jnp.einsum('gqd,gkd->gqk', q, k) * norm
        attn = jax.nn.softmax(attn, axis=-1)
        ctx = jnp.einsum('gqk,gkd->gqd', attn, v)
        ctx = ctx.reshape(nh, b, sq, hn)
        ctx = jnp.transpose(ctx, (2, 1, 0, 3)).reshape(sq * b, h)
        out = ctx @ Wproj.T + bproj
        out = out.reshape(sq, b, h)
        return jnp.transpose(out, (1, 0, 2))

    def _L1_attn_b_ref(x, Wqd, Wqu, Wqr, Wkvd, Wku, Wvu, Wkr, Wo):
        import jax, jax.numpy as jnp
        import numpy as np
        B, T, D = (2, 256, 256)
        H, LAT, RD = (16, 64, 64)
        HD = D // H

        def _rope_tables(rd, max_t, theta=10000.0):
            freqs = 1.0 / theta ** (np.arange(0, rd, 2, dtype=np.float32) / rd)
            t = np.arange(max_t, dtype=np.float32)
            ang = np.outer(t, freqs)
            cos = np.tile(np.cos(ang), (1, 2))
            sin = np.tile(np.sin(ang), (1, 2))
            return (jnp.asarray(cos), jnp.asarray(sin))

        def _rotate_half(x):
            d = x.shape[-1] // 2
            return jnp.concatenate([-x[..., d:], x[..., :d]], axis=-1)

        def _apply_rope(x, cos, sin):
            t = x.shape[2]
            return x * cos[:t][None, None] + _rotate_half(x) * sin[:t][None, None]
        b, t, d = x.shape
        cos, sin = _rope_tables(RD, t)
        ql = x @ Wqd
        q = (ql @ Wqu).reshape(b, t, H, HD).transpose(0, 2, 1, 3)
        qr = (ql @ Wqr).reshape(b, t, H, RD).transpose(0, 2, 1, 3)
        qr = _apply_rope(qr, cos, sin)
        ckv = x @ Wkvd
        k = (ckv @ Wku).reshape(b, t, H, HD).transpose(0, 2, 1, 3)
        v = (ckv @ Wvu).reshape(b, t, H, HD).transpose(0, 2, 1, 3)
        kr = _apply_rope((x @ Wkr)[:, None], cos, sin)[:, 0]
        scale = 1.0 / jnp.sqrt(jnp.float32(HD + RD))
        scores = (jnp.einsum('bhtd,bhsd->bhts', q, k) + jnp.einsum('bhtd,bsd->bhts', qr, kr)) * scale
        causal = jnp.tril(jnp.ones((t, t), dtype=bool))
        scores = jnp.where(causal[None, None], scores, jnp.float32(-jnp.inf))
        attn = jax.nn.softmax(scores, axis=-1)
        out = jnp.einsum('bhts,bhsd->bhtd', attn, v)
        out = out.transpose(0, 2, 1, 3).reshape(b, t, d)
        return out @ Wo

    def _L1_ffn_ref(x, gate_w, w_up, w_gate, w_down, up_A, up_B, gate_A, gate_B, down_A, down_B):
        import jax, jax.numpy as jnp
        import numpy as np
        NUM_EXPERTS = 8
        TOP_K = 2
        LORA_ALPHA = 2.0
        LORA_RANK = 16
        D_MODEL = 256
        D_HIDDEN = 704
        B, S, D = x.shape
        H = w_up.shape[0]
        gate_logits = jnp.einsum('bsd,ed->bse', x, gate_w)
        topw, sel = jax.lax.top_k(gate_logits, TOP_K)
        topw = jax.nn.softmax(topw.astype(jnp.float32), axis=1).astype(x.dtype)
        xt = x.reshape(-1, D)
        wf = topw.reshape(-1, TOP_K)
        sf = sel.reshape(-1, TOP_K)
        base_up = xt @ w_up.T
        base_gate = xt @ w_gate.T
        mixed_h = jnp.zeros((xt.shape[0], H), x.dtype)
        lora_down = jnp.zeros_like(xt)
        for e in range(NUM_EXPERTS):
            c = jnp.sum(jnp.where(sf == e, wf, 0.0), axis=1)
            lo_up = LORA_ALPHA * (xt @ up_A[e].T @ up_B[e].T)
            lo_gate = LORA_ALPHA * (xt @ gate_A[e].T @ gate_B[e].T)
            h_e = jax.nn.silu(base_up + lo_up) * (base_gate + lo_gate)
            ch = c[:, None] * h_e
            mixed_h = mixed_h + ch
            lora_down = lora_down + LORA_ALPHA * (ch @ down_A[e].T @ down_B[e].T)
        out = mixed_h @ w_down.T + lora_down
        return out.reshape(B, S, D)
    x = L0_attn_a_hidden_states
    x = x + _L0_attn_a_ref(_layernorm(x, axis=-1), L0_attn_a_Wq, L0_attn_a_bq, L0_attn_a_Wk, L0_attn_a_bk, L0_attn_a_Wv, L0_attn_a_bv, L0_attn_a_Wo, L0_attn_a_bo, L0_attn_a_truth_gate, L0_attn_a_balance_gate, L0_attn_a_order_gate, L0_attn_a_justice_gate, L0_attn_a_harmony_gate)
    x = x + _L0_ffn_ref(_layernorm(x, axis=-1), L0_ffn_W_up, L0_ffn_W_gate, L0_ffn_W_down)
    x = x + _L0_attn_b_ref(_layernorm(x, axis=-1), L0_attn_b_Wq, L0_attn_b_Wk, L0_attn_b_Wv, L0_attn_b_Wa, L0_attn_b_Wb, L0_attn_b_Wg, L0_attn_b_Wo, L0_attn_b_conv_wq, L0_attn_b_conv_wk, L0_attn_b_conv_wv, L0_attn_b_A_log, L0_attn_b_dt_bias, L0_attn_b_norm_weight)
    x = x + _L0_ffn_ref(_layernorm(x, axis=-1), L0_ffn_W_up, L0_ffn_W_gate, L0_ffn_W_down)
    x = x + _L1_attn_a_ref(_layernorm(x, axis=-1), L1_attn_a_key, L1_attn_a_value, L1_attn_a_Wqkv, L1_attn_a_Wproj, L1_attn_a_bproj)
    x = x + _L1_ffn_ref(_layernorm(x, axis=-1), L1_ffn_gate_w, L1_ffn_w_up, L1_ffn_w_gate, L1_ffn_w_down, L1_ffn_up_A, L1_ffn_up_B, L1_ffn_gate_A, L1_ffn_gate_B, L1_ffn_down_A, L1_ffn_down_B)
    x = x + _L1_attn_b_ref(_layernorm(x, axis=-1), L1_attn_b_Wqd, L1_attn_b_Wqu, L1_attn_b_Wqr, L1_attn_b_Wkvd, L1_attn_b_Wku, L1_attn_b_Wvu, L1_attn_b_Wkr, L1_attn_b_Wo)
    x = x + _L1_ffn_ref(_layernorm(x, axis=-1), L1_ffn_gate_w, L1_ffn_w_up, L1_ffn_w_gate, L1_ffn_w_down, L1_ffn_up_A, L1_ffn_up_B, L1_ffn_gate_A, L1_ffn_gate_B, L1_ffn_down_A, L1_ffn_down_B)
    return x

_drawn_inputs = setup_inputs


def setup_inputs(seed=0):
    import zlib

    import numpy as np

    out = dict(_drawn_inputs(seed))
    spreads = {'L0_attn_a_bq': (0.0, 0.8),
     'L0_attn_a_bk': (0.0, 0.8),
     'L0_attn_a_bv': (0.0, 0.1),
     'L0_attn_a_bo': (0.0, 0.1),
     'L0_attn_b_norm_weight': (1.0, 0.2),
     'L1_attn_a_bproj': (0.0, 0.1)}
    factors = {'L0_attn_a_Wq': 8.0,
     'L0_attn_a_Wk': 8.0,
     'L0_attn_a_Wv': 8.0,
     'L1_attn_b_Wqd': 8.0,
     'L1_attn_b_Wqu': 8.0,
     'L1_attn_b_Wqr': 8.0,
     'L1_attn_b_Wkvd': 8.0,
     'L1_attn_b_Wku': 8.0,
     'L1_attn_b_Wvu': 8.0,
     'L1_attn_b_Wkr': 8.0,
     'L1_attn_b_Wo': 8.0,
     'L1_ffn_gate_w': 4.728,
     'L1_ffn_w_up': 3.723,
     'L1_ffn_w_gate': 3.508,
     'L1_ffn_w_down': 3.468,
     'L1_ffn_up_A': 8.0,
     'L1_ffn_up_B': 8.0,
     'L1_ffn_gate_A': 8.0,
     'L1_ffn_gate_B': 8.0,
     'L1_ffn_down_A': 8.0,
     'L1_ffn_down_B': 8.0}
    for name, (base, spread) in spreads.items():
        noise = np.random.default_rng([zlib.crc32(name.encode()), seed]).standard_normal(out[name].shape)
        drawn = base * np.exp(spread * noise) if base else spread * noise
        out[name] = jnp.asarray(drawn.astype(out[name].dtype))
    for name, factor in factors.items():
        out[name] = (out[name] * factor).astype(out[name].dtype)
    return out
```

```python
from contextlib import ExitStack

import numpy as np

import concourse.bass as bass
from concourse import mybir

F32 = mybir.dt.float32
BF16 = mybir.dt.bfloat16
U32 = mybir.dt.uint32
ALU = mybir.AluOpType
ACT = mybir.ActivationFunctionType
AX = mybir.AxisListType

P = 128
S = 1024
D = 256
NT = S // P
KT = D // P
HALF = 512
NH2 = S // HALF
HEADS = 16
HD = D // HEADS
LN_EPS = 1e-5
STAGES = 8


class Core:

    def __init__(self, nc, ctx):
        self.nc, self.ctx, self.n, self.sems = nc, ctx, 0, []
        self.X = self.sb("x_tokens", [P, NT, D], F32)
        self.XNT = self.sb("xn_features", [P, KT, S], F32)
        self.ident = self.sb("identity", [P, P], F32)
        self.ones = self.sb("ones_row", [1, P], F32)
        self.ones_sq = self.sb("ones_square", [P, P], F32)
        self.bank = [self.ps(f"bank{i}", [P, HALF], F32) for i in range(8)] if False else None
        self.stored = nc.alloc_semaphore("stored")
        self.psum = self.ps("psum", [P, 8, HALF], F32)

    def sb(self, name, shape, dt, ctx=None):
        self.n += 1
        return (ctx or self.ctx).enter_context(self.nc.sbuf_tensor(f"{name}_{self.n}", shape, dt))

    def ps(self, name, shape, dt):
        return self.ctx.enter_context(self.nc.psum_tensor(name, shape, dt))

    def sem(self, name):
        self.n += 1
        self.sems.append(self.nc.alloc_semaphore(f"{name}_{self.n}"))
        return self.sems[-1]

    def layer_done(self):
        self.nc.clear_and_free_semaphores(self.sems)
        self.sems = []
        self.nc.all_engine_barrier()


def load_inputs(nc, core, x_dram):
    X, ident = core.X, core.ident
    x_loaded, zeroed, made = core.sem("x_loaded"), core.sem("ident_zeroed"), core.sem("consts_made")
    with nc.Block() as block:
        @block.sync
        def _(sp):
            sp.dma_start(X[:], x_dram.rearrange("(t p) d -> p t d", p=P)).then_inc(x_loaded, 16)
            sp.wait_ge(x_loaded, 16)

        @block.gpsimd
        def _(pool):
            pool.memset(ident[:], 0.0).then_inc(zeroed, 1)
            pool.memset(core.ones[:], 1.0).then_inc(made, 1)
            pool.memset(core.ones_sq[:], 1.0).then_inc(made, 1)
            pool.wait_ge(zeroed, 1)
            pool.affine_select(out=ident[:], in_=ident[:], compare_op=ALU.not_equal, fill=1.0, base=0,
                               pattern=[[-1, P]], channel_multiplier=1).then_inc(made, 1)


def norm_stage(nc, core, tag):
    X, XNT, ident, psum = core.X, core.XNT, core.ident, core.psum
    stat_done, mv_done, var_done = (core.sem(tag + n) for n in ("_stats", "_mean_var", "_var_eps"))
    std_done, rstd_done, xn_done = (core.sem(tag + n) for n in ("_std", "_rstd", "_xn"))
    turned, taken = core.sem(tag + "_transposed"), core.sem(tag + "_taken")
    with ExitStack() as tmp:
        st = core.sb("bn_stats", [P, NT, 6], F32, tmp)
        mv = core.sb("mean_var", [P, NT, 2], F32, tmp)
        ve = core.sb("var_eps", [P, NT], F32, tmp)
        std = core.sb("std", [P, NT], F32, tmp)
        rstd = core.sb("rstd", [P, NT], F32, tmp)
        xn = core.sb("xn", [P, NT, D], F32, tmp)
        with nc.Block() as block:
            @block.vector
            def _(dve):
                for t in range(NT):
                    dve.bn_stats(st[:, t, :], X[:, t, :]).then_inc(stat_done, 1)
                for t in range(NT):
                    dve.wait_ge(stat_done, t + 1)
                    dve.bn_aggr(mv[:, t, :], st[:, t, :]).then_inc(mv_done, 1)
                dve.wait_ge(mv_done, NT)
                dve.tensor_scalar(ve[:], mv[:, :, 1], LN_EPS, None, ALU.add).then_inc(var_done, 1)
                dve.wait_ge(std_done, 1)
                dve.reciprocal(rstd[:], std[:]).then_inc(rstd_done, 1)
                dve.wait_ge(rstd_done, 1)
                for t in range(NT):
                    dve.tensor_scalar(xn[:, t, :], X[:, t, :], mv[:, t, 0:1], rstd[:, t:t + 1],
                                      ALU.subtract, ALU.mult).then_inc(xn_done, 1)
                for half in range(NH2):
                    dve.wait_ge(turned, 2 * half + 2)
                    dve.tensor_copy(XNT[:, 1, half * HALF:(half + 1) * HALF],
                                    psum[:, 2 * half + 1, :]).then_inc(taken, 1)

            @block.scalar
            def _(act):
                act.wait_ge(var_done, 1)
                act.activation(std[:], ve[:], ACT.Sqrt).then_inc(std_done, 1)
                for half in range(NH2):
                    act.wait_ge(turned, 2 * half + 1)
                    act.activation(XNT[:, 0, half * HALF:(half + 1) * HALF], psum[:, 2 * half, :],
                                   ACT.Copy).then_inc(taken, 1)

            @block.tensor
            def _(pe):
                for half in range(NH2):
                    for f in range(KT):
                        for i in range(4):
                            t = 4 * half + i
                            pe.wait_ge(xn_done, t + 1)
                            last = pe.transpose(psum[:, 2 * half + f, i * P:(i + 1) * P],
                                                xn[:, t, f * P:(f + 1) * P], ident[:])
                        last.then_inc(turned, 1)


DE = 1024
NE = DE // P
TERNARY_EPS = 1e-8


def ternary_weights(nc, core, scope, wup_d, wgate_d, wdown_d):
    scale = core.sb("ternary_scales", [P, 3], F32, scope)
    ups = core.sb("w_up_signs", [P, KT, DE], F32, scope)
    gates = core.sb("w_gate_signs", [P, KT, DE], F32, scope)
    downs = core.sb("w_down_signs", [P, NE, D], F32, scope)
    flat = [ups[:].rearrange("p k n -> p (k n)"), gates[:].rearrange("p k n -> p (k n)"),
            downs[:].rearrange("p k n -> p (k n)")]
    N = KT * DE
    loaded = [core.sem(f"ternary_w{i}_loaded") for i in range(3)]
    absum, total, scaled, halves, low = (core.sem("ternary_" + n) for n in
                                         ("abs_summed", "total", "scaled", "halved", "low_side"))
    done = core.sem("ternary_signs")
    with ExitStack() as tmp:
        w = [core.sb(f"w{i}", [P, N], F32, tmp) for i in range(3)]
        b = core.sb("low_side", [P, N], F32, tmp)
        part = core.sb("abs_sums", [P, 3], F32, tmp)
        h = core.sb("half_scales", [P, 2, 3], F32, tmp)
        with nc.Block() as block:
            @block.sync
            def _(sp):
                sp.dma_start(w[0][:].rearrange("p (k n) -> p k n", k=KT),
                             wup_d.rearrange("(k p) n -> p k n", p=P)).then_inc(loaded[0], 16)
                sp.dma_start(w[1][:].rearrange("p (k n) -> p k n", k=KT),
                             wgate_d.rearrange("(k p) n -> p k n", p=P)).then_inc(loaded[1], 16)
                sp.dma_start(w[2][:].rearrange("p (k n) -> p k n", k=NE),
                             wdown_d.rearrange("(k p) n -> p k n", p=P)).then_inc(loaded[2], 16)

            @block.tensor
            def _(pe):
                pe.wait_ge(absum, 3)
                pe.matmul(core.psum[:, 0, 0:3], core.ones_sq[:], part[:], start=True, stop=True).then_inc(total, 1)

            @block.vector
            def _(dve):
                for i in range(3):
                    dve.wait_ge(loaded[i], 16)
                    dve.tensor_reduce(part[:, i:i + 1], w[i][:], AX.X, ALU.add,
                                      apply_absolute_value=True).then_inc(absum, 1)
                dve.wait_ge(total, 1)
                dve.tensor_scalar(scale[:], core.psum[:, 0, 0:3], 1.0 / (DE * D), TERNARY_EPS,
                                  ALU.mult, ALU.add).then_inc(scaled, 1)
                dve.wait_ge(scaled, 1)
                dve.tensor_scalar(h[:, 0, :], scale[:], 0.5, None, ALU.mult).then_inc(halves, 1)
                dve.tensor_scalar(h[:, 1, :], scale[:], -0.5, None, ALU.mult).then_inc(halves, 1)
                dve.wait_ge(halves, 2)
                for i in range(3):
                    if i:
                        dve.wait_ge(done, i)
                    dve.tensor_scalar(b[:], w[i][:], h[:, 1, i:i + 1], None, ALU.is_lt).then_inc(low, 1)
                    dve.wait_ge(low, i + 1)
                    dve.scalar_tensor_tensor(flat[i], w[i][:], h[:, 0, i:i + 1], b[:], ALU.is_gt,
                                             ALU.subtract).then_inc(done, 1)
    return scale, ups, gates, downs


def ternary_ffn(nc, core, tag, weights):
    scale, ups, gates, downs = weights
    X, XNT, psum = core.X, core.XNT, core.psum
    proj, act_done, hid = (core.sem(tag + n) for n in ("_projected", "_silu", "_hidden"))
    down, added = core.sem(tag + "_down"), core.sem(tag + "_added")
    with ExitStack() as tmp:
        H = core.sb("hidden", [P, NE, S], F32, tmp)
        sil = core.sb("silu_up", [P, 2, HALF], F32, tmp)
        units = [(e, half) for half in range(NH2) for e in range(NE)]
        with nc.Block() as block:
            @block.tensor
            def _(pe):
                for u, (e, half) in enumerate(units):
                    b = u % 2
                    if u >= 2:
                        pe.wait_ge(hid, u - 1)
                    for j, w in enumerate((ups, gates)):
                        for k in range(KT):
                            last = pe.matmul(psum[:, 2 * b + j, :], w[:, k, e * P:(e + 1) * P],
                                             XNT[:, k, half * HALF:(half + 1) * HALF],
                                             start=(k == 0), stop=(k == KT - 1))
                        last.then_inc(proj, 1)
                for t in range(NT):
                    pe.wait_ge(hid, NE * (t // 4 + 1))
                    if t >= 4:
                        pe.wait_ge(added, t - 3)
                    for e in range(NE):
                        last = pe.matmul(psum[:, 4 + t % 4, 0:D], H[:, e, t * P:(t + 1) * P], downs[:, e, :],
                                         start=(e == 0), stop=(e == NE - 1))
                    last.then_inc(down, 1)

            @block.scalar
            def _(act):
                for u, (e, half) in enumerate(units):
                    act.wait_ge(proj, 2 * u + 1)
                    if u >= 2:
                        act.wait_ge(hid, u - 1)
                    act.activation(sil[:, u % 2, :], psum[:, 2 * (u % 2), :], ACT.Silu,
                                   scale=scale[:, 0:1]).then_inc(act_done, 1)

            @block.vector
            def _(dve):
                for u, (e, half) in enumerate(units):
                    dve.wait_ge(proj, 2 * u + 2)
                    dve.wait_ge(act_done, u + 1)
                    dve.scalar_tensor_tensor(H[:, e, half * HALF:(half + 1) * HALF], psum[:, 2 * (u % 2) + 1, :],
                                             scale[:, 1:2], sil[:, u % 2, :], ALU.mult, ALU.mult).then_inc(hid, 1)
                for t in range(NT):
                    dve.wait_ge(down, t + 1)
                    dve.scalar_tensor_tensor(X[:, t, :], psum[:, 4 + t % 4, 0:D], scale[:, 2:3], X[:, t, :],
                                             ALU.mult, ALU.add).then_inc(added, 1)


VW = 32
PARTS = 6
K_PARTS = (0, 1, 2, 0, 1, 0)
Q_PARTS = (0, 0, 0, 1, 1, 2)
SHIFT_ROW = PARTS * HD
KROWS = SHIFT_ROW + 1


def attention16(nc, core, tag, wq_d, wk_d, wv_d, wo_d, biases, gates, pos_d):
    X, XNT, psum, ident = core.X, core.XNT, core.psum, core.ident
    sem = lambda n: core.sem(f"{tag}_{n}")
    with ExitStack() as tmp:
        sb = lambda n, shape, dt=F32: core.sb(n, shape, dt, tmp)
        KS = sb("k_stack", [P, HEADS, S], BF16)
        QS = sb("q_stack", [P, HEADS, S], BF16)
        V = sb("v_ones", [P, NT, HEADS, VW])
        O = sb("attended", [P, NT, D])
        wo = sb("wo", [P, KT, D])
        bo = sb("bo", [1, D])
        esc = sb("exp_scale", [P, 1])
        ebias = sb("exp_bias", [P, NT])
        with ExitStack() as tmp2:
            sb2 = lambda n, shape, dt=F32: core.sb(n, shape, dt, tmp2)
            wq, wk, wv = sb2("wq", [P, KT, D]), sb2("wk", [P, KT, D]), sb2("wv", [P, KT, D])
            bqk = sb2("bias_qk", [P, 2, KT])
            bv = sb2("bias_v", [1, D])
            g3 = sb2("gates", [P, 2])
            pos = sb2("positions", [P, NT])
            full = sb2("qk_full", [P, 2, S])
            parts = sb2("qk_parts", [P, 4, 3, S], BF16)
            rest = sb2("qk_rest", [P, 2, S])
            loaded, made = sem("loaded"), sem("ones_made")
            qk_ready, full_done = sem("qk_projected"), sem("qk_full")
            hi, r1, mid, lo, stacked = (sem(n) for n in ("high", "rest", "middle", "low", "stacked"))
            v_ready, v_done, zeroed = sem("v_projected"), sem("v_kept"), sem("v_zeroed")
            esc_done = sem("exp_scale")
            nb = 0 if biases is None else 3
            with nc.Block() as block:
                @block.sync
                def _(sp):
                    n = 0
                    for w, w_d in ((wq, wq_d), (wk, wk_d), (wv, wv_d), (wo, wo_d)):
                        sp.dma_start(w[:], w_d.rearrange("(k p) n -> p k n", p=P)).then_inc(loaded, 16)
                    sp.dma_start(bo[:], biases["bo"].rearrange("(a n) -> a n", a=1)).then_inc(loaded, 16)
                    if gates is not None:
                        sp.dma_start(bqk[:].rearrange("p w k -> p (w k)"), biases["bqk"]).then_inc(loaded, 16)
                        sp.dma_start(bv[:], biases["bv"].rearrange("(a n) -> a n", a=1)).then_inc(loaded, 16)
                        sp.dma_start(g3[:, 0:1], gates["justice"].rearrange("(a n) -> a n", a=1).broadcast_to([P, 1])).then_inc(loaded, 16)
                        sp.dma_start(g3[:, 1:2], gates["order"].rearrange("(a n) -> a n", a=1).broadcast_to([P, 1])).then_inc(loaded, 16)
                        sp.dma_start(pos[:], pos_d).then_inc(loaded, 16)
                    for u in range(4):
                        which, f = u // 2, u % 2
                        dst = (QS, KS)[which]
                        sp.wait_ge(hi, u + 1)
                        sp.wait_ge(mid, u + 1)
                        sp.wait_ge(lo, u + 1)
                        for j, part in enumerate((Q_PARTS, K_PARTS)[which]):
                            for hh in range(8):
                                sp.dma_start(dst[j * HD:(j + 1) * HD, 8 * f + hh, :],
                                             parts[hh * HD:(hh + 1) * HD, u, part, :]).then_inc(stacked, 16)
                    sp.wait_ge(stacked, 16 * 4 * PARTS * 8)

                nload = 5 + (5 if gates is not None else 0)

                @block.tensor
                def _(pe):
                    pe.wait_ge(loaded, 16 * nload)
                    for u in range(4):
                        which, f = u // 2, u % 2
                        w = (wq, wk)[which]
                        for half in range(NH2):
                            if u >= 2:
                                pe.wait_ge(full_done, 2 * (u - 2) + half + 1)
                            for k in range(KT):
                                last = pe.matmul(psum[:, 2 * (u % 2) + half, :], w[:, k, f * P:(f + 1) * P],
                                                 XNT[:, k, half * HALF:(half + 1) * HALF],
                                                 start=(k == 0), stop=(k == KT - 1))
                            last.then_inc(qk_ready, 1)
                    for t in range(NT):
                        if t >= 2:
                            pe.wait_ge(v_done, t - 1)
                        for k in range(KT):
                            last = pe.matmul(psum[:, 4 + t % 2, 0:D], XNT[:, k, t * P:(t + 1) * P], wv[:, k, :],
                                             start=(k == 0), stop=(k == KT - 1 and gates is None))
                        if gates is not None:
                            last = pe.matmul(psum[:, 4 + t % 2, 0:D], core.ones[:], bv[:], start=False, stop=True)
                        last.then_inc(v_ready, 1)

                @block.scalar
                def _(act):
                    if gates is not None:
                        act.wait_ge(loaded, 16 * nload)
                        act.activation(g3[:], g3[:], ACT.Sigmoid).then_inc(esc_done, 1)
                    for u in range(4):
                        which, f = u // 2, u % 2
                        for half in range(NH2):
                            act.wait_ge(qk_ready, 2 * u + half + 1)
                            if u >= 2:
                                act.wait_ge(r1, u - 1)
                                act.wait_ge(hi, u - 1)
                            act.activation(full[:, u % 2, half * HALF:(half + 1) * HALF],
                                           psum[:, 2 * (u % 2) + half, :], ACT.Identity,
                                           bias=bqk[:, which, f:f + 1] if gates is not None else 0.0
                                           ).then_inc(full_done, 1)
                        act.wait_ge(full_done, 2 * u + 2)
                        act.activation(parts[:, u, 0, :], full[:, u % 2, :], ACT.Copy).then_inc(hi, 1)
                        act.wait_ge(r1, u + 1)
                        act.activation(parts[:, u, 1, :], rest[:, u % 2, :], ACT.Copy).then_inc(mid, 1)

                @block.vector
                def _(dve):
                    if gates is not None:
                        dve.wait_ge(esc_done, 1)
                        dve.tensor_scalar(esc[:], g3[:, 0:1], -0.1 / HD ** 0.5, 1.0 / HD ** 0.5,
                                          ALU.mult, ALU.add).then_inc(esc_done, 1)
                        dve.tensor_scalar(ebias[:], pos[:], g3[:, 1:2], 0.05, ALU.mult, ALU.mult).then_inc(esc_done, 1)
                    else:
                        dve.memset(esc[:], 1.0 / HD ** 0.5).then_inc(esc_done, 1)
                        dve.memset(ebias[:], 0.0).then_inc(esc_done, 1)
                    for u in range(4):
                        dve.wait_ge(hi, u + 1)
                        if u >= 2:
                            dve.wait_ge(lo, u - 1)
                            dve.wait_ge(mid, u - 1)
                        dve.tensor_tensor(rest[:, u % 2, :], full[:, u % 2, :], parts[:, u, 0, :],
                                          ALU.subtract).then_inc(r1, 1)
                        dve.wait_ge(mid, u + 1)
                        dve.tensor_tensor(parts[:, u, 2, :], rest[:, u % 2, :], parts[:, u, 1, :],
                                          ALU.subtract).then_inc(lo, 1)
                    dve.wait_ge(zeroed, 3)
                    for t in range(NT):
                        dve.wait_ge(v_ready, t + 1)
                        dve.tensor_copy(V[:, t, :, 0:HD],
                                        psum[:, 4 + t % 2, 0:D].rearrange("p (h d) -> p h d", d=HD)).then_inc(v_done, 1)

                @block.gpsimd
                def _(pool):
                    pool.memset(V[:], 0.0).then_inc(zeroed, 1)
                    pool.wait_ge(zeroed, 1)
                    pool.memset(V[:, :, :, HD:HD + 1], 1.0).then_inc(zeroed, 1)
                    pool.wait_ge(zeroed, 2)
                    pool.memset(KS[SHIFT_ROW:KROWS, :, :], 1.0).then_inc(zeroed, 1)

        PB = 4
        with ExitStack() as tmp2:
            sb2 = lambda n, shape, dt=F32: core.sb(n, shape, dt, tmp2)
            mx = sb2("row_max_halves", [P, 2, NT, NH2])
            nm = sb2("minus_max", [P, 2, NT])
            nmT = sb2("minus_max_rows", [NT, 2, P], BF16)
            pr = sb2("probs", [P, PB, S])
            oT = sb2("out_features", [P, 2, D])
            rc = sb2("reciprocals", [P, 2, 2, 4])
            m_ready, m_half, m_done = sem("max_scores"), sem("max_halves"), sem("minus_max")
            mt_ready, mt_done, shift_in = sem("max_transposed"), sem("max_row_cast"), sem("shift_row")
            s_ready, e_done, pv_ready = sem("scores"), sem("exp"), sem("values_summed")
            o_kept, o_turned, r_done, o_done = sem("out_kept"), sem("out_transposed"), sem("recip"), sem("out_done")
            MB, PVB, TB = 4, 6, 7
            with nc.Block() as block:
                @block.tensor
                def _(pe):
                    def max_scores(h, qt):
                        for half in range(NH2):
                            n = (h * NT + qt) * NH2 + half
                            if n >= 2:
                                pe.wait_ge(m_half, n - 1)
                            pe.matmul(psum[:, MB + n % 2, :], QS[0:SHIFT_ROW, h, qt * P:(qt + 1) * P],
                                      KS[0:SHIFT_ROW, h, half * HALF:(half + 1) * HALF],
                                      start=True, stop=True).then_inc(m_ready, 1)

                    def turn_max(h):
                        pe.wait_ge(m_done, h + 1)
                        if h >= 1:
                            pe.wait_ge(mt_done, h)
                            pe.wait_ge(o_done, h - 1) if h >= 2 else None
                        pe.transpose(psum[0:NT, TB, 2 * P:3 * P], nm[:, h % 2, :], ident[:]).then_inc(mt_ready, 1)

                    def key_scores(h, c):
                        n = h * NT + c
                        if c == 0:
                            pe.wait_ge(shift_in, 16 * (h + 1))
                        if n >= 2:
                            pe.wait_ge(e_done, n - 1)
                        for half in range(NH2):
                            last = pe.matmul(psum[:, 2 * (n % 2) + half, :], KS[0:KROWS, h, c * P:(c + 1) * P],
                                             QS[0:KROWS, h, half * HALF:(half + 1) * HALF], start=True, stop=True)
                        last.then_inc(s_ready, 1)

                    def values(h, c):
                        n = h * NT + c
                        pe.wait_ge(e_done, n + 1)
                        if c == 0 and h >= 1:
                            pe.wait_ge(o_kept, h)
                        for g in range(4):
                            last = pe.matmul(psum[32 * g:32 * g + VW, PVB, 0:D], V[:, c, h, :],
                                             pr[:, n % PB, g * D:(g + 1) * D], start=(c == 0), stop=(c == NT - 1))
                        last.then_inc(pv_ready, 1)

                    def turn_out(h):
                        pe.wait_ge(o_kept, h + 1)
                        if h >= 1:
                            pe.wait_ge(o_done, h)
                            pe.wait_ge(mt_done, min(h + 2, HEADS))
                        for b in range(2):
                            last = pe.transpose(psum[:, TB, b * P:(b + 1) * P], oT[:, h % 2, b * P:(b + 1) * P],
                                                ident[:])
                        last.then_inc(o_turned, 1)

                    for qt in range(NT):
                        max_scores(0, qt)
                    turn_max(0)
                    for h in range(HEADS):
                        for c in range(NT):
                            key_scores(h, c)
                            if h + 1 < HEADS:
                                max_scores(h + 1, c)
                            if c >= 1:
                                values(h, c - 1)
                        if h + 1 < HEADS:
                            turn_max(h + 1)
                        values(h, NT - 1)
                        turn_out(h)

                @block.vector
                def _(dve):
                    def row_max(h, qt):
                        for half in range(NH2):
                            n = (h * NT + qt) * NH2 + half
                            dve.wait_ge(m_ready, n + 1)
                            dve.reduce_max(mx[:, h % 2, qt, half:half + 1], psum[:, MB + n % 2, :], AX.X
                                           ).then_inc(m_half, 1)

                    def minus_max(h):
                        dve.wait_ge(m_half, (h + 1) * NT * NH2)
                        if h >= 2:
                            dve.wait_ge(mt_ready, h - 1)
                        dve.tensor_reduce(nm[:, h % 2, :], mx[:, h % 2, :, :], AX.X, ALU.max,
                                          negate=True).then_inc(m_done, 1)
                        dve.wait_ge(mt_ready, h + 1)
                        if h >= 2:
                            dve.wait_ge(shift_in, 16 * (h - 1))
                        dve.tensor_copy(nmT[:, h % 2, :], psum[0:NT, TB, 2 * P:3 * P]).then_inc(mt_done, 1)

                    def keep_out(h):
                        dve.wait_ge(pv_ready, (h + 1) * NT)
                        dve.tensor_copy(oT[:, h % 2, :], psum[:, PVB, 0:D]).then_inc(o_kept, 1)

                    def finish(h):
                        dve.wait_ge(o_turned, h + 1)
                        t4 = psum[:, TB, 0:D].rearrange("p (b g d) -> p b g d", b=2, g=4)
                        dve.reciprocal(rc[:, h % 2, :, :], t4[:, :, :, HD]).then_inc(r_done, 1)
                        dve.wait_ge(r_done, h + 1)
                        for b in range(2):
                            last = dve.tensor_tensor(
                                O[:].rearrange("p (g b) n -> p b g n", b=2)[:, b, :, h * HD:(h + 1) * HD],
                                t4[:, b, :, 0:HD],
                                rc[:, h % 2, b, :].unsqueeze(2).broadcast_to([P, 4, HD]), ALU.mult)
                        last.then_inc(o_done, 1)

                    for qt in range(NT):
                        row_max(0, qt)
                    minus_max(0)
                    for h in range(HEADS):
                        for c in range(NT):
                            if h + 1 < HEADS:
                                row_max(h + 1, c)
                        if h + 1 < HEADS:
                            minus_max(h + 1)
                        keep_out(h)
                        finish(h)

                @block.sync
                def _(sp):
                    for h in range(HEADS):
                        sp.wait_ge(mt_done, h + 1)
                        sp.dma_start(QS[SHIFT_ROW:KROWS, h, :].rearrange("a (t p) -> a t p", t=NT),
                                     nmT[:, h % 2, :]).then_inc(shift_in, 16)

                @block.scalar
                def _(act):
                    for h in range(HEADS):
                        for c in range(NT):
                            n = h * NT + c
                            act.wait_ge(s_ready, n + 1)
                            if n >= PB:
                                act.wait_ge(pv_ready, n - PB + 1)
                            act.activation(pr[:, n % PB, :],
                                           psum[:, 2 * (n % 2):2 * (n % 2) + 2, :].rearrange("p a n -> p (a n)"),
                                           ACT.Exp, bias=ebias[:, c:c + 1], scale=esc[:]).then_inc(e_done, 1)

        project_out(nc, core, tag, O, wo, bo)


def project_out(nc, core, tag, O, wo, bo, tiles=KT):
    X, psum, ident = core.X, core.psum, core.ident
    turned, kept, ready, added = (core.sem(f"{tag}_{n}") for n in ("o_turned", "o_features", "proj", "added"))
    with ExitStack() as tmp:
        OT = core.sb("attended_features", [P, tiles, S], F32, tmp)
        with nc.Block() as block:
            @block.tensor
            def _(pe):
                for n in range(NH2 * tiles):
                    half, f = n // tiles, n % tiles
                    if n >= 4:
                        pe.wait_ge(kept, n - 3)
                    for i in range(4):
                        t = 4 * half + i
                        last = pe.transpose(psum[:, n % 4, i * P:(i + 1) * P], O[:, t, f * P:(f + 1) * P], ident[:])
                    last.then_inc(turned, 1)
                for t in range(NT):
                    pe.wait_ge(kept, tiles * (t // 4 + 1))
                    if t >= 4:
                        pe.wait_ge(added, t - 3)
                    for k in range(tiles):
                        last = pe.matmul(psum[:, 4 + t % 4, 0:D], OT[:, k, t * P:(t + 1) * P], wo[:, k, :],
                                         start=(k == 0), stop=(k == tiles - 1 and bo is None))
                    if bo is not None:
                        last = pe.matmul(psum[:, 4 + t % 4, 0:D], core.ones[:], bo[:], start=False, stop=True)
                    last.then_inc(ready, 1)

            @block.scalar
            def _(act):
                for n in range(NH2 * tiles):
                    half, f = n // tiles, n % tiles
                    act.wait_ge(turned, n + 1)
                    act.activation(OT[:, f, half * HALF:(half + 1) * HALF], psum[:, n % 4, :],
                                   ACT.Copy).then_inc(kept, 1)

            @block.vector
            def _(dve):
                for t in range(NT):
                    dve.wait_ge(ready, t + 1)
                    dve.tensor_tensor(X[:, t, :], psum[:, 4 + t % 4, 0:D], X[:, t, :], ALU.add).then_inc(added, 1)



GH, GK, GV = 6, 32, 64
QKW, VWD = GH * GK, GH * GV
FW = 2 * QKW + VWD
NF = FW // P
TAPS = 4
LEVELS = 7
RMS_EPS = 1e-5


def gated_delta(nc, core, tag, d):
    X, XNT, psum, ident = core.X, core.XNT, core.psum, core.ident
    sem = lambda n: core.sem(f"{tag}_{n}")
    with ExitStack() as tmp:
        sb = lambda n, shape, dt=F32: core.sb(n, shape, dt, tmp)
        SG = sb("silu_gate", [P, NT, VWD])
        KBE = sb("k_beta_eg", [P, NT, GH, GK])
        KD = sb("k_decayed", [P, NT, GH, GK])
        BV = sb("beta_v", [P, NT, GH, GV])
        ETH = sb("exp_total_by_row", [P, 2, NT])
        G = sb("g_sums", [P, NT, GH])
        g = sb("g", [P, NT, GH])
        wo = sb("delta_wo", [P, 3, D])
        nw = sb("norm_weight", [P, GV])
        tri = sb("upper_ones", [P, P])
        QET = sb("qe_features", [P, 2, S])
        wload = sem("wo_loaded")
        with ExitStack() as mid_scope:
            sbm = lambda n, shape, dt=F32: core.sb(n, shape, dt, mid_scope)
            PT = sbm("p_by_key", [P, GH * NT, P])
            EA = sbm("e_then_minus_a", [P, GH * NT, P])
            norm_scope = ExitStack()
            sbn = lambda n, shape, dt=F32: core.sb(n, shape, dt, norm_scope)
            KN, KB = sbn("k_normed", [P, NT, GH, GK]), sbn("k_beta", [P, NT, GH, GK])
            QN, QE = sbn("q_normed", [P, NT, GH, GK]), sbn("q_eg", [P, NT, GH, GK])
            with ExitStack() as tmp2:
                sb2 = lambda n, shape, dt=F32: core.sb(n, shape, dt, tmp2)
                YT = sb2("conv_tokens", [P, NT, FW])
                AB = sb2("ab", [P, NT, 2 * GH])
                with ExitStack() as tmp3:
                    sb3 = lambda n, shape, dt=F32: core.sb(n, shape, dt, tmp3)
                    wqkv, wgab = sb3("wqkv", [P, KT, FW]), sb3("wgab", [P, KT, VWD + 2 * GH])
                    cw = sb3("conv_w", [P, NF, TAPS])
                    Y = PT[:].rearrange("p (f a) n -> p f (a n)", f=NF)
                    loaded, proj, tapped, conv = sem("w_loaded"), sem("proj"), sem("tap"), sem("conv")
                    silu, turned, kept = sem("silu"), sem("turned"), sem("kept")
                    gate_in, gate_out, ab_out = sem("gate_in"), sem("gate_out"), sem("ab_out")
                    tri_made = sem("tri")
                    with nc.Block() as block:
                        @block.sync
                        def _(sp):
                            for k in range(KT):
                                sp.dma_start(wqkv[:, k, :], d["wqkv"][k * P:(k + 1) * P, :]).then_inc(loaded, 16)
                                sp.dma_start(wgab[:, k, :], d["wgab"][k * P:(k + 1) * P, :]).then_inc(loaded, 16)
                            sp.dma_start(cw[:].rearrange("p f t -> p (f t)"), d["conv"]).then_inc(loaded, 16)
                            sp.dma_start(wo[:], d["wo"].rearrange("(k p) n -> p k n", p=P)).then_inc(wload, 16)
                            sp.dma_start(nw[:], d["nw"].rearrange("(a n) -> a n", a=1).broadcast_to([P, GV])
                                         ).then_inc(wload, 16)
                            sp.wait_ge(wload, 32)

                        @block.gpsimd
                        def _(pool):
                            pool.affine_select(out=tri[:], in_=core.ones_sq[:], compare_op=ALU.is_ge, fill=0.0,
                                               base=0, pattern=[[1, P]], channel_multiplier=-1).then_inc(tri_made, 1)

                        @block.tensor
                        def _(pe):
                            pe.wait_ge(loaded, 16 * 5)

                            def project(f):
                                if f >= 2:
                                    pe.wait_ge(conv, TAPS - 1 + (TAPS - 1) * (f - 2))
                                for half in range(NH2):
                                    for k in range(KT):
                                        last = pe.matmul(psum[:, 2 * (f % 2) + half, :],
                                                         wqkv[:, k, f * P:(f + 1) * P],
                                                         XNT[:, k, half * HALF:(half + 1) * HALF],
                                                         start=(k == 0), stop=(k == KT - 1))
                                last.then_inc(proj, 1)

                            def turn(f):
                                pe.wait_ge(silu, f + 1)
                                for half in range(NH2):
                                    n = 2 * f + half
                                    if n >= 2:
                                        pe.wait_ge(kept, n - 1)
                                    for i in range(4):
                                        t = 4 * half + i
                                        last = pe.transpose(psum[:, 4 + n % 2, i * P:(i + 1) * P],
                                                            Y[:, f, t * P:(t + 1) * P], ident[:])
                                    last.then_inc(turned, 1)

                            def gates(t):
                                if t >= 2:
                                    pe.wait_ge(gate_out, t - 1)
                                    pe.wait_ge(ab_out, t - 1)
                                for k in range(KT):
                                    last = pe.matmul(psum[:, 6 + t % 2, 0:VWD + 2 * GH], XNT[:, k, t * P:(t + 1) * P],
                                                     wgab[:, k, :], start=(k == 0), stop=(k == KT - 1))
                                last.then_inc(gate_in, 1)

                            for f in range(NF + 1):
                                if f < NF:
                                    project(f)
                                if f >= 1:
                                    turn(f - 1)
                            for t in range(NT):
                                gates(t)

                        @block.scalar
                        def _(act):
                            act.wait_ge(loaded, 16 * 5)
                            for f in range(NF + 1):
                                if f < NF:
                                    act.wait_ge(proj, f + 1)
                                    act.activation(Y[:, f, :], psum[:, 2 * (f % 2):2 * (f % 2) + 2, :
                                                                    ].rearrange("p a n -> p (a n)"),
                                                   ACT.Copy, scale=cw[:, f, TAPS - 1:TAPS]).then_inc(tapped, 1)
                                if f >= 1:
                                    act.wait_ge(conv, (TAPS - 1) * f)
                                    act.activation(Y[:, f - 1, :], Y[:, f - 1, :], ACT.Silu).then_inc(silu, 1)
                                    for half in range(NH2):
                                        n = 2 * (f - 1) + half
                                        act.wait_ge(turned, n + 1)
                                        act.activation(YT[:, 4 * half:4 * half + 4, (f - 1) * P:f * P],
                                                       psum[:, 4 + n % 2, :].rearrange("p (t n) -> p t n", t=4),
                                                       ACT.Copy).then_inc(kept, 1)
                            for t in range(NT):
                                act.wait_ge(gate_in, t + 1)
                                act.activation(SG[:, t, :], psum[:, 6 + t % 2, 0:VWD], ACT.Silu).then_inc(gate_out, 1)

                        @block.vector
                        def _(dve):
                            for f in range(NF):
                                dve.wait_ge(tapped, f + 1)
                                src = psum[:, 2 * (f % 2):2 * (f % 2) + 2, :].rearrange("p a n -> p (a n)")
                                for i in range(1, TAPS):
                                    if i > 1:
                                        dve.wait_ge(conv, (TAPS - 1) * f + i - 1)
                                    dve.scalar_tensor_tensor(Y[:, f, i:], src[:, 0:S - i],
                                                             cw[:, f, TAPS - 1 - i:TAPS - i], Y[:, f, i:],
                                                             ALU.mult, ALU.add).then_inc(conv, 1)
                            for t in range(NT):
                                dve.wait_ge(gate_in, t + 1)
                                dve.wait_ge(gate_out, t + 1)
                                dve.tensor_copy(AB[:, t, :], psum[:, 6 + t % 2, VWD:VWD + 2 * GH]).then_inc(ab_out, 1)

                with ExitStack() as tmp3:
                    sb3 = lambda n, shape, dt=F32: core.sb(n, shape, dt, tmp3)
                    dtb, alog = sb3("dt_bias", [P, GH]), sb3("a_log", [P, GH])
                    x, ax, e, u, lnu, du, one = (sb3(n, [P, NT, GH]) for n in
                                                 ("a_in", "a_abs", "e_neg", "e_plus_1", "ln", "u_minus_1", "is_one"))
                    eb, beta = sb3("exp_minus_b", [P, NT, GH]), sb3("beta", [P, NT, GH])
                    ea = sb3("exp_a_log", [P, GH])
                    eG, eT, eD, dd = (sb3(n, [P, NT, GH]) for n in ("exp_G", "exp_total", "exp_rest", "rest"))
                    sq = sb3("squares", [P, NT, 2 * QKW])
                    ss, r = sb3("square_sums", [P, NT, 2 * GH]), sb3("inverse_norms", [P, NT, 2 * GH])
                    fk = sb3("factors", [P, 5, NT, GH])
                    loaded, ch, aux, from_act, from_pe = sem("ab_loaded"), sem("chain"), sem("to_act"), sem("from_act"), sem("from_pe")
                    to_pe, sq_done, fact, scaled = sem("to_pe"), sem("sq_done"), sem("factors"), sem("scaled")
                    with nc.Block() as block:
                        @block.sync
                        def _(sp):
                            sp.dma_start(dtb[:], d["dt"].rearrange("(a n) -> a n", a=1).broadcast_to([P, GH])).then_inc(loaded, 16)
                            sp.dma_start(alog[:], d["alog"].rearrange("(a n) -> a n", a=1).broadcast_to([P, GH])).then_inc(loaded, 16)

                        @block.tensor
                        def _(pe):
                            pe.wait_ge(to_pe, 1)
                            gf = g[:].rearrange("p t h -> p (t h)")
                            pe.matmul(psum[:, 0, 0:NT * GH], tri[:], gf, start=True, stop=True).then_inc(from_pe, 1)
                            pe.matmul(psum[:, 1, 0:NT * GH], core.ones_sq[:], gf, start=True, stop=True).then_inc(from_pe, 1)

                        @block.scalar
                        def _(act):
                            act.wait_ge(loaded, 32)
                            act.activation(ea[:], alog[:], ACT.Exp).then_inc(from_act, 1)
                            act.activation(eb[:], AB[:, :, GH:], ACT.Exp, scale=-1.0).then_inc(from_act, 1)
                            act.wait_ge(aux, 1)
                            act.activation(e[:], ax[:], ACT.Exp, scale=-1.0).then_inc(from_act, 1)
                            act.wait_ge(aux, 2)
                            act.activation(lnu[:], u[:], ACT.Ln).then_inc(from_act, 1)
                            act.wait_ge(aux, 3)
                            act.activation(eG[:], G[:], ACT.Exp).then_inc(from_act, 1)
                            act.activation(eT[:], psum[:, 1, 0:NT * GH].rearrange("p (t h) -> p t h", h=GH),
                                           ACT.Exp).then_inc(from_act, 1)
                            act.activation(eD[:], dd[:], ACT.Exp).then_inc(from_act, 1)
                            act.wait_ge(sq_done, 1)
                            act.activation(ss[:], ss[:], ACT.Sqrt).then_inc(from_act, 1)

                        @block.vector
                        def _(dve):
                            n = [0]

                            def link(i):
                                n[0] += 1
                                i.then_inc(ch, 1)
                                dve.wait_ge(ch, n[0])

                            dve.wait_ge(loaded, 32)
                            link(dve.tensor_tensor(x[:], AB[:, :, 0:GH], dtb[:].unsqueeze(1).broadcast_to([P, NT, GH]), ALU.add))
                            dve.scalar_tensor_tensor(ax[:], x[:], -1.0, x[:], ALU.mult, ALU.max).then_inc(aux, 1)
                            qk = YT[:, :, 0:2 * QKW]
                            link(dve.tensor_tensor(sq[:], qk, qk, ALU.mult))
                            dve.reduce_sum(ss[:].rearrange("p t h -> p (t h)"),
                                           sq[:].rearrange("p t (h c) -> p (t h) c", c=GK), AX.X).then_inc(sq_done, 1)
                            dve.wait_ge(from_act, 3)
                            dve.tensor_scalar(u[:], e[:], 1.0, None, ALU.add).then_inc(aux, 1)
                            dve.wait_ge(aux, 2)
                            link(dve.tensor_scalar(du[:], u[:], 1.0, None, ALU.subtract))
                            link(dve.tensor_scalar(one[:], du[:], 0.0, None, ALU.is_equal))
                            link(dve.tensor_tensor(du[:], du[:], one[:], ALU.add))
                            link(dve.reciprocal(du[:], du[:]))
                            link(dve.tensor_tensor(du[:], du[:], e[:], ALU.mult))
                            link(dve.tensor_tensor(one[:], one[:], e[:], ALU.mult))
                            dve.wait_ge(from_act, 4)
                            link(dve.tensor_tensor(lnu[:], lnu[:], du[:], ALU.mult))
                            link(dve.tensor_tensor(lnu[:], lnu[:], one[:], ALU.add))
                            link(dve.scalar_tensor_tensor(x[:], x[:], 0.0, lnu[:], ALU.max, ALU.add))
                            dve.scalar_tensor_tensor(g[:], x[:], -1.0, ea[:].unsqueeze(1).broadcast_to([P, NT, GH]),
                                                     ALU.mult, ALU.mult).then_inc(to_pe, 1)
                            link(dve.tensor_scalar(eb[:], eb[:], 1.0, None, ALU.add))
                            link(dve.reciprocal(beta[:], eb[:]))
                            dve.wait_ge(from_pe, 2)
                            link(dve.tensor_copy(G[:], psum[:, 0, 0:NT * GH].rearrange("p (t h) -> p t h", h=GH)))
                            dve.tensor_tensor(dd[:], psum[:, 1, 0:NT * GH].rearrange("p (t h) -> p t h", h=GH), G[:],
                                              ALU.subtract).then_inc(aux, 1)
                            dve.wait_ge(from_act, 8)
                            link(dve.reciprocal(r[:], ss[:]))
                            for h in range(GH):
                                rows = slice(32 * (h % 4), 32 * (h % 4) + 32)
                                link(dve.tensor_copy(ETH[rows, h // 4, :], eT[rows, :, h]))
                            rq, rk = r[:, :, 0:GH], r[:, :, GH:]
                            link(dve.tensor_scalar(fk[:, 0], rq, GK ** -0.5, None, ALU.mult))
                            link(dve.tensor_tensor(fk[:, 1], fk[:, 0], eG[:], ALU.mult))
                            link(dve.tensor_tensor(fk[:, 2], rk, beta[:], ALU.mult))
                            link(dve.tensor_tensor(fk[:, 3], fk[:, 2], eG[:], ALU.mult))
                            link(dve.tensor_tensor(fk[:, 4], rk, eD[:], ALU.mult))
                            q, k = YT[:, :, 0:QKW], YT[:, :, QKW:2 * QKW]
                            for out, src, f in ((QN, q, fk[:, 0]), (QE, q, fk[:, 1]), (KN, k, rk), (KB, k, fk[:, 2]),
                                                (KBE, k, fk[:, 3]), (KD, k, fk[:, 4])):
                                for t in range(NT):
                                    dve.tensor_tensor(out[:, t], src[:, t, :].rearrange("p (h c) -> p h c", c=GK),
                                                      f[:, t, :].unsqueeze(2).broadcast_to([P, GH, GK]), ALU.mult)
                            for t in range(NT):
                                last = dve.tensor_tensor(BV[:, t], YT[:, t, 2 * QKW:].rearrange("p (h c) -> p h c", c=GV),
                                                         beta[:, t, :].unsqueeze(2).broadcast_to([P, GH, GV]), ALU.mult)

            with ExitStack() as tmp2:
                sb2 = lambda n, shape, dt=F32: core.sb(n, shape, dt, tmp2)
                KNT, KBT, QNT = (sb2(n, [P, 2, S]) for n in ("kn_features", "kb_features", "qn_features"))
                ed = sb2("exponents", [P, 2, 4, P])
                turned, kept = sem("qk_turned"), sem("qk_kept")
                e_in, e_sub, e_exp, e_done = sem("e_in"), sem("e_sub"), sem("e_exp"), sem("e_done")
                p_in, p_done, a_in, a_done = sem("p_in"), sem("p_done"), sem("a_in"), sem("a_done")
                units = [(o, i, f, half) for o, i in ((QET, QE), (KNT, KN), (KBT, KB), (QNT, QN))
                         for f in range(2) for half in range(NH2)]
                NB = GH * 2
                with nc.Block() as block:
                    @block.tensor
                    def _(pe):
                        for n, (o, i, f, half) in enumerate(units):
                            w = P if f == 0 else QKW - P
                            if n >= 2:
                                pe.wait_ge(kept, n - 1)
                            for j in range(4):
                                t = 4 * half + j
                                last = pe.transpose(psum[0:w, n % 2, j * P:(j + 1) * P],
                                                    i[:, t].rearrange("p h c -> p (h c)")[:, f * P:f * P + w], ident[:])
                            last.then_inc(turned, 1)
                        pe.wait_ge(kept, len(units))
                        for b in range(NB):
                            h, half = b // 2, b % 2
                            rows = slice(32 * (h % 4), 32 * (h % 4) + 32)
                            if b >= 2:
                                pe.wait_ge(e_sub, b - 1)
                                pe.wait_ge(p_done, b - 1)
                                pe.wait_ge(a_done, b - 1)
                            for j in range(4):
                                t = 4 * half + j
                                last = pe.matmul(psum[:, 2 + b % 2, j * P:(j + 1) * P],
                                                 g[:, t, h:h + 1].broadcast_to([P, P]), tri[:], start=True, stop=True)
                            last.then_inc(e_in, 1)
                            for j in range(4):
                                t = 4 * half + j
                                last = pe.matmul(psum[:, 4 + b % 2, j * P:(j + 1) * P], KNT[rows, h // 4, t * P:(t + 1) * P],
                                                 QNT[rows, h // 4, t * P:(t + 1) * P], start=True, stop=True)
                            last.then_inc(p_in, 1)
                            for j in range(4):
                                t = 4 * half + j
                                last = pe.matmul(psum[:, 6 + b % 2, j * P:(j + 1) * P], KNT[rows, h // 4, t * P:(t + 1) * P],
                                                 KBT[rows, h // 4, t * P:(t + 1) * P], start=True, stop=True)
                            last.then_inc(a_in, 1)

                    @block.scalar
                    def _(act):
                        for n, (o, i, f, half) in enumerate(units):
                            w = P if f == 0 else QKW - P
                            act.wait_ge(turned, n + 1)
                            act.activation(o[0:w, f, half * HALF:(half + 1) * HALF], psum[0:w, n % 2, :],
                                           ACT.Copy).then_inc(kept, 1)
                        for b in range(NB):
                            act.wait_ge(e_sub, b + 1)
                            if b >= 1:
                                act.wait_ge(e_done, b)
                            act.activation(ed[:, b % 2], ed[:, b % 2], ACT.Exp).then_inc(e_exp, 1)

                    @block.vector
                    def _(dve):
                        for b in range(NB + 1):
                            if b < NB:
                                h, half = b // 2, b % 2
                                dve.wait_ge(e_in, b + 1)
                                if b >= 2:
                                    dve.wait_ge(e_done, b - 1)
                                for j in range(4):
                                    last = dve.tensor_scalar(ed[:, b % 2, j], psum[:, 2 + b % 2, j * P:(j + 1) * P],
                                                             G[:, 4 * half + j, h:h + 1], 0.0, ALU.subtract, ALU.min)
                                last.then_inc(e_sub, 1)
                            if b >= 1:
                                c = b - 1
                                blk = slice(4 * c, 4 * c + 4)
                                dve.wait_ge(e_exp, c + 1)
                                dve.tensor_tensor(EA[:, blk], ed[:, c % 2],
                                                  tri[:].unsqueeze(1).broadcast_to([P, 4, P]),
                                                  ALU.mult).then_inc(e_done, 1)
                                dve.wait_ge(e_done, c + 1)
                                dve.wait_ge(p_in, c + 1)
                                dve.tensor_tensor(PT[:, blk], psum[:, 4 + c % 2, :].rearrange("p (t n) -> p t n", t=4),
                                                  EA[:, blk], ALU.mult).then_inc(p_done, 1)
                                dve.wait_ge(p_done, c + 1)
                                dve.wait_ge(a_in, c + 1)
                                dve.scalar_tensor_tensor(EA[:, blk], psum[:, 6 + c % 2, :].rearrange("p (t n) -> p t n", t=4),
                                                         -1.0, EA[:, blk], ALU.mult, ALU.mult).then_inc(a_done, 1)

            norm_scope.close()

            TT = core.sb("t_inverse_transposed", [P, GH * NT, P], F32, mid_scope)
            nWT = core.sb("minus_w_features", [P, 2, S], F32, mid_scope)
            with ExitStack() as tmp2:
                sb2 = lambda n, shape, dt=F32: core.sb(n, shape, dt, tmp2)
                masks = sb2("level_masks", [P, 2, LEVELS, P], U32)
                T = sb2("t_inverse", [P, 2, 4, P])
                Xs = sb2("a_times_t", [P, 2, 4, P])
                mload, ident_in, t_init, a_turned = sem("masks"), sem("ident_in"), sem("t_init"), sem("a_turned")
                x_in, x_kept, y_in, t_upd, w_in, w_kept = (sem(n) for n in ("x_in", "x_kept", "y_in", "t_upd", "w_in", "w_kept"))
                NB = GH * 2
                L = LEVELS - 1
                with nc.Block() as block:
                    @block.sync
                    def _(sp):
                        sp.dma_start(masks[:].rearrange("p a l n -> p (a l n)"), d["masks"]).then_inc(mload, 16)

                    @block.tensor
                    def _(pe):
                        for grp in range(NB // 2):
                            for s in range(2):
                                b = 2 * grp + s
                                if grp >= 1:
                                    pe.wait_ge(w_kept, b - 1)
                                for j in range(4):
                                    last = pe.transpose(psum[:, 2 * s, j * P:(j + 1) * P], EA[:, 4 * b + j, :], ident[:])
                                last.then_inc(a_turned, 1)
                            for lv in range(L):
                                for s in range(2):
                                    b = 2 * grp + s
                                    pe.wait_ge(t_upd, 4 * (grp * (L + 1) + lv) + 2 * s + 2 - (0 if lv < L else 0))
                                    for j in range(4):
                                        last = pe.matmul(psum[:, 6 + s, j * P:(j + 1) * P], EA[:, 4 * b + j, :],
                                                         T[:, s, j, :], start=True, stop=True)
                                    last.then_inc(x_in, 1)
                                for s in range(2):
                                    b = 2 * grp + s
                                    pe.wait_ge(x_kept, 2 * (grp * L + lv) + s + 1)
                                    if lv < L - 1:
                                        for j in range(4):
                                            pe.matmul(psum[:, 2 * s, j * P:(j + 1) * P], TT[:, 4 * b + j, :],
                                                      Xs[:, s, j, :], start=True, stop=True)
                                    for j in range(4):
                                        last = pe.matmul(psum[:, 2 * s + 1, j * P:(j + 1) * P], Xs[:, s, j, :],
                                                         TT[:, 4 * b + j, :], start=True, stop=True)
                                    last.then_inc(y_in, 1)
                            for s in range(2):
                                b = 2 * grp + s
                                h, half = b // 2, b % 2
                                rows = slice(32 * (h % 4), 32 * (h % 4) + 32)
                                pe.wait_ge(t_upd, 4 * (grp * (L + 1) + L) + 2 * s + 2)
                                for j in range(4):
                                    t = 4 * half + j
                                    last = pe.matmul(psum[rows, 2 * s, j * P:(j + 1) * P], KBE[:, t, h, :],
                                                     TT[:, 4 * b + j, :], start=True, stop=True)
                                last.then_inc(w_in, 1)

                    @block.scalar
                    def _(act):
                        for grp in range(NB // 2):
                            for s in range(2):
                                b = 2 * grp + s
                                act.activation(TT[:, 4 * b:4 * b + 4, :], ident[:].unsqueeze(1).broadcast_to([P, 4, P]),
                                               ACT.Copy).then_inc(t_init, 1)
                                if grp >= 1:
                                    act.wait_ge(x_in, 2 * grp * L - (1 - s))
                                act.activation(T[:, s], ident[:].unsqueeze(1).broadcast_to([P, 4, P]),
                                               ACT.Copy).then_inc(t_init, 1)
                            for lv in range(L):
                                for s in range(2):
                                    act.wait_ge(x_in, 2 * (grp * L + lv) + s + 1)
                                    if grp * L + lv >= 1:
                                        act.wait_ge(y_in, 2 * (grp * L + lv - 1) + s + 1)
                                    act.activation(Xs[:, s], psum[:, 6 + s, :].rearrange("p (t n) -> p t n", t=4),
                                                   ACT.Copy).then_inc(x_kept, 1)
                            for s in range(2):
                                b = 2 * grp + s
                                h, half = b // 2, b % 2
                                rows = slice(32 * (h % 4), 32 * (h % 4) + 32)
                                act.wait_ge(w_in, b + 1)
                                act.activation(nWT[rows, h // 4, half * HALF:(half + 1) * HALF],
                                               psum[rows, 2 * s, :], ACT.Copy, scale=-1.0).then_inc(w_kept, 1)

                    @block.vector
                    def _(dve):
                        dve.wait_ge(mload, 16)
                        mk = lambda side, lv: masks[:, side, lv, :].unsqueeze(1).broadcast_to([P, 4, P])
                        for grp in range(NB // 2):
                            for lv in range(L + 1):
                                for s in range(2):
                                    b = 2 * grp + s
                                    blk = slice(4 * b, 4 * b + 4)
                                    if lv == 0:
                                        dve.wait_ge(a_turned, b + 1)
                                        dve.wait_ge(t_init, 2 * b + 2)
                                        src, srcT = psum[:, 2 * s, :].rearrange("p (t n) -> p t n", t=4), EA[:, blk]
                                    else:
                                        dve.wait_ge(y_in, 2 * (grp * L + lv - 1) + s + 1)
                                        src = psum[:, 2 * s, :].rearrange("p (t n) -> p t n", t=4)
                                        srcT = psum[:, 2 * s + 1, :].rearrange("p (t n) -> p t n", t=4)
                                    if lv < L:
                                        dve.copy_predicated(T[:, s], mk(0, lv), src).then_inc(t_upd, 1)
                                        dve.copy_predicated(TT[:, blk], mk(1, lv), srcT).then_inc(t_upd, 1)
                                    else:
                                        dve.copy_predicated(TT[:, blk], mk(1, lv), srcT).then_inc(t_upd, 2)

            O = core.sb("delta_out", [P, NT, VWD], F32, mid_scope)
            with ExitStack() as tmp2:
                sb2 = lambda n, shape, dt=F32: core.sb(n, shape, dt, tmp2)
                St = sb2("state", [P, 2, GV])
                SD = sb2("state_blocks", [P, 2, 4, GV])
                own = sb2("own_block", [P, 4, GV])
                U = sb2("u", [P, 2, VWD])
                s0, u_in, u_kept, s_in, s_done, o_in, o_kept = (sem(n) for n in
                    ("state_zeroed", "u_in", "u_kept", "s_in", "s_done", "o_in", "o_kept"))
                blocked, own_in = sem("state_blocked"), sem("own_loaded")
                WID = ((P, 4), (QKW - P, 2))
                with nc.Block() as block:
                    @block.sync
                    def _(sp):
                        sp.dma_start(own[:].rearrange("p a n -> p (a n)"), d["own"]).then_inc(own_in, 16)

                    @block.tensor
                    def _(pe):
                        def by_state(o, lhsT, t):
                            for f, (w, nh) in enumerate(WID):
                                last = pe.matmul(o[:, f * 4 * GV:(f * 4 + nh) * GV], lhsT[0:w, f, t * P:(t + 1) * P],
                                                 SD[0:w, f, 0:nh, :].rearrange("p a n -> p (a n)"),
                                                 start=False, stop=(f == 1), skip_group_check=True)
                            return last

                        for t in range(NT):
                            if t >= 2:
                                pe.wait_ge(u_kept, t - 1)
                            for h in range(GH):
                                pe.matmul(psum[:, t % 2, h * GV:(h + 1) * GV], TT[:, h * NT + t, :], BV[:, t, h, :],
                                          start=(h == 0), stop=False, skip_group_check=True)
                            pe.wait_ge(blocked, 2 * t + 2)
                            by_state(psum[:, t % 2, 0:VWD], nWT, t).then_inc(u_in, 1)
                            pe.wait_ge(u_kept, t + 1)
                            for h in range(GH):
                                rows = slice(32 * (h % 4), 32 * (h % 4) + 32)
                                last = pe.matmul(psum[rows, 4 + t % 2, (h // 4) * GV:(h // 4 + 1) * GV], KD[:, t, h, :],
                                                 U[:, t % 2, h * GV:(h + 1) * GV], start=True, stop=True)
                            last.then_inc(s_in, 1)
                            if t >= 2:
                                pe.wait_ge(o_kept, t - 1)
                            for h in range(GH):
                                pe.matmul(psum[:, 2 + t % 2, h * GV:(h + 1) * GV], PT[:, h * NT + t, :],
                                          U[:, t % 2, h * GV:(h + 1) * GV], start=(h == 0), stop=False,
                                          skip_group_check=True)
                            by_state(psum[:, 2 + t % 2, 0:VWD], QET, t).then_inc(o_in, 1)

                    @block.vector
                    def _(dve):
                        dve.memset(St[:], 0.0).then_inc(s0, 1)
                        dve.memset(SD[:], 0.0).then_inc(blocked, 2)
                        dve.wait_ge(s0, 1)
                        dve.wait_ge(own_in, 16)
                        dve.wait_ge(blocked, 2)
                        for t in range(NT):
                            dve.wait_ge(u_in, t + 1)
                            if t >= 2:
                                dve.wait_ge(s_in, t - 1)
                                dve.wait_ge(o_in, t - 1)
                            dve.tensor_copy(U[:, t % 2, :], psum[:, t % 2, 0:VWD]).then_inc(u_kept, 1)
                            dve.wait_ge(s_in, t + 1)
                            if t >= 1:
                                dve.wait_ge(blocked, 2 * t + 2)
                            for f, (w, nh) in enumerate(WID):
                                dve.scalar_tensor_tensor(St[0:w, f, :], St[0:w, f, :], ETH[0:w, f, t:t + 1],
                                                         psum[0:w, 4 + t % 2, f * GV:(f + 1) * GV],
                                                         ALU.mult, ALU.add).then_inc(s_done, 1)
                            dve.wait_ge(o_in, t + 1)
                            dve.wait_ge(s_done, 2 * t + 2)
                            for f, (w, nh) in enumerate(WID):
                                dve.tensor_tensor(SD[0:w, f, 0:nh, :], St[0:w, f, :].unsqueeze(1).broadcast_to([w, nh, GV]),
                                                  own[0:w, 0:nh, :], ALU.mult).then_inc(blocked, 1)

                    @block.scalar
                    def _(act):
                        for t in range(NT):
                            act.wait_ge(o_in, t + 1)
                            act.activation(O[:, t, :], psum[:, 2 + t % 2, 0:VWD], ACT.Copy).then_inc(o_kept, 1)

            with ExitStack() as tmp2:
                sb2 = lambda n, shape, dt=F32: core.sb(n, shape, dt, tmp2)
                sq = sb2("o_squares", [P, NT, VWD])
                ms, rr = sb2("o_mean_squares", [P, NT * GH]), sb2("o_inverse_rms", [P, NT * GH])
                ch, sw, sg_done, to_act, from_act = sem("norm_chain"), sem("gate_w"), sem("gate_w2"), sem("rms_in"), sem("rms_out")
                with nc.Block() as block:
                    @block.gpsimd
                    def _(pool):
                        for t in range(NT):
                            pool.tensor_tensor(SG[:, t].rearrange("p (h c) -> p h c", c=GV),
                                               SG[:, t].rearrange("p (h c) -> p h c", c=GV),
                                               nw[:].unsqueeze(1).broadcast_to([P, GH, GV]), ALU.mult).then_inc(sw, 1)

                    @block.scalar
                    def _(act):
                        act.wait_ge(to_act, 1)
                        act.activation(ms[:], ms[:], ACT.Sqrt).then_inc(from_act, 1)

                    @block.vector
                    def _(dve):
                        n = [0]

                        def link(i):
                            n[0] += 1
                            i.then_inc(ch, 1)
                            dve.wait_ge(ch, n[0])

                        link(dve.tensor_tensor(sq[:], O[:], O[:], ALU.mult))
                        link(dve.reduce_sum(ms[:], sq[:].rearrange("p t (h c) -> p (t h) c", c=GV), AX.X))
                        dve.tensor_scalar(ms[:], ms[:], 1.0 / GV, RMS_EPS, ALU.mult, ALU.add).then_inc(to_act, 1)
                        dve.wait_ge(from_act, 1)
                        link(dve.reciprocal(rr[:], ms[:]))
                        link(dve.tensor_tensor(O[:].rearrange("p t (h c) -> p (t h) c", c=GV),
                                               O[:].rearrange("p t (h c) -> p (t h) c", c=GV),
                                               rr[:].unsqueeze(2).broadcast_to([P, NT * GH, GV]), ALU.mult))
                        dve.wait_ge(sw, NT)
                        dve.tensor_tensor(O[:], O[:], SG[:], ALU.mult)

            project_out(nc, core, tag, O, wo, None, tiles=3)



NX = 8
RANK = 16
TOPK = 2
DH = 704
ALPHA = 2.0
FT = [(f * P, min(P, DH - f * P)) for f in range(-(-DH // P))]
NFT = len(FT)


def routed_weights(nc, core, d, scope):
    w = {
        "gate": core.sb("router", [P, KT, NX], F32, scope),
        "up": core.sb("w_up", [P, KT, DH], F32, scope), "gt": core.sb("w_gate", [P, KT, DH], F32, scope),
        "upA": core.sb("up_a", [P, KT, P], F32, scope), "gtA": core.sb("gate_a", [P, KT, P], F32, scope),
        "upB": core.sb("up_b", [P, DH], F32, scope), "gtB": core.sb("gate_b", [P, DH], F32, scope),
        "down": core.sb("w_down", [P, NFT, D], F32, scope), "dnA": core.sb("down_a", [P, NFT, P], F32, scope),
        "dnB": core.sb("down_b", [P, D], F32, scope), "expert": core.sb("expert_of_column", [P, P], F32, scope),
    }
    loaded = core.sem("routed_w_loaded")
    full = (NFT - 1) * P
    with nc.Block() as block:
        @block.sync
        def _(sp):
            n = 0
            for name in ("gate", "upA", "gtA", "up", "gt"):
                sp.dma_start(w[name][:], d[name].rearrange("(k p) n -> p k n", p=P)).then_inc(loaded, 16)
                n += 16
            for name in ("upB", "gtB", "dnB", "expert"):
                sp.dma_start(w[name][:], d[name]).then_inc(loaded, 16)
                n += 16
            for name in ("down", "dnA"):
                sp.dma_start(w[name][:, 0:NFT - 1, :], d[name][0:full, :].rearrange("(k p) n -> p k n", p=P)
                             ).then_inc(loaded, 16)
                sp.dma_start(w[name][0:DH - full, NFT - 1, :], d[name][full:DH, :]).then_inc(loaded, 16)
                n += 32
            sp.wait_ge(loaded, n)
    return w


def routed_layer(nc, core, tag, d):
    with ExitStack() as scope:
        w = routed_weights(nc, core, d, scope)
        norm_stage(nc, core, tag + "n")
        routed_ffn(nc, core, tag, w)


def routed_ffn(nc, core, tag, w):
    X, XNT, psum, ident = core.X, core.XNT, core.psum, core.ident
    sem = lambda n: core.sem(f"{tag}_{n}")
    with ExitStack() as tmp:
        sb = lambda n, shape, dt=F32: core.sb(n, shape, dt, tmp)
        MASK = sb("expert_mask", [P, TOPK, S])
        CB = sb("weight_rows", [P, TOPK, S])
        with ExitStack() as tmp2:
            sb2 = lambda n, shape, dt=F32: core.sb(n, shape, dt, tmp2)
            LG, m8 = sb2("logits", [P, NT, NX]), sb2("sorted", [P, NT, 8])
            ix, ixf = sb2("indices", [P, NT, 8], U32), sb2("indices_f", [P, NT, TOPK])
            pm, gm, ps_, rs = (sb2(n, [P, TOPK]) for n in ("part_max", "all_max", "part_sum", "inv_sum"))
            ev, cw = sb2("exp_top", [P, NT, TOPK]), sb2("weights", [P, NT, TOPK])
            mk = sb2("wide_rows", [P, 2, TOPK, NT, P])
            lg_in, lg_out, top, idx, ch = sem("logits"), sem("logits_kept"), sem("top"), sem("index"), sem("chain")
            pmax, gmax, dif, ex, tot, tot_in = sem("part_max"), sem("all_max"), sem("dif"), sem("exp"), sem("part_sum"), sem("total")
            wide, turned, kept = sem("wide"), sem("turned"), sem("kept")
            with nc.Block() as block:
                @block.tensor
                def _(pe):
                    for t in range(NT):
                        for k in range(KT):
                            last = pe.matmul(psum[:, 0, t * NX:(t + 1) * NX], XNT[:, k, t * P:(t + 1) * P],
                                             w["gate"][:, k, :], start=(k == 0), stop=(k == KT - 1))
                    last.then_inc(lg_in, 1)
                    pe.wait_ge(tot, 1)
                    pe.matmul(psum[:, 1, 0:TOPK], core.ones_sq[:], ps_[:], start=True, stop=True).then_inc(tot_in, 1)
                    n = 0
                    for kind in range(2):
                        pe.wait_ge(wide, kind + 1)
                        for k in range(TOPK):
                            for half in range(NH2):
                                if n >= 4:
                                    pe.wait_ge(kept, n - 3)
                                for j in range(4):
                                    last = pe.transpose(psum[:, 4 + n % 4, j * P:(j + 1) * P],
                                                        mk[:, kind, k, 4 * half + j, :], ident[:])
                                last.then_inc(turned, 1)
                                n += 1

                @block.gpsimd
                def _(pool):
                    pool.wait_ge(pmax, 1)
                    pool.partition_all_reduce(gm[:], pm[:], P, bass.bass_isa.ReduceOp.max).then_inc(gmax, 1)

                @block.scalar
                def _(act):
                    act.wait_ge(dif, 1)
                    act.activation(ev[:], ev[:], ACT.Exp).then_inc(ex, 1)
                    n = 0
                    for o in (MASK, CB):
                        for k in range(TOPK):
                            for half in range(NH2):
                                act.wait_ge(turned, n + 1)
                                act.activation(o[:, k, half * HALF:(half + 1) * HALF], psum[:, 4 + n % 4, :],
                                               ACT.Copy).then_inc(kept, 1)
                                n += 1

                @block.vector
                def _(dve):
                    c = [0]

                    def link(i):
                        c[0] += 1
                        i.then_inc(ch, 1)
                        dve.wait_ge(ch, c[0])

                    dve.wait_ge(lg_in, 1)
                    dve.tensor_copy(LG[:].rearrange("p t n -> p (t n)"), psum[:, 0, 0:NT * NX]).then_inc(lg_out, 1)
                    dve.wait_ge(lg_out, 1)
                    for t in range(NT):
                        dve.max(m8[:, t, :], LG[:, t, :]).then_inc(top, 1)
                    dve.wait_ge(top, NT)
                    dve.reduce_max(pm[:], m8[:, :, 0:TOPK].rearrange("p t k -> p k t"), AX.X).then_inc(pmax, 1)
                    for t in range(NT):
                        dve.max_index(ix[:, t, :], m8[:, t, :], LG[:, t, :]).then_inc(idx, 1)
                    dve.wait_ge(idx, NT)
                    link(dve.tensor_copy(ixf[:], ix[:, :, 0:TOPK]))
                    for k in range(TOPK):
                        for t in range(NT):
                            last = dve.tensor_scalar(mk[:, 0, k, t, :], w["expert"][:], ixf[:, t, k:k + 1], ALPHA,
                                                     ALU.is_equal, ALU.mult)
                    last.then_inc(wide, 1)
                    dve.wait_ge(gmax, 1)
                    dve.tensor_tensor(ev[:], m8[:, :, 0:TOPK], gm[:].unsqueeze(1).broadcast_to([P, NT, TOPK]),
                                      ALU.subtract).then_inc(dif, 1)
                    dve.wait_ge(ex, 1)
                    dve.reduce_sum(ps_[:], ev[:].rearrange("p t k -> p k t"), AX.X).then_inc(tot, 1)
                    dve.wait_ge(tot_in, 1)
                    link(dve.reciprocal(rs[:], psum[:, 1, 0:TOPK]))
                    link(dve.tensor_tensor(cw[:], ev[:], rs[:].unsqueeze(1).broadcast_to([P, NT, TOPK]), ALU.mult))
                    for k in range(TOPK):
                        for t in range(NT):
                            last = dve.tensor_scalar(mk[:, 1, k, t, :], core.ones_sq[:], cw[:, t, k:k + 1], None, ALU.mult)
                    last.then_inc(wide, 1)

        H = sb("slot_hidden", [P, TOPK, NFT, S])
        MX = sb("mixed_hidden", [P, NFT, S])
        DL = sb("lora_down", [P, S])
        with ExitStack() as tmp2:
            sb2 = lambda n, shape, dt=F32: core.sb(n, shape, dt, tmp2)
            Z = sb2("lora_in", [P, 2, TOPK, S])
            sil, gc = sb2("silu", [P, 2, HALF]), sb2("gate_weighted", [P, 2, HALF])
            z_in, z_done, up_in, silu, gated, hid, mixed = (sem(n) for n in
                ("z_in", "z_done", "up_in", "silu", "gated", "hidden", "mixed"))
            units = [(half, f, k) for half in range(NH2) for f in range(NFT) for k in range(TOPK)]
            with nc.Block() as block:
                @block.tensor
                def _(pe):
                    for half in range(NH2):
                        for j, wa in enumerate(("upA", "gtA")):
                            for k in range(KT):
                                last = pe.matmul(psum[:, 4 + 2 * half + j, :], w[wa][:, k, :],
                                                 XNT[:, k, half * HALF:(half + 1) * HALF],
                                                 start=(k == 0), stop=(k == KT - 1))
                            last.then_inc(z_in, 1)
                    for u, (half, f, k) in enumerate(units):
                        a, n = FT[f]
                        cols = slice(half * HALF, (half + 1) * HALF)
                        if u == 0:
                            pe.wait_ge(z_done, 2 * TOPK)
                        if (half, f, k) == (1, 0, 0):
                            pe.wait_ge(z_done, 4 * TOPK)
                        if u >= 2:
                            pe.wait_ge(silu, u - 1)
                            pe.wait_ge(gated, u - 1)
                        for j, (wb, wl) in enumerate((("up", "upB"), ("gt", "gtB"))):
                            o = psum[0:n, 2 * (u % 2) + j, :]
                            for kk in range(KT):
                                pe.matmul(o, w[wb][:, kk, a:a + n], XNT[:, kk, cols], start=(kk == 0), stop=False)
                            pe.matmul(o, w[wl][:, a:a + n], Z[:, j, k, cols], start=False, stop=True).then_inc(up_in, 1)

                @block.scalar
                def _(act):
                    for u, (half, f, k) in enumerate(units):
                        n = FT[f][1]
                        act.wait_ge(up_in, 2 * u + 1)
                        if u >= 2:
                            act.wait_ge(hid, u - 1)
                        act.activation(sil[0:n, u % 2, :], psum[0:n, 2 * (u % 2), :], ACT.Silu).then_inc(silu, 1)

                @block.vector
                def _(dve):
                    n = 0
                    for half in range(NH2):
                        for j in range(2):
                            dve.wait_ge(z_in, 2 * half + j + 1)
                            for k in range(TOPK):
                                dve.tensor_tensor(Z[:, j, k, half * HALF:(half + 1) * HALF], psum[:, 4 + 2 * half + j, :],
                                                  MASK[:, k, half * HALF:(half + 1) * HALF], ALU.mult).then_inc(z_done, 1)
                    for u, (half, f, k) in enumerate(units):
                        n = FT[f][1]
                        cols = slice(half * HALF, (half + 1) * HALF)
                        dve.wait_ge(up_in, 2 * u + 2)
                        dve.tensor_tensor(gc[0:n, u % 2, :], psum[0:n, 2 * (u % 2) + 1, :], CB[0:n, k, cols],
                                          ALU.mult).then_inc(gated, 1)
                        dve.wait_ge(gated, u + 1)
                        dve.wait_ge(silu, u + 1)
                        dve.tensor_tensor(H[0:n, k, f, cols], gc[0:n, u % 2, :], sil[0:n, u % 2, :],
                                          ALU.mult).then_inc(hid, 1)

                @block.gpsimd
                def _(pool):
                    for half in range(NH2):
                        for f in range(NFT):
                            n = FT[f][1]
                            cols = slice(half * HALF, (half + 1) * HALF)
                            pool.wait_ge(hid, TOPK * (half * NFT + f + 1))
                            pool.tensor_tensor(MX[0:n, f, cols], H[0:n, 0, f, cols], H[0:n, 1, f, cols],
                                               ALU.add).then_inc(mixed, 1)

        with ExitStack() as tmp2:
            d1 = core.sb("lora_down_second", [P, S], F32, tmp2)
            d_in, d_part, d_done, out_in, added = sem("d_in"), sem("d_part"), sem("d_done"), sem("out_in"), sem("added")
            with nc.Block() as block:
                @block.tensor
                def _(pe):
                    for half in range(NH2):
                        for k in range(TOPK):
                            for f, (a, n) in enumerate(FT):
                                last = pe.matmul(psum[:, 2 * half + k, :], w["dnA"][0:n, f, :],
                                                 H[0:n, k, f, half * HALF:(half + 1) * HALF],
                                                 start=(f == 0), stop=(f == NFT - 1))
                            last.then_inc(d_in, 1)
                    for t in range(NT):
                        if t >= 4:
                            pe.wait_ge(added, t - 3)
                        for f, (a, n) in enumerate(FT):
                            pe.matmul(psum[:, 4 + t % 4, 0:D], MX[0:n, f, t * P:(t + 1) * P], w["down"][0:n, f, :],
                                      start=(f == 0), stop=False)
                        pe.wait_ge(d_done, t // 4 + 1)
                        pe.matmul(psum[:, 4 + t % 4, 0:D], DL[:, t * P:(t + 1) * P], w["dnB"][:],
                                  start=False, stop=True).then_inc(out_in, 1)

                @block.vector
                def _(dve):
                    for half in range(NH2):
                        cols = slice(half * HALF, (half + 1) * HALF)
                        for k, o in enumerate((DL, d1)):
                            dve.wait_ge(d_in, 2 * half + k + 1)
                            dve.tensor_tensor(o[:, cols], psum[:, 2 * half + k, :], MASK[:, k, cols],
                                              ALU.mult).then_inc(d_part, 1)
                        dve.wait_ge(d_part, 2 * half + 2)
                        dve.tensor_tensor(DL[:, cols], DL[:, cols], d1[:, cols], ALU.add).then_inc(d_done, 1)
                    for t in range(NT):
                        dve.wait_ge(out_in, t + 1)
                        dve.tensor_tensor(X[:, t, :], psum[:, 4 + t % 4, 0:D], X[:, t, :], ALU.add).then_inc(added, 1)


LAT, RD = 64, 64
NOPE = LAT
QROWS = RD + HD
SHIFT = 96
NEG = -1e30


def latent_attention(nc, core, tag, d):
    X, XNT, psum, ident = core.X, core.XNT, core.psum, core.ident
    sem = lambda n: core.sem(f"{tag}_{n}")
    SC = float(1.0 / np.sqrt(np.float32(HD + RD)))
    with ExitStack() as tmp:
        sb = lambda n, shape, dt=F32: core.sb(n, shape, dt, tmp)
        V = sb("v_ones", [P, NT, HEADS, VW])
        O = sb("attended", [P, NT, D])
        wo = sb("wo", [P, KT, D])
        with ExitStack() as tmpA:
            sba = lambda n, shape, dt=F32: core.sb(n, shape, dt, tmpA)
            Q = sba("q_all", [P, HEADS, S])
            Qb = sba("q_all_bf16", [QROWS, HEADS, S], BF16)
            K = sba("k_head", [P, 3, S])
            Kb = sba("k_head_bf16", [QROWS, 3, S], BF16)
            kT = sba("k_features", [P, KT, S])
            with ExitStack() as tmp2:
                sb2 = lambda n, shape, dt=F32: core.sb(n, shape, dt, tmp2)
                w1 = sb2("w_latents", [P, KT, 3 * LAT])
                w1r = sb2("w_kr_rotated", [P, KT, RD])
                wq = sb2("w_q", [LAT, HEADS, QROWS])
                wqr = sb2("w_q_rotated", [LAT, HEADS, RD])
                wk, wv = sb2("w_ku", [LAT, D]), sb2("w_vu", [LAT, D])
                cos, sin = sb2("cos", [RD, S]), sb2("sin", [RD, S])
                L = sb2("latents", [LAT, 2, S])
                t1 = O[0:RD].rearrange("p (a t) n -> p a (t n)", a=2)
                t2 = sb2("by_sin", [RD, 2, S])
                loaded, rot, made = sem("loaded"), sem("rotated_w"), sem("made")
                l_in, l_out = sem("l_in"), sem("l_out")
                q_in, c_done, s_done, q_done, qn_done, qb_done = (sem(n) for n in
                    ("q_in", "by_cos", "by_sin", "q_rope", "q_plain", "q_bf16"))
                kr_ready, kfeat, kf_out, v_in, v_out = sem("kr_ready"), sem("kf_in"), sem("kf_out"), sem("v_in"), sem("v_out")
                krep, q_zeroed = sem("kr_copies"), sem("q_rows_zeroed")
                pair = lambda b: psum[:, 2 * b:2 * b + 2, :].rearrange("p a n -> p (a n)")
                with nc.Block() as block:
                    @block.sync
                    def _(sp):
                        sp.dma_start(w1[:], d["w1"].rearrange("(k p) n -> p k n", p=P)).then_inc(loaded, 16)
                        sp.dma_start(wq[:].rearrange("p h n -> p (h n)"), d["wq"]).then_inc(loaded, 16)
                        sp.dma_start(wk[:], d["wku"]).then_inc(loaded, 16)
                        sp.dma_start(wv[:], d["wvu"]).then_inc(loaded, 16)
                        sp.dma_start(cos[:], d["cos"]).then_inc(loaded, 16)
                        sp.dma_start(sin[:], d["sin"]).then_inc(loaded, 16)
                        sp.dma_start(wo[:], d["wo"].rearrange("(k p) n -> p k n", p=P)).then_inc(loaded, 16)
                        sp.wait_ge(loaded, 16 * 7)

                    @block.gpsimd
                    def _(pool):
                        pool.memset(V[:], 0.0).then_inc(made, 1)
                        pool.wait_ge(made, 1)
                        pool.memset(V[:, :, :, HD:HD + 1], 1.0).then_inc(made, 1)
                        pool.wait_ge(made, 2)
                        pool.memset(K[64:96, :, :], 0.0).then_inc(made, 1)
                        pool.wait_ge(made, 3)
                        pool.memset(K[SHIFT:SHIFT + 1, :, :], 1.0).then_inc(made, 1)
                        for n in range(1 + HEADS):
                            pool.wait_ge(c_done, n + 1)
                            pool.wait_ge(s_done, n + 1)
                            if n == 0:
                                pool.tensor_tensor(K[0:RD, 0, :], t1[:, 0, :], t2[:, 0, :], ALU.add).then_inc(q_done, 1)
                            else:
                                pool.tensor_tensor(Q[0:RD, n - 1, :], t1[:, n % 2, :], t2[:, n % 2, :],
                                                   ALU.add).then_inc(q_done, 1)

                    @block.tensor
                    def _(pe):
                        pe.wait_ge(rot, 3)
                        for n, wsl in enumerate((w1[:, :, 0:LAT], w1[:, :, LAT:2 * LAT], w1[:, :, 2 * LAT:], w1r[:, :, :])):
                            for half in range(NH2):
                                for k in range(KT):
                                    last = pe.matmul(psum[0:LAT, 2 * n + half, :], wsl[:, k, :],
                                                     XNT[:, k, half * HALF:(half + 1) * HALF],
                                                     start=(k == 0), stop=(k == KT - 1))
                            last.then_inc(l_in, 1)
                        pe.wait_ge(l_out, 2)
                        for f in range(KT):
                            for half in range(NH2):
                                last = pe.matmul(psum[:, 2 * f + half, :], wk[:, f * P:(f + 1) * P],
                                                 L[:, 1, half * HALF:(half + 1) * HALF], start=True, stop=True)
                            last.then_inc(kfeat, 1)
                        for t in range(NT):
                            pe.wait_ge(kf_out, 2)
                            if t >= 2:
                                pe.wait_ge(v_out, t - 1)
                            pe.matmul(psum[:, t % 2, 0:D], L[:, 1, t * P:(t + 1) * P], wv[:], start=True,
                                      stop=True).then_inc(v_in, 1)
                        for h in range(HEADS):
                            b = 2 * (h % 2)
                            if h == 0:
                                pe.wait_ge(v_out, NT)
                                pe.wait_ge(c_done, 1)
                                pe.wait_ge(s_done, 1)
                            if h >= 2:
                                pe.wait_ge(c_done, h)
                                pe.wait_ge(s_done, h)
                                pe.wait_ge(qn_done, h - 1)
                            for half in range(NH2):
                                pe.matmul(psum[0:QROWS, 2 * b + half, :], wq[:, h, :], L[:, 0, half * HALF:(half + 1) * HALF],
                                          start=True, stop=True)
                            for half in range(NH2):
                                last = pe.matmul(psum[0:RD, 2 * b + 2 + half, :], wqr[:, h, :],
                                                 L[:, 0, half * HALF:(half + 1) * HALF], start=True, stop=True)
                            last.then_inc(q_in, 1)

                    @block.scalar
                    def _(act):
                        for n in range(2):
                            act.wait_ge(l_in, n + 1)
                            act.activation(L[:, n, :], pair(n)[0:LAT], ACT.Copy).then_inc(l_out, 1)
                        for f in range(KT):
                            act.wait_ge(kfeat, f + 1)
                            act.activation(kT[:, f, :], pair(f), ACT.Copy).then_inc(kf_out, 1)
                        act.wait_ge(made, 2)
                        for t in range(NT):
                            act.wait_ge(v_in, t + 1)
                            act.activation(V[:, t, :, 0:HD], psum[:, t % 2, 0:D].rearrange("p (h d) -> p h d", d=HD),
                                           ACT.Copy).then_inc(v_out, 1)
                        act.wait_ge(q_done, 1)
                        for b in range(1, 3):
                            act.activation(K[0:RD, b, :], K[0:RD, 0, :], ACT.Copy).then_inc(krep, 1)
                        for b in range(3):
                            act.activation(Kb[0:RD, b, :], K[0:RD, 0, :], ACT.Copy).then_inc(krep, 1)
                        act.wait_ge(q_zeroed, 1)
                        for h in range(HEADS + 1):
                            if h < HEADS:
                                b = 2 * (h % 2)
                                act.wait_ge(q_in, h + 1)
                                act.activation(Q[NOPE:QROWS, h, :], pair(b)[NOPE:QROWS], ACT.Copy).then_inc(qn_done, 1)
                            if h >= 1:
                                act.wait_ge(q_done, h + 1)
                                act.wait_ge(qn_done, h)
                                act.activation(Qb[:, h - 1, :], Q[0:QROWS, h - 1, :], ACT.Copy).then_inc(qb_done, 1)

                    @block.vector
                    def _(dve):
                        dve.wait_ge(loaded, 16 * 7)
                        hf = RD // 2
                        kr = w1[:, :, 2 * LAT:]
                        dve.tensor_scalar(w1r[:, :, 0:hf], kr[:, :, hf:], -1.0, None, ALU.mult).then_inc(rot, 1)
                        dve.tensor_copy(w1r[:, :, hf:], kr[:, :, 0:hf])
                        dve.tensor_scalar(wqr[:, :, 0:hf], wq[:, :, hf:RD], -1.0, None, ALU.mult).then_inc(rot, 1)
                        dve.tensor_copy(wqr[:, :, hf:], wq[:, :, 0:hf]).then_inc(rot, 1)
                        dve.memset(Q[64:96, :, :], 0.0).then_inc(q_zeroed, 1)
                        for n in range(1 + HEADS):
                            if n == 0:
                                dve.wait_ge(l_in, 4)
                                p, r = pair(2)[0:RD], pair(3)[0:RD]
                            else:
                                dve.wait_ge(q_in, n)
                                b = 2 * ((n - 1) % 2)
                                p, r = pair(b)[0:RD], pair(b + 1)[0:RD]
                            if n >= 2:
                                dve.wait_ge(q_done, n - 1)
                            dve.tensor_tensor(t1[:, n % 2, :], p, cos[:], ALU.mult).then_inc(c_done, 1)
                            dve.tensor_tensor(t2[:, n % 2, :], r, sin[:], ALU.mult).then_inc(s_done, 1)

            PB = 4
            with ExitStack() as tmp2:
                sb2 = lambda n, shape, dt=F32: core.sb(n, shape, dt, tmp2)
                mx = sb2("row_max_halves", [P, 2, NT, NH2])
                nm = sb2("minus_max", [P, 2, NT])
                nmT = sb2("minus_max_rows", [NT, 2, P])
                pr = sb2("probs", [P, PB, S])
                oT = sb2("out_features", [P, 2, D])
                rc = sb2("reciprocals", [P, 2, 2, 4])
                idb = sb2("identity_bf16", [P, P], BF16)
                mQ, mK = sb2("mask_by_query", [P, P], BF16), sb2("mask_by_key", [P, P], BF16)
                setup, k_in, kb_done = sem("masks"), [sem("k_in_even"), sem("k_in_odd")], sem("k_bf16")
                m_ready, m_half, m_done = sem("max_scores"), sem("max_halves"), sem("minus_max")
                mt_ready, mt_done, shift_in = sem("max_transposed"), sem("max_row"), sem("shift_row")
                s_ready, e_done, pv_ready = sem("scores"), sem("exp"), sem("values_summed")
                o_kept, o_turned, r_done, o_done = sem("out_kept"), sem("out_transposed"), sem("recip"), sem("out_done")
                MB, PVB, TB = 4, 6, 7
                pieces = lambda qt: [(a, min(a + HALF, (qt + 1) * P)) for a in range(0, (qt + 1) * P, HALF)]
                PIECES = [(qt, i, a, b) for qt in range(NT) for i, (a, b) in enumerate(pieces(qt))]
                per_head = len(PIECES)
                first = [next(n for n, x in enumerate(PIECES) if x[0] == qt) for qt in range(NT)]
                with nc.Block() as block:
                    @block.gpsimd
                    def _(pool):
                        pool.memset(mQ[:], 0.0).then_inc(setup, 1)
                        pool.wait_ge(setup, 1)
                        pool.memset(mK[:], 0.0).then_inc(setup, 1)
                        pool.wait_ge(setup, 2)
                        pool.affine_select(out=mQ[:], in_=mQ[:], compare_op=ALU.is_ge, fill=NEG, base=0,
                                           pattern=[[-1, P]], channel_multiplier=1).then_inc(setup, 1)
                        pool.wait_ge(setup, 3)
                        pool.affine_select(out=mK[:], in_=mK[:], compare_op=ALU.is_ge, fill=NEG, base=0,
                                           pattern=[[1, P]], channel_multiplier=-1).then_inc(setup, 1)
                        pool.wait_ge(setup, 4)
                        pool.tensor_copy(idb[:], ident[:]).then_inc(setup, 1)
                        pool.wait_ge(setup, 5)
                        for h in range(HEADS):
                            if h >= 1:
                                pool.wait_ge(kb_done, h)
                            pool.wait_ge(k_in[h % 2], 16 * (h // 2 + 1))
                            if h >= 3:
                                pool.wait_ge(m_ready, per_head * (h - 2))
                            pool.tensor_copy(Kb[NOPE:QROWS, h % 3, :], K[NOPE:QROWS, h % 3, :]).then_inc(kb_done, 1)

                    @block.sync
                    def _(sp):
                        def key_rows(h):
                            if h >= 3:
                                sp.wait_ge(s_ready, NT * (h - 2))
                                sp.wait_ge(kb_done, h - 2)
                            sp.dma_start(K[NOPE:QROWS, h % 3, :], kT[(h % 8) * HD:(h % 8 + 1) * HD, h // 8, :]
                                         ).then_inc(k_in[h % 2], 16)
                        key_rows(0)
                        key_rows(1)
                        for h in range(HEADS):
                            sp.wait_ge(mt_done, h + 1)
                            sp.dma_start(Q[SHIFT:SHIFT + 1, h, :].rearrange("a (t p) -> a t p", t=NT),
                                         nmT[:, h % 2, :]).then_inc(shift_in, 16)
                            if h + 2 < HEADS:
                                key_rows(h + 2)

                    @block.tensor
                    def _(pe):
                        def max_scores(h, qt):
                            if qt == 0:
                                pe.wait_ge(kb_done, h + 1)
                            for i, (a, b) in enumerate(pieces(qt)):
                                n = h * per_head + first[qt] + i
                                if n >= 2:
                                    pe.wait_ge(m_half, n - 1)
                                own = i == len(pieces(qt)) - 1
                                last = pe.matmul(psum[:, MB + n % 2, 0:b - a], Qb[:, h, qt * P:(qt + 1) * P],
                                                 Kb[:, h % 3, a:b], start=True, stop=not own)
                                if own:
                                    last = pe.matmul(psum[:, MB + n % 2, b - a - P:b - a], idb[:], mQ[:],
                                                     start=False, stop=True)
                                last.then_inc(m_ready, 1)

                        def turn_max(h):
                            pe.wait_ge(m_done, h + 1)
                            if h >= 1:
                                pe.wait_ge(mt_done, h)
                                if h >= 2:
                                    pe.wait_ge(o_done, h - 1)
                            pe.transpose(psum[0:NT, TB, 2 * P:3 * P], nm[:, h % 2, :], ident[:]).then_inc(mt_ready, 1)

                        def key_scores(h, c):
                            n = h * NT + c
                            if c == 0:
                                pe.wait_ge(shift_in, 16 * (h + 1))
                            if n >= 2:
                                pe.wait_ge(e_done, n - 1)
                            q0 = c * P
                            for half in range(q0 // HALF, NH2):
                                a = max(q0, half * HALF)
                                o = psum[:, 2 * (n % 2) + half, a - half * HALF:]
                                own = a == q0
                                last = pe.matmul(o, K[0:SHIFT + 1, h % 3, c * P:(c + 1) * P],
                                                 Q[0:SHIFT + 1, h, a:(half + 1) * HALF], start=True, stop=not own)
                                if own:
                                    last = pe.matmul(o[:, 0:P], idb[:], mK[:], start=False, stop=True)
                            last.then_inc(s_ready, 1)

                        def values(h, c):
                            n = h * NT + c
                            pe.wait_ge(e_done, n + 1)
                            if c == 0 and h >= 1:
                                pe.wait_ge(o_kept, h)
                            for g in range(c // 2, 4):
                                a = max(c * P, g * D)
                                last = pe.matmul(psum[32 * g:32 * g + VW, PVB, a - g * D:D], V[:, c, h, :],
                                                 pr[:, n % PB, a:(g + 1) * D], start=(c == 0), stop=(c == 2 * g + 1))
                            last.then_inc(pv_ready, 1)

                        def turn_out(h):
                            pe.wait_ge(o_kept, h + 1)
                            if h >= 1:
                                pe.wait_ge(o_done, h)
                                pe.wait_ge(mt_done, min(h + 2, HEADS))
                            for b in range(2):
                                last = pe.transpose(psum[:, TB, b * P:(b + 1) * P], oT[:, h % 2, b * P:(b + 1) * P],
                                                    ident[:])
                            last.then_inc(o_turned, 1)

                        pe.wait_ge(setup, 5)
                        for qt in range(NT):
                            max_scores(0, qt)
                        turn_max(0)
                        for h in range(HEADS):
                            for c in range(NT):
                                key_scores(h, c)
                                if h + 1 < HEADS:
                                    max_scores(h + 1, c)
                                if c >= 1:
                                    values(h, c - 1)
                            if h + 1 < HEADS:
                                turn_max(h + 1)
                            values(h, NT - 1)
                            turn_out(h)

                    @block.vector
                    def _(dve):
                        def row_max(h, qt):
                            for i, (a, b) in enumerate(pieces(qt)):
                                n = h * per_head + first[qt] + i
                                dve.wait_ge(m_ready, n + 1)
                                dve.reduce_max(mx[:, h % 2, qt, i:i + 1], psum[:, MB + n % 2, 0:b - a], AX.X
                                               ).then_inc(m_half, 1)

                        def minus_max(h):
                            dve.wait_ge(m_half, (h + 1) * per_head)
                            if h >= 2:
                                dve.wait_ge(mt_ready, h - 1)
                            dve.tensor_reduce(nm[:, h % 2, :], mx[:, h % 2, :, :], AX.X, ALU.max,
                                              negate=True).then_inc(m_done, 1)
                            dve.wait_ge(mt_ready, h + 1)
                            if h >= 2:
                                dve.wait_ge(shift_in, 16 * (h - 1))
                            dve.tensor_copy(nmT[:, h % 2, :], psum[0:NT, TB, 2 * P:3 * P]).then_inc(mt_done, 1)

                        def keep_out(h):
                            dve.wait_ge(pv_ready, (h + 1) * NT)
                            dve.tensor_copy(oT[:, h % 2, :], psum[:, PVB, 0:D]).then_inc(o_kept, 1)

                        def finish(h):
                            dve.wait_ge(o_turned, h + 1)
                            t4 = psum[:, TB, 0:D].rearrange("p (b g d) -> p b g d", b=2, g=4)
                            dve.reciprocal(rc[:, h % 2, :, :], t4[:, :, :, HD]).then_inc(r_done, 1)
                            dve.wait_ge(r_done, h + 1)
                            for b in range(2):
                                last = dve.tensor_tensor(
                                    O[:].rearrange("p (g b) n -> p b g n", b=2)[:, b, :, h * HD:(h + 1) * HD],
                                    t4[:, b, :, 0:HD],
                                    rc[:, h % 2, b, :].unsqueeze(2).broadcast_to([P, 4, HD]), ALU.mult)
                            last.then_inc(o_done, 1)

                        for b in range(2):
                            last = dve.memset(mx[:, b, 0:4, 1:2], -3e38)
                        for qt in range(NT):
                            row_max(0, qt)
                        minus_max(0)
                        for h in range(HEADS):
                            for c in range(NT):
                                if h + 1 < HEADS:
                                    row_max(h + 1, c)
                            if h + 1 < HEADS:
                                minus_max(h + 1)
                            keep_out(h)
                            finish(h)

                    @block.scalar
                    def _(act):
                        for h in range(HEADS):
                            for c in range(NT):
                                n = h * NT + c
                                act.wait_ge(s_ready, n + 1)
                                if n >= PB:
                                    act.wait_ge(pv_ready, n - PB + 1)
                                act.activation(pr[:, n % PB, c * P:],
                                               psum[:, 2 * (n % 2):2 * (n % 2) + 2, :].rearrange("p a n -> p (a n)")[:, c * P:],
                                               ACT.Exp, scale=SC).then_inc(e_done, 1)

        project_out(nc, core, tag, O, wo, None)


def store_output(nc, core, out_dram):
    stored = core.stored
    with nc.Block() as block:
        @block.sync
        def _(sp):
            sp.dma_start(out_dram.rearrange("(t p) d -> p t d", p=P), core.X[:]).then_inc(stored, 16)
            sp.wait_ge(stored, 16)


def build(nc, a, out):
    with ExitStack() as ctx:
        core = Core(nc, ctx)
        load_inputs(nc, core, a["x"])
        if STAGES >= 1:
            norm_stage(nc, core, "n1")
            attention16(nc, core, "aa", a["a_wq"], a["a_wk"], a["a_wv"], a["a_wo"],
                        {"bqk": a["a_bqk"], "bv": a["a_bv"], "bo": a["a_bo"]},
                        {"justice": a["a_justice"], "order": a["a_order"]}, a["pos"])
            core.layer_done()
        if STAGES >= 2:
            ternary_scope = ExitStack()
            ternary = ternary_weights(nc, core, ternary_scope, a["f_up"], a["f_gate"], a["f_down"])
            norm_stage(nc, core, "n2")
            ternary_ffn(nc, core, "f0", ternary)
            core.layer_done()
        if STAGES >= 3:
            norm_stage(nc, core, "n3")
            gated_delta(nc, core, "gd", {k[2:]: a[k] for k in a if k.startswith("g_")})
            core.layer_done()
        if STAGES >= 4:
            norm_stage(nc, core, "n4")
            ternary_ffn(nc, core, "f1", ternary)
            ternary_scope.close()
            core.layer_done()
        if STAGES >= 5:
            norm_stage(nc, core, "n5")
            attention16(nc, core, "ac", a["c_wq"], a["c_wk"], a["c_wv"], a["c_wo"], {"bo": a["c_bo"]}, None, None)
            core.layer_done()
        if STAGES >= 6:
            routed_layer(nc, core, "r0", {k[2:]: a[k] for k in a if k.startswith("r_")})
            core.layer_done()
        if STAGES >= 7:
            norm_stage(nc, core, "n7")
            latent_attention(nc, core, "la", {k[2:]: a[k] for k in a if k.startswith("m_")})
            core.layer_done()
        if STAGES >= 8:
            routed_layer(nc, core, "r1", {k[2:]: a[k] for k in a if k.startswith("r_")})
        store_output(nc, core, out)


def lay_out(inputs):
    c = np.ascontiguousarray
    i = {k: np.asarray(v) for k, v in inputs.items()}
    a = {
        "x": c(i["L0_attn_a_hidden_states"][0]),
        "a_wq": c(i["L0_attn_a_Wq"].T), "a_wk": c(i["L0_attn_a_Wk"].T), "a_wv": c(i["L0_attn_a_Wv"].T),
        "a_wo": c(i["L0_attn_a_Wo"].T),
        "a_bqk": c(np.concatenate([i["L0_attn_a_bq"].reshape(KT, P).T, i["L0_attn_a_bk"].reshape(KT, P).T], axis=1)),
        "a_bv": c(i["L0_attn_a_bv"]),
        "a_bo": c(i["L0_attn_a_bo"]),
        "a_justice": c(i["L0_attn_a_justice_gate"]), "a_order": c(i["L0_attn_a_order_gate"]),
        "pos": c((np.arange(S, dtype=np.float32) / S).reshape(NT, P).T),
        "f_up": c(i["L0_ffn_W_up"].T), "f_gate": c(i["L0_ffn_W_gate"].T), "f_down": c(i["L0_ffn_W_down"].T),
    }
    cat = np.concatenate
    b = {k[len("L0_attn_b_"):]: v for k, v in i.items() if k.startswith("L0_attn_b_")}
    conv = cat([b["conv_wq"], b["conv_wk"], b["conv_wv"]], axis=0)
    a.update({
        "g_wqkv": c(cat([b["Wq"], b["Wk"], b["Wv"]], axis=1)),
        "g_wgab": c(cat([b["Wg"], b["Wa"], b["Wb"]], axis=1)),
        "g_conv": c(conv.reshape(NF, P, TAPS).transpose(1, 0, 2).reshape(P, NF * TAPS)),
        "g_wo": c(b["Wo"]), "g_nw": c(b["norm_weight"]), "g_dt": c(b["dt_bias"]), "g_alog": c(b["A_log"]),
        "g_masks": level_masks(),
        "g_own": c(np.repeat(np.repeat(np.eye(4, dtype=np.float32), GK, axis=0), GV, axis=1)),
    })
    w = i["L1_attn_a_Wqkv"].reshape(HEADS, 3, HD, D)
    a.update({
        "c_wq": c(w[:, 0].reshape(D, D).T), "c_wk": c(w[:, 1].reshape(D, D).T), "c_wv": c(w[:, 2].reshape(D, D).T),
        "c_wo": c(i["L1_attn_a_Wproj"].T), "c_bo": c(i["L1_attn_a_bproj"]),
    })
    r = {k[len("L1_ffn_"):]: v for k, v in i.items() if k.startswith("L1_ffn_")}
    a.update({
        "r_gate": c(r["gate_w"].T), "r_up": c(r["w_up"].T), "r_gt": c(r["w_gate"].T), "r_down": c(r["w_down"].T),
        "r_upA": c(r["up_A"].reshape(P, D).T), "r_gtA": c(r["gate_A"].reshape(P, D).T),
        "r_upB": c(r["up_B"].transpose(0, 2, 1).reshape(P, DH)), "r_gtB": c(r["gate_B"].transpose(0, 2, 1).reshape(P, DH)),
        "r_dnA": c(r["down_A"].reshape(P, DH).T), "r_dnB": c(r["down_B"].transpose(0, 2, 1).reshape(P, D)),
        "r_expert": c(np.broadcast_to((np.arange(P) // RANK).astype(np.float32), (P, P))),
    })
    m = {k[len("L1_attn_b_"):]: v for k, v in i.items() if k.startswith("L1_attn_b_")}
    cos, sin = rope_tables()
    a.update({
        "m_w1": c(cat([m["Wqd"], m["Wkvd"], m["Wkr"]], axis=1)),
        "m_wq": c(cat([m["Wqr"].reshape(LAT, HEADS, RD), m["Wqu"].reshape(LAT, HEADS, HD)], axis=2).reshape(LAT, -1)),
        "m_wku": c(m["Wku"]), "m_wvu": c(m["Wvu"]), "m_wo": c(m["Wo"]), "m_cos": cos, "m_sin": sin,
    })
    return a


def rope_tables():
    freqs = 1.0 / 10000.0 ** (np.arange(0, RD, 2, dtype=np.float32) / RD)
    ang = np.outer(np.arange(S, dtype=np.float32), freqs)
    return (np.ascontiguousarray(np.tile(np.cos(ang), (1, 2)).T.astype(np.float32)),
            np.ascontiguousarray(np.tile(np.sin(ang), (1, 2)).T.astype(np.float32)))


def level_masks():
    row, col = np.arange(P)[:, None], np.arange(P)[None, :]
    below = [((row >> (n + 1)) == (col >> (n + 1))) & ((row >> n) > (col >> n)) for n in range(LEVELS)]
    both = [[m.astype(np.uint32) for m in below], [m.T.astype(np.uint32) for m in below]]
    return np.ascontiguousarray(np.stack([np.stack(x) for x in both]).transpose(2, 0, 1, 3).reshape(P, -1))


def kernel(**inputs):
    import concourse.bacc as bacc
    from concourse.bass_utils import run_bass_kernel_spmd

    nc = bacc.Bacc("TRN2", target_bir_lowering=False, num_devices=1)
    arrays = lay_out(inputs)
    aps = {n: nc.dram_tensor(f"in_{n}", v.shape, mybir.dt.from_np(v.dtype), kind="ExternalInput").ap()
           for n, v in arrays.items()}
    out = nc.dram_tensor("out", (S, D), F32, kind="ExternalOutput").ap()
    build(nc, aps, out)
    r = run_bass_kernel_spmd(nc, [{f"in_{n}": v for n, v in arrays.items()}], core_ids=[0])
    return r.results[0]["out"].reshape(1, S, D)
```

```python
from contextlib import ExitStack

import numpy as np

import concourse.bass as bass
from concourse import mybir

F32 = mybir.dt.float32
BF16 = mybir.dt.bfloat16
U32 = mybir.dt.uint32
ALU = mybir.AluOpType
ACT = mybir.ActivationFunctionType
AX = mybir.AxisListType

P = 128
S = 1024
D = 256
NT = S // P
KT = D // P
HALF = 512
NH2 = S // HALF
HEADS = 16
HD = D // HEADS
LN_EPS = 1e-5
STAGES = 8


class Core:

    def __init__(self, nc, ctx):
        self.nc, self.ctx, self.n, self.sems = nc, ctx, 0, []
        self.X = self.sb("x_tokens", [P, NT, D], F32)
        self.XNT = self.sb("xn_features", [P, KT, S], F32)
        self.ident = self.sb("identity", [P, P], F32)
        self.ones = self.sb("ones_row", [1, P], F32)
        self.ones_sq = self.sb("ones_square", [P, P], F32)
        self.bank = [self.ps(f"bank{i}", [P, HALF], F32) for i in range(8)] if False else None
        self.stored = nc.alloc_semaphore("stored")
        self.psum = self.ps("psum", [P, 8, HALF], F32)

    def sb(self, name, shape, dt, ctx=None):
        self.n += 1
        return (ctx or self.ctx).enter_context(self.nc.sbuf_tensor(f"{name}_{self.n}", shape, dt))

    def ps(self, name, shape, dt):
        return self.ctx.enter_context(self.nc.psum_tensor(name, shape, dt))

    def sem(self, name):
        self.n += 1
        self.sems.append(self.nc.alloc_semaphore(f"{name}_{self.n}"))
        return self.sems[-1]

    def layer_done(self):
        self.nc.clear_and_free_semaphores(self.sems)
        self.sems = []
        self.nc.all_engine_barrier()


def load_inputs(nc, core, x_dram):
    X, ident = core.X, core.ident
    x_loaded, zeroed, made = core.sem("x_loaded"), core.sem("ident_zeroed"), core.sem("consts_made")
    with nc.Block() as block:
        @block.sync
        def _(sp):
            sp.dma_start(X[:], x_dram.rearrange("(t p) d -> p t d", p=P)).then_inc(x_loaded, 16)
            sp.wait_ge(x_loaded, 16)

        @block.gpsimd
        def _(pool):
            pool.memset(ident[:], 0.0).then_inc(zeroed, 1)
            pool.memset(core.ones[:], 1.0).then_inc(made, 1)
            pool.memset(core.ones_sq[:], 1.0).then_inc(made, 1)
            pool.wait_ge(zeroed, 1)
            pool.affine_select(out=ident[:], in_=ident[:], compare_op=ALU.not_equal, fill=1.0, base=0,
                               pattern=[[-1, P]], channel_multiplier=1).then_inc(made, 1)


def norm_stage(nc, core, tag):
    X, XNT, ident, psum = core.X, core.XNT, core.ident, core.psum
    stat_done, mv_done, var_done = (core.sem(tag + n) for n in ("_stats", "_mean_var", "_var_eps"))
    std_done, rstd_done, xn_done = (core.sem(tag + n) for n in ("_std", "_rstd", "_xn"))
    turned, taken = core.sem(tag + "_transposed"), core.sem(tag + "_taken")
    with ExitStack() as tmp:
        st = core.sb("bn_stats", [P, NT, 6], F32, tmp)
        mv = core.sb("mean_var", [P, NT, 2], F32, tmp)
        ve = core.sb("var_eps", [P, NT], F32, tmp)
        std = core.sb("std", [P, NT], F32, tmp)
        rstd = core.sb("rstd", [P, NT], F32, tmp)
        xn = core.sb("xn", [P, NT, D], F32, tmp)
        with nc.Block() as block:
            @block.vector
            def _(dve):
                for t in range(NT):
                    dve.bn_stats(st[:, t, :], X[:, t, :]).then_inc(stat_done, 1)
                for t in range(NT):
                    dve.wait_ge(stat_done, t + 1)
                    dve.bn_aggr(mv[:, t, :], st[:, t, :]).then_inc(mv_done, 1)
                dve.wait_ge(mv_done, NT)
                dve.tensor_scalar(ve[:], mv[:, :, 1], LN_EPS, None, ALU.add).then_inc(var_done, 1)
                dve.wait_ge(std_done, 1)
                dve.reciprocal(rstd[:], std[:]).then_inc(rstd_done, 1)
                dve.wait_ge(rstd_done, 1)
                for t in range(NT):
                    dve.tensor_scalar(xn[:, t, :], X[:, t, :], mv[:, t, 0:1], rstd[:, t:t + 1],
                                      ALU.subtract, ALU.mult).then_inc(xn_done, 1)
                for half in range(NH2):
                    dve.wait_ge(turned, 2 * half + 2)
                    dve.tensor_copy(XNT[:, 1, half * HALF:(half + 1) * HALF],
                                    psum[:, 2 * half + 1, :]).then_inc(taken, 1)

            @block.scalar
            def _(act):
                act.wait_ge(var_done, 1)
                act.activation(std[:], ve[:], ACT.Sqrt).then_inc(std_done, 1)
                for half in range(NH2):
                    act.wait_ge(turned, 2 * half + 1)
                    act.activation(XNT[:, 0, half * HALF:(half + 1) * HALF], psum[:, 2 * half, :],
                                   ACT.Copy).then_inc(taken, 1)

            @block.tensor
            def _(pe):
                for half in range(NH2):
                    for f in range(KT):
                        for i in range(4):
                            t = 4 * half + i
                            pe.wait_ge(xn_done, t + 1)
                            last = pe.transpose(psum[:, 2 * half + f, i * P:(i + 1) * P],
                                                xn[:, t, f * P:(f + 1) * P], ident[:])
                        last.then_inc(turned, 1)


DE = 1024
NE = DE // P
TERNARY_EPS = 1e-8


def ternary_weights(nc, core, scope, wup_d, wgate_d, wdown_d):
    scale = core.sb("ternary_scales", [P, 3], F32, scope)
    ups = core.sb("w_up_signs", [P, KT, DE], F32, scope)
    gates = core.sb("w_gate_signs", [P, KT, DE], F32, scope)
    downs = core.sb("w_down_signs", [P, NE, D], F32, scope)
    flat = [ups[:].rearrange("p k n -> p (k n)"), gates[:].rearrange("p k n -> p (k n)"),
            downs[:].rearrange("p k n -> p (k n)")]
    N = KT * DE
    loaded = [core.sem(f"ternary_w{i}_loaded") for i in range(3)]
    absum, total, scaled, halves, low = (core.sem("ternary_" + n) for n in
                                         ("abs_summed", "total", "scaled", "halved", "low_side"))
    done = core.sem("ternary_signs")
    with ExitStack() as tmp:
        w = [core.sb(f"w{i}", [P, N], F32, tmp) for i in range(3)]
        b = core.sb("low_side", [P, N], F32, tmp)
        part = core.sb("abs_sums", [P, 3], F32, tmp)
        h = core.sb("half_scales", [P, 2, 3], F32, tmp)
        with nc.Block() as block:
            @block.sync
            def _(sp):
                sp.dma_start(w[0][:].rearrange("p (k n) -> p k n", k=KT),
                             wup_d.rearrange("(k p) n -> p k n", p=P)).then_inc(loaded[0], 16)
                sp.dma_start(w[1][:].rearrange("p (k n) -> p k n", k=KT),
                             wgate_d.rearrange("(k p) n -> p k n", p=P)).then_inc(loaded[1], 16)
                sp.dma_start(w[2][:].rearrange("p (k n) -> p k n", k=NE),
                             wdown_d.rearrange("(k p) n -> p k n", p=P)).then_inc(loaded[2], 16)

            @block.tensor
            def _(pe):
                pe.wait_ge(absum, 3)
                pe.matmul(core.psum[:, 0, 0:3], core.ones_sq[:], part[:], start=True, stop=True).then_inc(total, 1)

            @block.vector
            def _(dve):
                for i in range(3):
                    dve.wait_ge(loaded[i], 16)
                    dve.tensor_reduce(part[:, i:i + 1], w[i][:], AX.X, ALU.add,
                                      apply_absolute_value=True).then_inc(absum, 1)
                dve.wait_ge(total, 1)
                dve.tensor_scalar(scale[:], core.psum[:, 0, 0:3], 1.0 / (DE * D), TERNARY_EPS,
                                  ALU.mult, ALU.add).then_inc(scaled, 1)
                dve.wait_ge(scaled, 1)
                dve.tensor_scalar(h[:, 0, :], scale[:], 0.5, None, ALU.mult).then_inc(halves, 1)
                dve.tensor_scalar(h[:, 1, :], scale[:], -0.5, None, ALU.mult).then_inc(halves, 1)
                dve.wait_ge(halves, 2)
                for i in range(3):
                    if i:
                        dve.wait_ge(done, i)
                    dve.tensor_scalar(b[:], w[i][:], h[:, 1, i:i + 1], None, ALU.is_lt).then_inc(low, 1)
                    dve.wait_ge(low, i + 1)
                    dve.scalar_tensor_tensor(flat[i], w[i][:], h[:, 0, i:i + 1], b[:], ALU.is_gt,
                                             ALU.subtract).then_inc(done, 1)
    return scale, ups, gates, downs


def ternary_ffn(nc, core, tag, weights):
    scale, ups, gates, downs = weights
    X, XNT, psum = core.X, core.XNT, core.psum
    proj, act_done, hid = (core.sem(tag + n) for n in ("_projected", "_silu", "_hidden"))
    down, added = core.sem(tag + "_down"), core.sem(tag + "_added")
    with ExitStack() as tmp:
        H = core.sb("hidden", [P, NE, S], F32, tmp)
        sil = core.sb("silu_up", [P, 2, HALF], F32, tmp)
        units = [(e, half) for half in range(NH2) for e in range(NE)]
        with nc.Block() as block:
            @block.tensor
            def _(pe):
                for u, (e, half) in enumerate(units):
                    b = u % 2
                    if u >= 2:
                        pe.wait_ge(hid, u - 1)
                    for j, w in enumerate((ups, gates)):
                        for k in range(KT):
                            last = pe.matmul(psum[:, 2 * b + j, :], w[:, k, e * P:(e + 1) * P],
                                             XNT[:, k, half * HALF:(half + 1) * HALF],
                                             start=(k == 0), stop=(k == KT - 1))
                        last.then_inc(proj, 1)
                for t in range(NT):
                    pe.wait_ge(hid, NE * (t // 4 + 1))
                    if t >= 4:
                        pe.wait_ge(added, t - 3)
                    for e in range(NE):
                        last = pe.matmul(psum[:, 4 + t % 4, 0:D], H[:, e, t * P:(t + 1) * P], downs[:, e, :],
                                         start=(e == 0), stop=(e == NE - 1))
                    last.then_inc(down, 1)

            @block.scalar
            def _(act):
                for u, (e, half) in enumerate(units):
                    act.wait_ge(proj, 2 * u + 1)
                    if u >= 2:
                        act.wait_ge(hid, u - 1)
                    act.activation(sil[:, u % 2, :], psum[:, 2 * (u % 2), :], ACT.Silu,
                                   scale=scale[:, 0:1]).then_inc(act_done, 1)

            @block.vector
            def _(dve):
                for u, (e, half) in enumerate(units):
                    dve.wait_ge(proj, 2 * u + 2)
                    dve.wait_ge(act_done, u + 1)
                    dve.scalar_tensor_tensor(H[:, e, half * HALF:(half + 1) * HALF], psum[:, 2 * (u % 2) + 1, :],
                                             scale[:, 1:2], sil[:, u % 2, :], ALU.mult, ALU.mult).then_inc(hid, 1)
                for t in range(NT):
                    dve.wait_ge(down, t + 1)
                    dve.scalar_tensor_tensor(X[:, t, :], psum[:, 4 + t % 4, 0:D], scale[:, 2:3], X[:, t, :],
                                             ALU.mult, ALU.add).then_inc(added, 1)


VW = 32
AHEAD = 2


def attention_heads(nc, core, tag, causal, V, O, q_max, k_max, keys, queries, shift_row, exp_kw,
                    shift_dt, masks=None, head_loads=None, before=None):
    psum, ident = core.psum, core.ident
    sem = lambda n: core.sem(f"{tag}_{n}")
    PB = 4
    SB, MB, PVB, TB = 0, 4, 6, 7
    end = lambda qt: (qt + 1) * P if causal else S
    pieces = lambda qt: [(a, min(a + HALF, end(qt))) for a in range(0, end(qt), HALF)]
    count = [len(pieces(qt)) for qt in range(NT)]
    per_head = sum(count)
    start = [sum(count[:qt]) for qt in range(NT)]
    q_from = lambda c: c * P if causal else 0
    with ExitStack() as tmp:
        sb = lambda n, shape, dt=F32: core.sb(n, shape, dt, tmp)
        mx = sb("row_max_pieces", [P, 2, NT, NH2])
        nm = sb("minus_max", [P, 2, NT])
        nmT = sb("minus_max_rows", [NT, 2, P], shift_dt)
        pr = sb("probs", [P, PB, S])
        oT = sb("out_features", [P, 2, D])
        rc = sb("reciprocals", [P, 2, 2, 4])
        m_ready, m_piece, m_done = sem("max_scores"), sem("max_pieces"), sem("minus_max")
        mt_ready, mt_done, shift_in = sem("max_transposed"), sem("max_row"), sem("shift_row")
        s_ready, e_done, pv_ready = sem("scores"), sem("exp"), sem("values_summed")
        o_kept, o_turned, r_done, o_done = sem("out_kept"), sem("out_transposed"), sem("recip"), sem("out_done")
        with nc.Block() as block:
            @block.tensor
            def _(pe):
                def max_scores(h, qt):
                    if qt == 0 and head_loads:
                        head_loads.wait_max(pe, h)
                    for i, (a, b) in enumerate(pieces(qt)):
                        n = h * per_head + start[qt] + i
                        if n >= 2:
                            pe.wait_ge(m_piece, n - 1)
                        own = causal and i == count[qt] - 1
                        last = pe.matmul(psum[:, MB + n % 2, 0:b - a], q_max(h, qt * P, (qt + 1) * P), k_max(h, a, b),
                                         start=True, stop=not own)
                        if own:
                            last = pe.matmul(psum[:, MB + n % 2, b - a - P:b - a], masks[0], masks[1],
                                             start=False, stop=True)
                        last.then_inc(m_ready, 1)

                def turn_max(h):
                    pe.wait_ge(m_done, h + 1)
                    if h >= 1:
                        pe.wait_ge(mt_done, h)
                    if h >= 3:
                        pe.wait_ge(o_done, h - 2)
                    pe.transpose(psum[0:NT, TB, 2 * P:3 * P], nm[:, h % 2, :], ident[:]).then_inc(mt_ready, 1)

                def key_scores(h, c):
                    n = h * NT + c
                    if c == 0:
                        pe.wait_ge(shift_in, 16 * (h + 1))
                        if head_loads:
                            head_loads.wait_keys(pe, h)
                    if n >= 2:
                        pe.wait_ge(e_done, n - 1)
                    for half in range(q_from(c) // HALF, NH2):
                        a = max(q_from(c), half * HALF)
                        o = psum[:, SB + 2 * (n % 2) + half, a - half * HALF:]
                        own = causal and a == q_from(c)
                        last = pe.matmul(o, keys(h, c), queries(h, a, (half + 1) * HALF), start=True, stop=not own)
                        if own:
                            last = pe.matmul(o[:, 0:P], masks[0], masks[2], start=False, stop=True)
                    last.then_inc(s_ready, 1)

                def values(n):
                    h, c = n // NT, n % NT
                    pe.wait_ge(e_done, n + 1)
                    if c == 0 and h >= 1:
                        pe.wait_ge(o_kept, h)
                    for g in range(q_from(c) // D, 4):
                        a = max(q_from(c), g * D)
                        last = pe.matmul(psum[32 * g:32 * g + VW, PVB, a - g * D:D], V[:, c, h, :],
                                         pr[:, n % PB, a:(g + 1) * D], start=(c == 0),
                                         stop=(c == (2 * g + 1 if causal else NT - 1)))
                    last.then_inc(pv_ready, 1)

                def turn_out(h):
                    pe.wait_ge(o_kept, h + 1)
                    if h >= 1:
                        pe.wait_ge(o_done, h)
                    pe.wait_ge(mt_done, min(h + 3, HEADS))
                    for b in range(2):
                        last = pe.transpose(psum[:, TB, b * P:(b + 1) * P], oT[:, h % 2, b * P:(b + 1) * P], ident[:])
                    last.then_inc(o_turned, 1)

                if before:
                    before.tensor(pe)
                for h in range(AHEAD):
                    for qt in range(NT):
                        max_scores(h, qt)
                        if h == 1 and qt == 2:
                            turn_max(0)
                for h in range(HEADS):
                    for c in range(NT):
                        n = h * NT + c
                        key_scores(h, c)
                        if h + AHEAD < HEADS:
                            max_scores(h + AHEAD, c)
                        if c == 2 and h + 1 < HEADS:
                            turn_max(h + 1)
                        if c == 4 and h >= 1:
                            turn_out(h - 1)
                        if n >= 1:
                            values(n - 1)
                values(HEADS * NT - 1)
                turn_out(HEADS - 1)

            @block.vector
            def _(dve):
                def row_max(h, qt):
                    for i, (a, b) in enumerate(pieces(qt)):
                        n = h * per_head + start[qt] + i
                        dve.wait_ge(m_ready, n + 1)
                        dve.reduce_max(mx[:, h % 2, qt, i:i + 1], psum[:, MB + n % 2, 0:b - a], AX.X
                                       ).then_inc(m_piece, 1)

                def minus_max(h):
                    dve.wait_ge(m_piece, (h + 1) * per_head)
                    if h >= 2:
                        dve.wait_ge(mt_ready, h - 1)
                    dve.tensor_reduce(nm[:, h % 2, :], mx[:, h % 2, :, :], AX.X, ALU.max, negate=True).then_inc(m_done, 1)

                def max_row(h):
                    dve.wait_ge(mt_ready, h + 1)
                    if h >= 2:
                        dve.wait_ge(shift_in, 16 * (h - 1))
                    dve.tensor_copy(nmT[:, h % 2, :], psum[0:NT, TB, 2 * P:3 * P]).then_inc(mt_done, 1)

                def finish(h):
                    dve.wait_ge(o_turned, h + 1)
                    t4 = psum[:, TB, 0:D].rearrange("p (b g d) -> p b g d", b=2, g=4)
                    dve.reciprocal(rc[:, h % 2, :, :], t4[:, :, :, HD]).then_inc(r_done, 1)
                    dve.wait_ge(r_done, h + 1)
                    for b in range(2):
                        last = dve.tensor_tensor(
                            O[:].rearrange("p (g b) n -> p b g n", b=2)[:, b, :, h * HD:(h + 1) * HD],
                            t4[:, b, :, 0:HD], rc[:, h % 2, b, :].unsqueeze(2).broadcast_to([P, 4, HD]), ALU.mult)
                    last.then_inc(o_done, 1)

                if causal:
                    for b in range(2):
                        dve.memset(mx[:, b, 0:NT // 2, 1:2], -3e38)
                if before:
                    before.vector(dve)
                for h in range(AHEAD):
                    for qt in range(NT):
                        row_max(h, qt)
                        if h == 1 and qt == 2:
                            max_row(0)
                    minus_max(h)
                for h in range(HEADS):
                    for c in range(NT):
                        if h + AHEAD < HEADS:
                            row_max(h + AHEAD, c)
                        if c == 2 and h + 1 < HEADS:
                            max_row(h + 1)
                        if c == 4 and h >= 1:
                            finish(h - 1)
                    if h + AHEAD < HEADS:
                        minus_max(h + AHEAD)
                finish(HEADS - 1)

            @block.sync
            def _(sp):
                if head_loads:
                    head_loads.first(sp)
                for h in range(HEADS):
                    sp.wait_ge(mt_done, h + 1)
                    sp.dma_start(shift_row(h).rearrange("a (t p) -> a t p", t=NT), nmT[:, h % 2, :]).then_inc(shift_in, 16)
                    if head_loads:
                        head_loads.load(sp, h, m_ready, per_head, s_ready)

            @block.scalar
            def _(act):
                def keep_out(h):
                    act.wait_ge(pv_ready, (h + 1) * NT)
                    if h >= 2:
                        act.wait_ge(o_turned, h - 1)
                    act.activation(oT[:, h % 2, :], psum[:, PVB, 0:D], ACT.Copy).then_inc(o_kept, 1)

                if before:
                    before.scalar(act)
                for h in range(HEADS):
                    for c in range(NT):
                        n = h * NT + c
                        act.wait_ge(s_ready, n + 1)
                        if n >= PB:
                            act.wait_ge(pv_ready, n - PB + 1)
                        act.activation(pr[:, n % PB, q_from(c):],
                                       psum[:, SB + 2 * (n % 2):SB + 2 * (n % 2) + 2, :].rearrange("p a n -> p (a n)")[:, q_from(c):],
                                       ACT.Exp, **exp_kw(c)).then_inc(e_done, 1)
                        if c == 0 and h >= 1:
                            keep_out(h - 1)
                keep_out(HEADS - 1)


PARTS = 6
K_PARTS = (0, 1, 2, 0, 1, 0)
Q_PARTS = (0, 0, 0, 1, 1, 2)
SHIFT_ROW = PARTS * HD
KROWS = SHIFT_ROW + 1


def attention16(nc, core, tag, wq_d, wk_d, wv_d, wo_d, biases, gates, pos_d):
    X, XNT, psum, ident = core.X, core.XNT, core.psum, core.ident
    sem = lambda n: core.sem(f"{tag}_{n}")
    scratch = nc.dram_tensor(f"{tag}_parts", (4, 3, P, S), BF16, kind="Internal").ap()
    with ExitStack() as tmp:
        sb = lambda n, shape, dt=F32: core.sb(n, shape, dt, tmp)
        KS = sb("k_stack", [P, HEADS, S], BF16)
        QS = sb("q_stack", [P, HEADS, S], BF16)
        V = sb("v_ones", [P, NT, HEADS, VW])
        O = sb("attended", [P, NT, D])
        wo = sb("wo", [P, KT, D])
        bo = sb("bo", [1, D])
        esc = sb("exp_scale", [P, 1])
        ebias = sb("exp_bias", [P, NT])
        with ExitStack() as tmp2:
            sb2 = lambda n, shape, dt=F32: core.sb(n, shape, dt, tmp2)
            wq, wk, wv = sb2("wq", [P, KT, D]), sb2("wk", [P, KT, D]), sb2("wv", [P, KT, D])
            bqk = sb2("bias_qk", [P, 2, KT])
            bv = sb2("bias_v", [1, D])
            g3 = sb2("gates", [P, 2])
            pos = sb2("positions", [P, NT])
            full = sb2("qk_full", [P, 2, S])
            parts = sb2("qk_parts", [P, 4, 3, S], BF16)
            rest = sb2("qk_rest", [P, 2, S])
            loaded, made = sem("loaded"), sem("ones_made")
            qk_ready, full_done = sem("qk_projected"), sem("qk_full")
            hi, r1, mid, lo = (sem(n) for n in ("high", "rest", "middle", "low"))
            stacked = [sem("stacked_first_half"), sem("stacked_second_half")]
            written = [sem(f"parts_written_{u}") for u in range(4)]
            ORDER = (0, 2, 1, 3)
            v_ready, v_done, zeroed = sem("v_projected"), sem("v_kept"), sem("v_zeroed")
            esc_done = sem("exp_scale")
            nb = 0 if biases is None else 3
            with nc.Block() as block:
                @block.sync
                def _(sp):
                    n = 0
                    for w, w_d in ((wq, wq_d), (wk, wk_d), (wv, wv_d), (wo, wo_d)):
                        sp.dma_start(w[:], w_d.rearrange("(k p) n -> p k n", p=P)).then_inc(loaded, 16)
                    sp.dma_start(bo[:], biases["bo"].rearrange("(a n) -> a n", a=1)).then_inc(loaded, 16)
                    if gates is not None:
                        sp.dma_start(bqk[:].rearrange("p w k -> p (w k)"), biases["bqk"]).then_inc(loaded, 16)
                        sp.dma_start(bv[:], biases["bv"].rearrange("(a n) -> a n", a=1)).then_inc(loaded, 16)
                        sp.dma_start(g3[:, 0:1], gates["justice"].rearrange("(a n) -> a n", a=1).broadcast_to([P, 1])).then_inc(loaded, 16)
                        sp.dma_start(g3[:, 1:2], gates["order"].rearrange("(a n) -> a n", a=1).broadcast_to([P, 1])).then_inc(loaded, 16)
                        sp.dma_start(pos[:], pos_d).then_inc(loaded, 16)
                    for n, u in enumerate(ORDER):
                        which, f = u // 2, u % 2
                        for part, ready in enumerate((hi, mid, lo)):
                            sp.wait_ge(ready, n + 1)
                            sp.dma_start(scratch[u, part], parts[:, u, part, :]).then_inc(written[u], 16)
                        if n % 2:
                            for uu in ORDER[n - 1:n + 1]:
                                sp.wait_ge(written[uu], 16 * 3)
                                w_, f_ = uu // 2, uu % 2
                                for j, part in enumerate((Q_PARTS, K_PARTS)[w_]):
                                    sp.dma_start((QS, KS)[w_][j * HD:(j + 1) * HD, 8 * f_:8 * f_ + 8, :],
                                                 scratch[uu, part].rearrange("(h d) t -> d h t", d=HD)
                                                 ).then_inc(stacked[f_], 16)

                nload = 5 + (5 if gates is not None else 0)

                @block.tensor
                def _(pe):
                    pe.wait_ge(loaded, 16 * nload)
                    for n, u in enumerate(ORDER):
                        which, f = u // 2, u % 2
                        w = (wq, wk)[which]
                        for half in range(NH2):
                            if n >= 2:
                                pe.wait_ge(full_done, 2 * (n - 2) + half + 1)
                            for k in range(KT):
                                last = pe.matmul(psum[:, 2 * (n % 2) + half, :], w[:, k, f * P:(f + 1) * P],
                                                 XNT[:, k, half * HALF:(half + 1) * HALF],
                                                 start=(k == 0), stop=(k == KT - 1))
                            last.then_inc(qk_ready, 1)
                    for t in range(NT):
                        if t >= 2:
                            pe.wait_ge(v_done, t - 1)
                        for k in range(KT):
                            last = pe.matmul(psum[:, 4 + t % 2, 0:D], XNT[:, k, t * P:(t + 1) * P], wv[:, k, :],
                                             start=(k == 0), stop=(k == KT - 1 and gates is None))
                        if gates is not None:
                            last = pe.matmul(psum[:, 4 + t % 2, 0:D], core.ones[:], bv[:], start=False, stop=True)
                        last.then_inc(v_ready, 1)

                @block.scalar
                def _(act):
                    if gates is not None:
                        act.wait_ge(loaded, 16 * nload)
                        act.activation(g3[:], g3[:], ACT.Sigmoid).then_inc(esc_done, 1)
                    for n, u in enumerate(ORDER):
                        which, f = u // 2, u % 2
                        for half in range(NH2):
                            act.wait_ge(qk_ready, 2 * n + half + 1)
                            if n >= 2:
                                act.wait_ge(r1, n - 1)
                                act.wait_ge(hi, n - 1)
                            act.activation(full[:, n % 2, half * HALF:(half + 1) * HALF],
                                           psum[:, 2 * (n % 2) + half, :], ACT.Identity,
                                           bias=bqk[:, which, f:f + 1] if gates is not None else 0.0
                                           ).then_inc(full_done, 1)
                        act.wait_ge(full_done, 2 * n + 2)
                        act.activation(parts[:, u, 0, :], full[:, n % 2, :], ACT.Copy).then_inc(hi, 1)
                        act.wait_ge(r1, n + 1)
                        act.activation(parts[:, u, 1, :], rest[:, n % 2, :], ACT.Copy).then_inc(mid, 1)

                @block.vector
                def _(dve):
                    if gates is not None:
                        dve.wait_ge(esc_done, 1)
                        dve.tensor_scalar(esc[:], g3[:, 0:1], -0.1 / HD ** 0.5, 1.0 / HD ** 0.5,
                                          ALU.mult, ALU.add).then_inc(esc_done, 1)
                        dve.tensor_scalar(ebias[:], pos[:], g3[:, 1:2], 0.05, ALU.mult, ALU.mult).then_inc(esc_done, 1)
                    else:
                        dve.memset(esc[:], 1.0 / HD ** 0.5).then_inc(esc_done, 1)
                        dve.memset(ebias[:], 0.0).then_inc(esc_done, 1)
                    for n, u in enumerate(ORDER):
                        dve.wait_ge(hi, n + 1)
                        if n >= 2:
                            dve.wait_ge(lo, n - 1)
                            dve.wait_ge(mid, n - 1)
                        dve.tensor_tensor(rest[:, n % 2, :], full[:, n % 2, :], parts[:, u, 0, :],
                                          ALU.subtract).then_inc(r1, 1)
                        dve.wait_ge(mid, n + 1)
                        dve.tensor_tensor(parts[:, u, 2, :], rest[:, n % 2, :], parts[:, u, 1, :],
                                          ALU.subtract).then_inc(lo, 1)
                    dve.wait_ge(zeroed, 3)
                    for t in range(NT):
                        dve.wait_ge(v_ready, t + 1)
                        dve.tensor_copy(V[:, t, :, 0:HD],
                                        psum[:, 4 + t % 2, 0:D].rearrange("p (h d) -> p h d", d=HD)).then_inc(v_done, 1)

                @block.gpsimd
                def _(pool):
                    pool.memset(V[:], 0.0).then_inc(zeroed, 1)
                    pool.wait_ge(zeroed, 1)
                    pool.memset(V[:, :, :, HD:HD + 1], 1.0).then_inc(zeroed, 1)
                    pool.wait_ge(zeroed, 2)
                    pool.memset(KS[SHIFT_ROW:KROWS, :, :], 1.0).then_inc(zeroed, 1)

        class V_first:

            def tensor(pe):
                pe.wait_ge(stacked[0], 16 * 2 * PARTS)

            vector = scalar = staticmethod(lambda eng: None)

        class Stacks:
            wait_keys = first = load = staticmethod(lambda *x: None)

            @staticmethod
            def wait_max(pe, h):
                if h == HEADS // 2:
                    pe.wait_ge(stacked[1], 16 * 2 * PARTS)

        attention_heads(nc, core, tag, False, V, O,
                        q_max=lambda h, a, b: QS[0:SHIFT_ROW, h, a:b], k_max=lambda h, a, b: KS[0:SHIFT_ROW, h, a:b],
                        keys=lambda h, c: KS[0:KROWS, h, c * P:(c + 1) * P],
                        queries=lambda h, a, b: QS[0:KROWS, h, a:b], shift_row=lambda h: QS[SHIFT_ROW:KROWS, h, :],
                        exp_kw=lambda c: {"bias": ebias[:, c:c + 1], "scale": esc[:]}, shift_dt=BF16,
                        head_loads=Stacks, before=V_first)
        project_out(nc, core, tag, O, wo, bo)


def project_out(nc, core, tag, O, wo, bo, tiles=KT):
    X, psum, ident = core.X, core.psum, core.ident
    turned, kept, ready, added = (core.sem(f"{tag}_{n}") for n in ("o_turned", "o_features", "proj", "added"))
    with ExitStack() as tmp:
        OT = core.sb("attended_features", [P, tiles, S], F32, tmp)
        with nc.Block() as block:
            @block.tensor
            def _(pe):
                for n in range(NH2 * tiles):
                    half, f = n // tiles, n % tiles
                    if n >= 4:
                        pe.wait_ge(kept, n - 3)
                    for i in range(4):
                        t = 4 * half + i
                        last = pe.transpose(psum[:, n % 4, i * P:(i + 1) * P], O[:, t, f * P:(f + 1) * P], ident[:])
                    last.then_inc(turned, 1)
                for t in range(NT):
                    pe.wait_ge(kept, tiles * (t // 4 + 1))
                    if t >= 4:
                        pe.wait_ge(added, t - 3)
                    for k in range(tiles):
                        last = pe.matmul(psum[:, 4 + t % 4, 0:D], OT[:, k, t * P:(t + 1) * P], wo[:, k, :],
                                         start=(k == 0), stop=(k == tiles - 1 and bo is None))
                    if bo is not None:
                        last = pe.matmul(psum[:, 4 + t % 4, 0:D], core.ones[:], bo[:], start=False, stop=True)
                    last.then_inc(ready, 1)

            @block.scalar
            def _(act):
                for n in range(NH2 * tiles):
                    half, f = n // tiles, n % tiles
                    act.wait_ge(turned, n + 1)
                    act.activation(OT[:, f, half * HALF:(half + 1) * HALF], psum[:, n % 4, :],
                                   ACT.Copy).then_inc(kept, 1)

            @block.vector
            def _(dve):
                for t in range(NT):
                    dve.wait_ge(ready, t + 1)
                    dve.tensor_tensor(X[:, t, :], psum[:, 4 + t % 4, 0:D], X[:, t, :], ALU.add).then_inc(added, 1)



GH, GK, GV = 6, 32, 64
QKW, VWD = GH * GK, GH * GV
FW = 2 * QKW + VWD
NF = FW // P
TAPS = 4
LEVELS = 7
RMS_EPS = 1e-5


def gated_delta(nc, core, tag, d):
    X, XNT, psum, ident = core.X, core.XNT, core.psum, core.ident
    sem = lambda n: core.sem(f"{tag}_{n}")
    with ExitStack() as tmp:
        sb = lambda n, shape, dt=F32: core.sb(n, shape, dt, tmp)
        SG = sb("silu_gate", [P, NT, VWD])
        KBE = sb("k_beta_eg", [P, NT, GH, GK])
        KD = sb("k_decayed", [P, NT, GH, GK])
        BV = sb("beta_v", [P, NT, GH, GV])
        ETH = sb("exp_total_by_row", [P, 2, NT])
        G = sb("g_sums", [P, NT, GH])
        g = sb("g", [P, NT, GH])
        wo = sb("delta_wo", [P, 3, D])
        nw = sb("norm_weight", [P, GV])
        tri = sb("upper_ones", [P, P])
        QET = sb("qe_features", [P, 2, S])
        wload = sem("wo_loaded")
        with ExitStack() as mid_scope:
            sbm = lambda n, shape, dt=F32: core.sb(n, shape, dt, mid_scope)
            PT = sbm("p_by_key", [P, GH * NT, P])
            EA = sbm("e_then_minus_a", [P, GH * NT, P])
            norm_scope = ExitStack()
            sbn = lambda n, shape, dt=F32: core.sb(n, shape, dt, norm_scope)
            KN, KB = sbn("k_normed", [P, NT, GH, GK]), sbn("k_beta", [P, NT, GH, GK])
            QN, QE = sbn("q_normed", [P, NT, GH, GK]), sbn("q_eg", [P, NT, GH, GK])
            with ExitStack() as tmp2:
                sb2 = lambda n, shape, dt=F32: core.sb(n, shape, dt, tmp2)
                YT = sb2("conv_tokens", [P, NT, FW])
                AB = sb2("ab", [P, NT, 2 * GH])
                with ExitStack() as tmp3:
                    sb3 = lambda n, shape, dt=F32: core.sb(n, shape, dt, tmp3)
                    wqkv, wgab = sb3("wqkv", [P, KT, FW]), sb3("wgab", [P, KT, VWD + 2 * GH])
                    cw = sb3("conv_w", [P, NF, TAPS])
                    Y = PT[:].rearrange("p (f a) n -> p f (a n)", f=NF)
                    loaded, proj, tapped, conv = sem("w_loaded"), sem("proj"), sem("tap"), sem("conv")
                    silu, turned, kept = sem("silu"), sem("turned"), sem("kept")
                    gate_in, gate_out, ab_out = sem("gate_in"), sem("gate_out"), sem("ab_out")
                    tri_made = sem("tri")
                    with nc.Block() as block:
                        @block.sync
                        def _(sp):
                            for k in range(KT):
                                sp.dma_start(wqkv[:, k, :], d["wqkv"][k * P:(k + 1) * P, :]).then_inc(loaded, 16)
                                sp.dma_start(wgab[:, k, :], d["wgab"][k * P:(k + 1) * P, :]).then_inc(loaded, 16)
                            sp.dma_start(cw[:].rearrange("p f t -> p (f t)"), d["conv"]).then_inc(loaded, 16)
                            sp.dma_start(wo[:], d["wo"].rearrange("(k p) n -> p k n", p=P)).then_inc(wload, 16)
                            sp.dma_start(nw[:], d["nw"].rearrange("(a n) -> a n", a=1).broadcast_to([P, GV])
                                         ).then_inc(wload, 16)
                            sp.wait_ge(wload, 32)

                        @block.gpsimd
                        def _(pool):
                            pool.affine_select(out=tri[:], in_=core.ones_sq[:], compare_op=ALU.is_ge, fill=0.0,
                                               base=0, pattern=[[1, P]], channel_multiplier=-1).then_inc(tri_made, 1)

                        @block.tensor
                        def _(pe):
                            pe.wait_ge(loaded, 16 * 5)

                            def project(f):
                                if f >= 2:
                                    pe.wait_ge(conv, TAPS - 1 + (TAPS - 1) * (f - 2))
                                for half in range(NH2):
                                    for k in range(KT):
                                        last = pe.matmul(psum[:, 2 * (f % 2) + half, :],
                                                         wqkv[:, k, f * P:(f + 1) * P],
                                                         XNT[:, k, half * HALF:(half + 1) * HALF],
                                                         start=(k == 0), stop=(k == KT - 1))
                                last.then_inc(proj, 1)

                            def turn(f):
                                pe.wait_ge(silu, f + 1)
                                for half in range(NH2):
                                    n = 2 * f + half
                                    if n >= 2:
                                        pe.wait_ge(kept, n - 1)
                                    for i in range(4):
                                        t = 4 * half + i
                                        last = pe.transpose(psum[:, 4 + n % 2, i * P:(i + 1) * P],
                                                            Y[:, f, t * P:(t + 1) * P], ident[:])
                                    last.then_inc(turned, 1)

                            def gates(t):
                                if t >= 2:
                                    pe.wait_ge(gate_out, t - 1)
                                    pe.wait_ge(ab_out, t - 1)
                                for k in range(KT):
                                    last = pe.matmul(psum[:, 6 + t % 2, 0:VWD + 2 * GH], XNT[:, k, t * P:(t + 1) * P],
                                                     wgab[:, k, :], start=(k == 0), stop=(k == KT - 1))
                                last.then_inc(gate_in, 1)

                            for f in range(NF + 1):
                                if f < NF:
                                    project(f)
                                if f >= 1:
                                    turn(f - 1)
                            for t in range(NT):
                                gates(t)

                        @block.scalar
                        def _(act):
                            act.wait_ge(loaded, 16 * 5)
                            for f in range(NF + 1):
                                if f < NF:
                                    act.wait_ge(proj, f + 1)
                                    act.activation(Y[:, f, :], psum[:, 2 * (f % 2):2 * (f % 2) + 2, :
                                                                    ].rearrange("p a n -> p (a n)"),
                                                   ACT.Copy, scale=cw[:, f, TAPS - 1:TAPS]).then_inc(tapped, 1)
                                if f >= 1:
                                    act.wait_ge(conv, (TAPS - 1) * f)
                                    act.activation(Y[:, f - 1, :], Y[:, f - 1, :], ACT.Silu).then_inc(silu, 1)
                                    for half in range(NH2):
                                        n = 2 * (f - 1) + half
                                        act.wait_ge(turned, n + 1)
                                        act.activation(YT[:, 4 * half:4 * half + 4, (f - 1) * P:f * P],
                                                       psum[:, 4 + n % 2, :].rearrange("p (t n) -> p t n", t=4),
                                                       ACT.Copy).then_inc(kept, 1)
                            for t in range(NT):
                                act.wait_ge(gate_in, t + 1)
                                act.activation(SG[:, t, :], psum[:, 6 + t % 2, 0:VWD], ACT.Silu).then_inc(gate_out, 1)

                        @block.vector
                        def _(dve):
                            for f in range(NF):
                                dve.wait_ge(tapped, f + 1)
                                src = psum[:, 2 * (f % 2):2 * (f % 2) + 2, :].rearrange("p a n -> p (a n)")
                                for i in range(1, TAPS):
                                    if i > 1:
                                        dve.wait_ge(conv, (TAPS - 1) * f + i - 1)
                                    dve.scalar_tensor_tensor(Y[:, f, i:], src[:, 0:S - i],
                                                             cw[:, f, TAPS - 1 - i:TAPS - i], Y[:, f, i:],
                                                             ALU.mult, ALU.add).then_inc(conv, 1)
                            for t in range(NT):
                                dve.wait_ge(gate_in, t + 1)
                                dve.wait_ge(gate_out, t + 1)
                                dve.tensor_copy(AB[:, t, :], psum[:, 6 + t % 2, VWD:VWD + 2 * GH]).then_inc(ab_out, 1)

                with ExitStack() as tmp3:
                    sb3 = lambda n, shape, dt=F32: core.sb(n, shape, dt, tmp3)
                    dtb, alog = sb3("dt_bias", [P, GH]), sb3("a_log", [P, GH])
                    x, ax, e, u, lnu, du, one = (sb3(n, [P, NT, GH]) for n in
                                                 ("a_in", "a_abs", "e_neg", "e_plus_1", "ln", "u_minus_1", "is_one"))
                    eb, beta = sb3("exp_minus_b", [P, NT, GH]), sb3("beta", [P, NT, GH])
                    ea = sb3("exp_a_log", [P, GH])
                    eG, eT, eD, dd = (sb3(n, [P, NT, GH]) for n in ("exp_G", "exp_total", "exp_rest", "rest"))
                    sq = sb3("squares", [P, NT, 2 * QKW])
                    ss, r = sb3("square_sums", [P, NT, 2 * GH]), sb3("inverse_norms", [P, NT, 2 * GH])
                    fk = sb3("factors", [P, 5, NT, GH])
                    loaded, ch, aux, from_act, from_pe = sem("ab_loaded"), sem("chain"), sem("to_act"), sem("from_act"), sem("from_pe")
                    to_pe, sq_done, fact, scaled = sem("to_pe"), sem("sq_done"), sem("factors"), sem("scaled")
                    with nc.Block() as block:
                        @block.sync
                        def _(sp):
                            sp.dma_start(dtb[:], d["dt"].rearrange("(a n) -> a n", a=1).broadcast_to([P, GH])).then_inc(loaded, 16)
                            sp.dma_start(alog[:], d["alog"].rearrange("(a n) -> a n", a=1).broadcast_to([P, GH])).then_inc(loaded, 16)

                        @block.tensor
                        def _(pe):
                            pe.wait_ge(to_pe, 1)
                            gf = g[:].rearrange("p t h -> p (t h)")
                            pe.matmul(psum[:, 0, 0:NT * GH], tri[:], gf, start=True, stop=True).then_inc(from_pe, 1)
                            pe.matmul(psum[:, 1, 0:NT * GH], core.ones_sq[:], gf, start=True, stop=True).then_inc(from_pe, 1)

                        @block.scalar
                        def _(act):
                            act.wait_ge(loaded, 32)
                            act.activation(ea[:], alog[:], ACT.Exp).then_inc(from_act, 1)
                            act.activation(eb[:], AB[:, :, GH:], ACT.Exp, scale=-1.0).then_inc(from_act, 1)
                            act.wait_ge(aux, 1)
                            act.activation(e[:], ax[:], ACT.Exp, scale=-1.0).then_inc(from_act, 1)
                            act.wait_ge(aux, 2)
                            act.activation(lnu[:], u[:], ACT.Ln).then_inc(from_act, 1)
                            act.wait_ge(aux, 3)
                            act.activation(eG[:], G[:], ACT.Exp).then_inc(from_act, 1)
                            act.activation(eT[:], psum[:, 1, 0:NT * GH].rearrange("p (t h) -> p t h", h=GH),
                                           ACT.Exp).then_inc(from_act, 1)
                            act.activation(eD[:], dd[:], ACT.Exp).then_inc(from_act, 1)
                            act.wait_ge(sq_done, 1)
                            act.activation(ss[:], ss[:], ACT.Sqrt).then_inc(from_act, 1)

                        @block.vector
                        def _(dve):
                            n = [0]

                            def link(i):
                                n[0] += 1
                                i.then_inc(ch, 1)
                                dve.wait_ge(ch, n[0])

                            dve.wait_ge(loaded, 32)
                            link(dve.tensor_tensor(x[:], AB[:, :, 0:GH], dtb[:].unsqueeze(1).broadcast_to([P, NT, GH]), ALU.add))
                            dve.scalar_tensor_tensor(ax[:], x[:], -1.0, x[:], ALU.mult, ALU.max).then_inc(aux, 1)
                            qk = YT[:, :, 0:2 * QKW]
                            link(dve.tensor_tensor(sq[:], qk, qk, ALU.mult))
                            dve.reduce_sum(ss[:].rearrange("p t h -> p (t h)"),
                                           sq[:].rearrange("p t (h c) -> p (t h) c", c=GK), AX.X).then_inc(sq_done, 1)
                            dve.wait_ge(from_act, 3)
                            dve.tensor_scalar(u[:], e[:], 1.0, None, ALU.add).then_inc(aux, 1)
                            dve.wait_ge(aux, 2)
                            link(dve.tensor_scalar(du[:], u[:], 1.0, None, ALU.subtract))
                            link(dve.tensor_scalar(one[:], du[:], 0.0, None, ALU.is_equal))
                            link(dve.tensor_tensor(du[:], du[:], one[:], ALU.add))
                            link(dve.reciprocal(du[:], du[:]))
                            link(dve.tensor_tensor(du[:], du[:], e[:], ALU.mult))
                            link(dve.tensor_tensor(one[:], one[:], e[:], ALU.mult))
                            dve.wait_ge(from_act, 4)
                            link(dve.tensor_tensor(lnu[:], lnu[:], du[:], ALU.mult))
                            link(dve.tensor_tensor(lnu[:], lnu[:], one[:], ALU.add))
                            link(dve.scalar_tensor_tensor(x[:], x[:], 0.0, lnu[:], ALU.max, ALU.add))
                            dve.scalar_tensor_tensor(g[:], x[:], -1.0, ea[:].unsqueeze(1).broadcast_to([P, NT, GH]),
                                                     ALU.mult, ALU.mult).then_inc(to_pe, 1)
                            link(dve.tensor_scalar(eb[:], eb[:], 1.0, None, ALU.add))
                            link(dve.reciprocal(beta[:], eb[:]))
                            dve.wait_ge(from_pe, 2)
                            link(dve.tensor_copy(G[:], psum[:, 0, 0:NT * GH].rearrange("p (t h) -> p t h", h=GH)))
                            dve.tensor_tensor(dd[:], psum[:, 1, 0:NT * GH].rearrange("p (t h) -> p t h", h=GH), G[:],
                                              ALU.subtract).then_inc(aux, 1)
                            dve.wait_ge(from_act, 8)
                            link(dve.reciprocal(r[:], ss[:]))
                            for h in range(GH):
                                rows = slice(32 * (h % 4), 32 * (h % 4) + 32)
                                link(dve.tensor_copy(ETH[rows, h // 4, :], eT[rows, :, h]))
                            rq, rk = r[:, :, 0:GH], r[:, :, GH:]
                            link(dve.tensor_scalar(fk[:, 0], rq, GK ** -0.5, None, ALU.mult))
                            link(dve.tensor_tensor(fk[:, 1], fk[:, 0], eG[:], ALU.mult))
                            link(dve.tensor_tensor(fk[:, 2], rk, beta[:], ALU.mult))
                            link(dve.tensor_tensor(fk[:, 3], fk[:, 2], eG[:], ALU.mult))
                            link(dve.tensor_tensor(fk[:, 4], rk, eD[:], ALU.mult))
                            q, k = YT[:, :, 0:QKW], YT[:, :, QKW:2 * QKW]
                            for out, src, f in ((QN, q, fk[:, 0]), (QE, q, fk[:, 1]), (KN, k, rk), (KB, k, fk[:, 2]),
                                                (KBE, k, fk[:, 3]), (KD, k, fk[:, 4])):
                                for t in range(NT):
                                    dve.tensor_tensor(out[:, t], src[:, t, :].rearrange("p (h c) -> p h c", c=GK),
                                                      f[:, t, :].unsqueeze(2).broadcast_to([P, GH, GK]), ALU.mult)
                            for t in range(NT):
                                last = dve.tensor_tensor(BV[:, t], YT[:, t, 2 * QKW:].rearrange("p (h c) -> p h c", c=GV),
                                                         beta[:, t, :].unsqueeze(2).broadcast_to([P, GH, GV]), ALU.mult)

            with ExitStack() as tmp2:
                sb2 = lambda n, shape, dt=F32: core.sb(n, shape, dt, tmp2)
                KNT, KBT, QNT = (sb2(n, [P, 2, S]) for n in ("kn_features", "kb_features", "qn_features"))
                ed = sb2("exponents", [P, 2, 4, P])
                turned, kept = sem("qk_turned"), sem("qk_kept")
                e_in, e_sub, e_exp, e_done = sem("e_in"), sem("e_sub"), sem("e_exp"), sem("e_done")
                p_in, p_done, a_in, a_done = sem("p_in"), sem("p_done"), sem("a_in"), sem("a_done")
                units = [(o, i, f, half) for o, i in ((QET, QE), (KNT, KN), (KBT, KB), (QNT, QN))
                         for f in range(2) for half in range(NH2)]
                NB = GH * 2
                with nc.Block() as block:
                    @block.tensor
                    def _(pe):
                        for n, (o, i, f, half) in enumerate(units):
                            w = P if f == 0 else QKW - P
                            if n >= 2:
                                pe.wait_ge(kept, n - 1)
                            for j in range(4):
                                t = 4 * half + j
                                last = pe.transpose(psum[0:w, n % 2, j * P:(j + 1) * P],
                                                    i[:, t].rearrange("p h c -> p (h c)")[:, f * P:f * P + w], ident[:])
                            last.then_inc(turned, 1)
                        pe.wait_ge(kept, len(units))
                        for b in range(NB):
                            h, half = b // 2, b % 2
                            rows = slice(32 * (h % 4), 32 * (h % 4) + 32)
                            if b >= 2:
                                pe.wait_ge(e_sub, b - 1)
                                pe.wait_ge(p_done, b - 1)
                                pe.wait_ge(a_done, b - 1)
                            for j in range(4):
                                t = 4 * half + j
                                last = pe.matmul(psum[:, 2 + b % 2, j * P:(j + 1) * P],
                                                 g[:, t, h:h + 1].broadcast_to([P, P]), tri[:], start=True, stop=True)
                            last.then_inc(e_in, 1)
                            for j in range(4):
                                t = 4 * half + j
                                last = pe.matmul(psum[:, 4 + b % 2, j * P:(j + 1) * P], KNT[rows, h // 4, t * P:(t + 1) * P],
                                                 QNT[rows, h // 4, t * P:(t + 1) * P], start=True, stop=True)
                            last.then_inc(p_in, 1)
                            for j in range(4):
                                t = 4 * half + j
                                last = pe.matmul(psum[:, 6 + b % 2, j * P:(j + 1) * P], KNT[rows, h // 4, t * P:(t + 1) * P],
                                                 KBT[rows, h // 4, t * P:(t + 1) * P], start=True, stop=True)
                            last.then_inc(a_in, 1)

                    @block.scalar
                    def _(act):
                        for n, (o, i, f, half) in enumerate(units):
                            w = P if f == 0 else QKW - P
                            act.wait_ge(turned, n + 1)
                            act.activation(o[0:w, f, half * HALF:(half + 1) * HALF], psum[0:w, n % 2, :],
                                           ACT.Copy).then_inc(kept, 1)
                        for b in range(NB):
                            act.wait_ge(e_sub, b + 1)
                            if b >= 1:
                                act.wait_ge(e_done, b)
                            act.activation(ed[:, b % 2], ed[:, b % 2], ACT.Exp).then_inc(e_exp, 1)

                    @block.vector
                    def _(dve):
                        for b in range(NB + 1):
                            if b < NB:
                                h, half = b // 2, b % 2
                                dve.wait_ge(e_in, b + 1)
                                if b >= 2:
                                    dve.wait_ge(e_done, b - 1)
                                for j in range(4):
                                    last = dve.tensor_scalar(ed[:, b % 2, j], psum[:, 2 + b % 2, j * P:(j + 1) * P],
                                                             G[:, 4 * half + j, h:h + 1], 0.0, ALU.subtract, ALU.min)
                                last.then_inc(e_sub, 1)
                            if b >= 1:
                                c = b - 1
                                blk = slice(4 * c, 4 * c + 4)
                                dve.wait_ge(e_exp, c + 1)
                                dve.tensor_tensor(EA[:, blk], ed[:, c % 2],
                                                  tri[:].unsqueeze(1).broadcast_to([P, 4, P]),
                                                  ALU.mult).then_inc(e_done, 1)
                                dve.wait_ge(e_done, c + 1)
                                dve.wait_ge(p_in, c + 1)
                                dve.tensor_tensor(PT[:, blk], psum[:, 4 + c % 2, :].rearrange("p (t n) -> p t n", t=4),
                                                  EA[:, blk], ALU.mult).then_inc(p_done, 1)
                                dve.wait_ge(p_done, c + 1)
                                dve.wait_ge(a_in, c + 1)
                                dve.scalar_tensor_tensor(EA[:, blk], psum[:, 6 + c % 2, :].rearrange("p (t n) -> p t n", t=4),
                                                         -1.0, EA[:, blk], ALU.mult, ALU.mult).then_inc(a_done, 1)

            norm_scope.close()

            TT = core.sb("t_inverse_transposed", [P, GH * NT, P], F32, mid_scope)
            nWT = core.sb("minus_w_features", [P, 2, S], F32, mid_scope)
            with ExitStack() as tmp2:
                sb2 = lambda n, shape, dt=F32: core.sb(n, shape, dt, tmp2)
                masks = sb2("level_masks", [P, 2, LEVELS, P], U32)
                T = sb2("t_inverse", [P, 2, 4, P])
                Xs = sb2("a_times_t", [P, 2, 4, P])
                mload, ident_in, t_init, a_turned = sem("masks"), sem("ident_in"), sem("t_init"), sem("a_turned")
                x_in, x_kept, y_in, t_upd, w_in, w_kept = (sem(n) for n in ("x_in", "x_kept", "y_in", "t_upd", "w_in", "w_kept"))
                NB = GH * 2
                L = LEVELS - 1
                with nc.Block() as block:
                    @block.sync
                    def _(sp):
                        sp.dma_start(masks[:].rearrange("p a l n -> p (a l n)"), d["masks"]).then_inc(mload, 16)

                    @block.tensor
                    def _(pe):
                        for grp in range(NB // 2):
                            for s in range(2):
                                b = 2 * grp + s
                                if grp >= 1:
                                    pe.wait_ge(w_kept, b - 1)
                                for j in range(4):
                                    last = pe.transpose(psum[:, 2 * s, j * P:(j + 1) * P], EA[:, 4 * b + j, :], ident[:])
                                last.then_inc(a_turned, 1)
                            for lv in range(L):
                                for s in range(2):
                                    b = 2 * grp + s
                                    pe.wait_ge(t_upd, 4 * (grp * (L + 1) + lv) + 2 * s + 2 - (0 if lv < L else 0))
                                    for j in range(4):
                                        last = pe.matmul(psum[:, 6 + s, j * P:(j + 1) * P], EA[:, 4 * b + j, :],
                                                         T[:, s, j, :], start=True, stop=True)
                                    last.then_inc(x_in, 1)
                                for s in range(2):
                                    b = 2 * grp + s
                                    pe.wait_ge(x_kept, 2 * (grp * L + lv) + s + 1)
                                    if lv < L - 1:
                                        for j in range(4):
                                            pe.matmul(psum[:, 2 * s, j * P:(j + 1) * P], TT[:, 4 * b + j, :],
                                                      Xs[:, s, j, :], start=True, stop=True)
                                    for j in range(4):
                                        last = pe.matmul(psum[:, 2 * s + 1, j * P:(j + 1) * P], Xs[:, s, j, :],
                                                         TT[:, 4 * b + j, :], start=True, stop=True)
                                    last.then_inc(y_in, 1)
                            for s in range(2):
                                b = 2 * grp + s
                                h, half = b // 2, b % 2
                                rows = slice(32 * (h % 4), 32 * (h % 4) + 32)
                                pe.wait_ge(t_upd, 4 * (grp * (L + 1) + L) + 2 * s + 2)
                                for j in range(4):
                                    t = 4 * half + j
                                    last = pe.matmul(psum[rows, 2 * s, j * P:(j + 1) * P], KBE[:, t, h, :],
                                                     TT[:, 4 * b + j, :], start=True, stop=True)
                                last.then_inc(w_in, 1)

                    @block.scalar
                    def _(act):
                        for grp in range(NB // 2):
                            for s in range(2):
                                b = 2 * grp + s
                                act.activation(TT[:, 4 * b:4 * b + 4, :], ident[:].unsqueeze(1).broadcast_to([P, 4, P]),
                                               ACT.Copy).then_inc(t_init, 1)
                                if grp >= 1:
                                    act.wait_ge(x_in, 2 * grp * L - (1 - s))
                                act.activation(T[:, s], ident[:].unsqueeze(1).broadcast_to([P, 4, P]),
                                               ACT.Copy).then_inc(t_init, 1)
                            for lv in range(L):
                                for s in range(2):
                                    act.wait_ge(x_in, 2 * (grp * L + lv) + s + 1)
                                    if grp * L + lv >= 1:
                                        act.wait_ge(y_in, 2 * (grp * L + lv - 1) + s + 1)
                                    act.activation(Xs[:, s], psum[:, 6 + s, :].rearrange("p (t n) -> p t n", t=4),
                                                   ACT.Copy).then_inc(x_kept, 1)
                            for s in range(2):
                                b = 2 * grp + s
                                h, half = b // 2, b % 2
                                rows = slice(32 * (h % 4), 32 * (h % 4) + 32)
                                act.wait_ge(w_in, b + 1)
                                act.activation(nWT[rows, h // 4, half * HALF:(half + 1) * HALF],
                                               psum[rows, 2 * s, :], ACT.Copy, scale=-1.0).then_inc(w_kept, 1)

                    @block.vector
                    def _(dve):
                        dve.wait_ge(mload, 16)
                        mk = lambda side, lv: masks[:, side, lv, :].unsqueeze(1).broadcast_to([P, 4, P])
                        for grp in range(NB // 2):
                            for lv in range(L + 1):
                                for s in range(2):
                                    b = 2 * grp + s
                                    blk = slice(4 * b, 4 * b + 4)
                                    if lv == 0:
                                        dve.wait_ge(a_turned, b + 1)
                                        dve.wait_ge(t_init, 2 * b + 2)
                                        src, srcT = psum[:, 2 * s, :].rearrange("p (t n) -> p t n", t=4), EA[:, blk]
                                    else:
                                        dve.wait_ge(y_in, 2 * (grp * L + lv - 1) + s + 1)
                                        src = psum[:, 2 * s, :].rearrange("p (t n) -> p t n", t=4)
                                        srcT = psum[:, 2 * s + 1, :].rearrange("p (t n) -> p t n", t=4)
                                    if lv < L:
                                        dve.copy_predicated(T[:, s], mk(0, lv), src).then_inc(t_upd, 1)
                                        dve.copy_predicated(TT[:, blk], mk(1, lv), srcT).then_inc(t_upd, 1)
                                    else:
                                        dve.copy_predicated(TT[:, blk], mk(1, lv), srcT).then_inc(t_upd, 2)

            O = core.sb("delta_out", [P, NT, VWD], F32, mid_scope)
            with ExitStack() as tmp2:
                sb2 = lambda n, shape, dt=F32: core.sb(n, shape, dt, tmp2)
                St = sb2("state", [P, 2, GV])
                SD = sb2("state_blocks", [P, 2, 4, GV])
                own = sb2("own_block", [P, 4, GV])
                U = sb2("u", [P, 2, VWD])
                s0, u_in, u_kept, s_in, s_done, o_in, o_kept = (sem(n) for n in
                    ("state_zeroed", "u_in", "u_kept", "s_in", "s_done", "o_in", "o_kept"))
                blocked, own_in = sem("state_blocked"), sem("own_loaded")
                WID = ((P, 4), (QKW - P, 2))
                with nc.Block() as block:
                    @block.sync
                    def _(sp):
                        sp.dma_start(own[:].rearrange("p a n -> p (a n)"), d["own"]).then_inc(own_in, 16)

                    @block.tensor
                    def _(pe):
                        def by_state(o, lhsT, t):
                            for f, (w, nh) in enumerate(WID):
                                last = pe.matmul(o[:, f * 4 * GV:(f * 4 + nh) * GV], lhsT[0:w, f, t * P:(t + 1) * P],
                                                 SD[0:w, f, 0:nh, :].rearrange("p a n -> p (a n)"),
                                                 start=False, stop=(f == 1), skip_group_check=True)
                            return last

                        for t in range(NT):
                            if t >= 2:
                                pe.wait_ge(u_kept, t - 1)
                            for h in range(GH):
                                pe.matmul(psum[:, t % 2, h * GV:(h + 1) * GV], TT[:, h * NT + t, :], BV[:, t, h, :],
                                          start=(h == 0), stop=False, skip_group_check=True)
                            pe.wait_ge(blocked, 2 * t + 2)
                            by_state(psum[:, t % 2, 0:VWD], nWT, t).then_inc(u_in, 1)
                            pe.wait_ge(u_kept, t + 1)
                            for h in range(GH):
                                rows = slice(32 * (h % 4), 32 * (h % 4) + 32)
                                last = pe.matmul(psum[rows, 4 + t % 2, (h // 4) * GV:(h // 4 + 1) * GV], KD[:, t, h, :],
                                                 U[:, t % 2, h * GV:(h + 1) * GV], start=True, stop=True)
                            last.then_inc(s_in, 1)
                            if t >= 2:
                                pe.wait_ge(o_kept, t - 1)
                            for h in range(GH):
                                pe.matmul(psum[:, 2 + t % 2, h * GV:(h + 1) * GV], PT[:, h * NT + t, :],
                                          U[:, t % 2, h * GV:(h + 1) * GV], start=(h == 0), stop=False,
                                          skip_group_check=True)
                            by_state(psum[:, 2 + t % 2, 0:VWD], QET, t).then_inc(o_in, 1)

                    @block.vector
                    def _(dve):
                        dve.memset(St[:], 0.0).then_inc(s0, 1)
                        dve.memset(SD[:], 0.0).then_inc(blocked, 2)
                        dve.wait_ge(s0, 1)
                        dve.wait_ge(own_in, 16)
                        dve.wait_ge(blocked, 2)
                        for t in range(NT):
                            dve.wait_ge(u_in, t + 1)
                            if t >= 2:
                                dve.wait_ge(s_in, t - 1)
                                dve.wait_ge(o_in, t - 1)
                            dve.tensor_copy(U[:, t % 2, :], psum[:, t % 2, 0:VWD]).then_inc(u_kept, 1)
                            dve.wait_ge(s_in, t + 1)
                            if t >= 1:
                                dve.wait_ge(blocked, 2 * t + 2)
                            for f, (w, nh) in enumerate(WID):
                                dve.scalar_tensor_tensor(St[0:w, f, :], St[0:w, f, :], ETH[0:w, f, t:t + 1],
                                                         psum[0:w, 4 + t % 2, f * GV:(f + 1) * GV],
                                                         ALU.mult, ALU.add).then_inc(s_done, 1)
                            dve.wait_ge(o_in, t + 1)
                            dve.wait_ge(s_done, 2 * t + 2)
                            for f, (w, nh) in enumerate(WID):
                                dve.tensor_tensor(SD[0:w, f, 0:nh, :], St[0:w, f, :].unsqueeze(1).broadcast_to([w, nh, GV]),
                                                  own[0:w, 0:nh, :], ALU.mult).then_inc(blocked, 1)

                    @block.scalar
                    def _(act):
                        for t in range(NT):
                            act.wait_ge(o_in, t + 1)
                            act.activation(O[:, t, :], psum[:, 2 + t % 2, 0:VWD], ACT.Copy).then_inc(o_kept, 1)

            with ExitStack() as tmp2:
                sb2 = lambda n, shape, dt=F32: core.sb(n, shape, dt, tmp2)
                sq = sb2("o_squares", [P, NT, VWD])
                ms, rr = sb2("o_mean_squares", [P, NT * GH]), sb2("o_inverse_rms", [P, NT * GH])
                ch, sw, sg_done, to_act, from_act = sem("norm_chain"), sem("gate_w"), sem("gate_w2"), sem("rms_in"), sem("rms_out")
                with nc.Block() as block:
                    @block.gpsimd
                    def _(pool):
                        for t in range(NT):
                            pool.tensor_tensor(SG[:, t].rearrange("p (h c) -> p h c", c=GV),
                                               SG[:, t].rearrange("p (h c) -> p h c", c=GV),
                                               nw[:].unsqueeze(1).broadcast_to([P, GH, GV]), ALU.mult).then_inc(sw, 1)

                    @block.scalar
                    def _(act):
                        act.wait_ge(to_act, 1)
                        act.activation(ms[:], ms[:], ACT.Sqrt).then_inc(from_act, 1)

                    @block.vector
                    def _(dve):
                        n = [0]

                        def link(i):
                            n[0] += 1
                            i.then_inc(ch, 1)
                            dve.wait_ge(ch, n[0])

                        link(dve.tensor_tensor(sq[:], O[:], O[:], ALU.mult))
                        link(dve.reduce_sum(ms[:], sq[:].rearrange("p t (h c) -> p (t h) c", c=GV), AX.X))
                        dve.tensor_scalar(ms[:], ms[:], 1.0 / GV, RMS_EPS, ALU.mult, ALU.add).then_inc(to_act, 1)
                        dve.wait_ge(from_act, 1)
                        link(dve.reciprocal(rr[:], ms[:]))
                        link(dve.tensor_tensor(O[:].rearrange("p t (h c) -> p (t h) c", c=GV),
                                               O[:].rearrange("p t (h c) -> p (t h) c", c=GV),
                                               rr[:].unsqueeze(2).broadcast_to([P, NT * GH, GV]), ALU.mult))
                        dve.wait_ge(sw, NT)
                        dve.tensor_tensor(O[:], O[:], SG[:], ALU.mult)

            project_out(nc, core, tag, O, wo, None, tiles=3)



NX = 8
RANK = 16
TOPK = 2
DH = 704
ALPHA = 2.0
FT = [(f * P, min(P, DH - f * P)) for f in range(-(-DH // P))]
NFT = len(FT)


def routed_weights(nc, core, d, scope):
    w = {
        "gate": core.sb("router", [P, KT, NX], F32, scope),
        "up": core.sb("w_up", [P, KT, DH], F32, scope), "gt": core.sb("w_gate", [P, KT, DH], F32, scope),
        "upA": core.sb("up_a", [P, KT, P], F32, scope), "gtA": core.sb("gate_a", [P, KT, P], F32, scope),
        "upB": core.sb("up_b", [P, DH], F32, scope), "gtB": core.sb("gate_b", [P, DH], F32, scope),
        "down": core.sb("w_down", [P, NFT, D], F32, scope), "dnA": core.sb("down_a", [P, NFT, P], F32, scope),
        "dnB": core.sb("down_b", [P, D], F32, scope), "expert": core.sb("expert_of_column", [P, P], F32, scope),
    }
    loaded = core.sem("routed_w_loaded")
    full = (NFT - 1) * P
    with nc.Block() as block:
        @block.sync
        def _(sp):
            n = 0
            for name in ("gate", "upA", "gtA", "up", "gt"):
                sp.dma_start(w[name][:], d[name].rearrange("(k p) n -> p k n", p=P)).then_inc(loaded, 16)
                n += 16
            for name in ("upB", "gtB", "dnB", "expert"):
                sp.dma_start(w[name][:], d[name]).then_inc(loaded, 16)
                n += 16
            for name in ("down", "dnA"):
                sp.dma_start(w[name][:, 0:NFT - 1, :], d[name][0:full, :].rearrange("(k p) n -> p k n", p=P)
                             ).then_inc(loaded, 16)
                sp.dma_start(w[name][0:DH - full, NFT - 1, :], d[name][full:DH, :]).then_inc(loaded, 16)
                n += 32
            sp.wait_ge(loaded, n)
    return w


def routed_layer(nc, core, tag, d):
    with ExitStack() as scope:
        w = routed_weights(nc, core, d, scope)
        norm_stage(nc, core, tag + "n")
        routed_ffn(nc, core, tag, w)


def routed_ffn(nc, core, tag, w):
    X, XNT, psum, ident = core.X, core.XNT, core.psum, core.ident
    sem = lambda n: core.sem(f"{tag}_{n}")
    with ExitStack() as tmp:
        sb = lambda n, shape, dt=F32: core.sb(n, shape, dt, tmp)
        MASK = sb("expert_mask", [P, TOPK, S])
        CB = sb("weight_rows", [P, TOPK, S])
        with ExitStack() as tmp2:
            sb2 = lambda n, shape, dt=F32: core.sb(n, shape, dt, tmp2)
            LG, m8 = sb2("logits", [P, NT, NX]), sb2("sorted", [P, NT, 8])
            ix, ixf = sb2("indices", [P, NT, 8], U32), sb2("indices_f", [P, NT, TOPK])
            pm, gm, ps_, rs = (sb2(n, [P, TOPK]) for n in ("part_max", "all_max", "part_sum", "inv_sum"))
            ev, cw = sb2("exp_top", [P, NT, TOPK]), sb2("weights", [P, NT, TOPK])
            mk = sb2("wide_rows", [P, 2, TOPK, NT, P])
            lg_in, lg_out, top, idx, ch = sem("logits"), sem("logits_kept"), sem("top"), sem("index"), sem("chain")
            pmax, gmax, dif, ex, tot, tot_in = sem("part_max"), sem("all_max"), sem("dif"), sem("exp"), sem("part_sum"), sem("total")
            wide, turned, kept = sem("wide"), sem("turned"), sem("kept")
            with nc.Block() as block:
                @block.tensor
                def _(pe):
                    for t in range(NT):
                        for k in range(KT):
                            last = pe.matmul(psum[:, 0, t * NX:(t + 1) * NX], XNT[:, k, t * P:(t + 1) * P],
                                             w["gate"][:, k, :], start=(k == 0), stop=(k == KT - 1))
                    last.then_inc(lg_in, 1)
                    pe.wait_ge(tot, 1)
                    pe.matmul(psum[:, 1, 0:TOPK], core.ones_sq[:], ps_[:], start=True, stop=True).then_inc(tot_in, 1)
                    n = 0
                    for kind in range(2):
                        pe.wait_ge(wide, kind + 1)
                        for k in range(TOPK):
                            for half in range(NH2):
                                if n >= 4:
                                    pe.wait_ge(kept, n - 3)
                                for j in range(4):
                                    last = pe.transpose(psum[:, 4 + n % 4, j * P:(j + 1) * P],
                                                        mk[:, kind, k, 4 * half + j, :], ident[:])
                                last.then_inc(turned, 1)
                                n += 1

                @block.gpsimd
                def _(pool):
                    pool.wait_ge(pmax, 1)
                    pool.partition_all_reduce(gm[:], pm[:], P, bass.bass_isa.ReduceOp.max).then_inc(gmax, 1)

                @block.scalar
                def _(act):
                    act.wait_ge(dif, 1)
                    act.activation(ev[:], ev[:], ACT.Exp).then_inc(ex, 1)
                    n = 0
                    for o in (MASK, CB):
                        for k in range(TOPK):
                            for half in range(NH2):
                                act.wait_ge(turned, n + 1)
                                act.activation(o[:, k, half * HALF:(half + 1) * HALF], psum[:, 4 + n % 4, :],
                                               ACT.Copy).then_inc(kept, 1)
                                n += 1

                @block.vector
                def _(dve):
                    c = [0]

                    def link(i):
                        c[0] += 1
                        i.then_inc(ch, 1)
                        dve.wait_ge(ch, c[0])

                    dve.wait_ge(lg_in, 1)
                    dve.tensor_copy(LG[:].rearrange("p t n -> p (t n)"), psum[:, 0, 0:NT * NX]).then_inc(lg_out, 1)
                    dve.wait_ge(lg_out, 1)
                    for t in range(NT):
                        dve.max(m8[:, t, :], LG[:, t, :]).then_inc(top, 1)
                    dve.wait_ge(top, NT)
                    dve.reduce_max(pm[:], m8[:, :, 0:TOPK].rearrange("p t k -> p k t"), AX.X).then_inc(pmax, 1)
                    for t in range(NT):
                        dve.max_index(ix[:, t, :], m8[:, t, :], LG[:, t, :]).then_inc(idx, 1)
                    dve.wait_ge(idx, NT)
                    link(dve.tensor_copy(ixf[:], ix[:, :, 0:TOPK]))
                    for k in range(TOPK):
                        for t in range(NT):
                            last = dve.tensor_scalar(mk[:, 0, k, t, :], w["expert"][:], ixf[:, t, k:k + 1], ALPHA,
                                                     ALU.is_equal, ALU.mult)
                    last.then_inc(wide, 1)
                    dve.wait_ge(gmax, 1)
                    dve.tensor_tensor(ev[:], m8[:, :, 0:TOPK], gm[:].unsqueeze(1).broadcast_to([P, NT, TOPK]),
                                      ALU.subtract).then_inc(dif, 1)
                    dve.wait_ge(ex, 1)
                    dve.reduce_sum(ps_[:], ev[:].rearrange("p t k -> p k t"), AX.X).then_inc(tot, 1)
                    dve.wait_ge(tot_in, 1)
                    link(dve.reciprocal(rs[:], psum[:, 1, 0:TOPK]))
                    link(dve.tensor_tensor(cw[:], ev[:], rs[:].unsqueeze(1).broadcast_to([P, NT, TOPK]), ALU.mult))
                    for k in range(TOPK):
                        for t in range(NT):
                            last = dve.tensor_scalar(mk[:, 1, k, t, :], core.ones_sq[:], cw[:, t, k:k + 1], None, ALU.mult)
                    last.then_inc(wide, 1)

        H = sb("slot_hidden", [P, TOPK, NFT, S])
        MX = sb("mixed_hidden", [P, NFT, S])
        DL = sb("lora_down", [P, S])
        with ExitStack() as tmp2:
            sb2 = lambda n, shape, dt=F32: core.sb(n, shape, dt, tmp2)
            Z = sb2("lora_in", [P, 2, TOPK, S])
            sil, gc = sb2("silu", [P, 2, HALF]), sb2("gate_weighted", [P, 2, HALF])
            z_in, z_done, up_in, silu, gated, hid, mixed = (sem(n) for n in
                ("z_in", "z_done", "up_in", "silu", "gated", "hidden", "mixed"))
            units = [(half, f, k) for half in range(NH2) for f in range(NFT) for k in range(TOPK)]
            with nc.Block() as block:
                @block.tensor
                def _(pe):
                    for half in range(NH2):
                        for j, wa in enumerate(("upA", "gtA")):
                            for k in range(KT):
                                last = pe.matmul(psum[:, 4 + 2 * half + j, :], w[wa][:, k, :],
                                                 XNT[:, k, half * HALF:(half + 1) * HALF],
                                                 start=(k == 0), stop=(k == KT - 1))
                            last.then_inc(z_in, 1)
                    for u, (half, f, k) in enumerate(units):
                        a, n = FT[f]
                        cols = slice(half * HALF, (half + 1) * HALF)
                        if u == 0:
                            pe.wait_ge(z_done, 2 * TOPK)
                        if (half, f, k) == (1, 0, 0):
                            pe.wait_ge(z_done, 4 * TOPK)
                        if u >= 2:
                            pe.wait_ge(silu, u - 1)
                            pe.wait_ge(gated, u - 1)
                        for j, (wb, wl) in enumerate((("up", "upB"), ("gt", "gtB"))):
                            o = psum[0:n, 2 * (u % 2) + j, :]
                            for kk in range(KT):
                                pe.matmul(o, w[wb][:, kk, a:a + n], XNT[:, kk, cols], start=(kk == 0), stop=False)
                            pe.matmul(o, w[wl][:, a:a + n], Z[:, j, k, cols], start=False, stop=True).then_inc(up_in, 1)

                @block.scalar
                def _(act):
                    for u, (half, f, k) in enumerate(units):
                        n = FT[f][1]
                        act.wait_ge(up_in, 2 * u + 1)
                        if u >= 2:
                            act.wait_ge(hid, u - 1)
                        act.activation(sil[0:n, u % 2, :], psum[0:n, 2 * (u % 2), :], ACT.Silu).then_inc(silu, 1)

                @block.vector
                def _(dve):
                    n = 0
                    for half in range(NH2):
                        for j in range(2):
                            dve.wait_ge(z_in, 2 * half + j + 1)
                            for k in range(TOPK):
                                dve.tensor_tensor(Z[:, j, k, half * HALF:(half + 1) * HALF], psum[:, 4 + 2 * half + j, :],
                                                  MASK[:, k, half * HALF:(half + 1) * HALF], ALU.mult).then_inc(z_done, 1)
                    for u, (half, f, k) in enumerate(units):
                        n = FT[f][1]
                        cols = slice(half * HALF, (half + 1) * HALF)
                        dve.wait_ge(up_in, 2 * u + 2)
                        dve.tensor_tensor(gc[0:n, u % 2, :], psum[0:n, 2 * (u % 2) + 1, :], CB[0:n, k, cols],
                                          ALU.mult).then_inc(gated, 1)
                        dve.wait_ge(gated, u + 1)
                        dve.wait_ge(silu, u + 1)
                        dve.tensor_tensor(H[0:n, k, f, cols], gc[0:n, u % 2, :], sil[0:n, u % 2, :],
                                          ALU.mult).then_inc(hid, 1)

                @block.gpsimd
                def _(pool):
                    for half in range(NH2):
                        for f in range(NFT):
                            n = FT[f][1]
                            cols = slice(half * HALF, (half + 1) * HALF)
                            pool.wait_ge(hid, TOPK * (half * NFT + f + 1))
                            pool.tensor_tensor(MX[0:n, f, cols], H[0:n, 0, f, cols], H[0:n, 1, f, cols],
                                               ALU.add).then_inc(mixed, 1)

        with ExitStack() as tmp2:
            d1 = core.sb("lora_down_second", [P, S], F32, tmp2)
            d_in, d_part, d_done, out_in, added = sem("d_in"), sem("d_part"), sem("d_done"), sem("out_in"), sem("added")
            with nc.Block() as block:
                @block.tensor
                def _(pe):
                    for half in range(NH2):
                        for k in range(TOPK):
                            for f, (a, n) in enumerate(FT):
                                last = pe.matmul(psum[:, 2 * half + k, :], w["dnA"][0:n, f, :],
                                                 H[0:n, k, f, half * HALF:(half + 1) * HALF],
                                                 start=(f == 0), stop=(f == NFT - 1))
                            last.then_inc(d_in, 1)
                    for t in range(NT):
                        if t >= 4:
                            pe.wait_ge(added, t - 3)
                        for f, (a, n) in enumerate(FT):
                            pe.matmul(psum[:, 4 + t % 4, 0:D], MX[0:n, f, t * P:(t + 1) * P], w["down"][0:n, f, :],
                                      start=(f == 0), stop=False)
                        pe.wait_ge(d_done, t // 4 + 1)
                        pe.matmul(psum[:, 4 + t % 4, 0:D], DL[:, t * P:(t + 1) * P], w["dnB"][:],
                                  start=False, stop=True).then_inc(out_in, 1)

                @block.vector
                def _(dve):
                    for half in range(NH2):
                        cols = slice(half * HALF, (half + 1) * HALF)
                        for k, o in enumerate((DL, d1)):
                            dve.wait_ge(d_in, 2 * half + k + 1)
                            dve.tensor_tensor(o[:, cols], psum[:, 2 * half + k, :], MASK[:, k, cols],
                                              ALU.mult).then_inc(d_part, 1)
                        dve.wait_ge(d_part, 2 * half + 2)
                        dve.tensor_tensor(DL[:, cols], DL[:, cols], d1[:, cols], ALU.add).then_inc(d_done, 1)
                    for t in range(NT):
                        dve.wait_ge(out_in, t + 1)
                        dve.tensor_tensor(X[:, t, :], psum[:, 4 + t % 4, 0:D], X[:, t, :], ALU.add).then_inc(added, 1)


LAT, RD = 64, 64
NOPE = LAT
QROWS = RD + HD
SHIFT = 96
NEG = -1e30


def latent_attention(nc, core, tag, d):
    X, XNT, psum, ident = core.X, core.XNT, core.psum, core.ident
    sem = lambda n: core.sem(f"{tag}_{n}")
    SC = float(1.0 / np.sqrt(np.float32(HD + RD)))
    with ExitStack() as tmp:
        sb = lambda n, shape, dt=F32: core.sb(n, shape, dt, tmp)
        V = sb("v_ones", [P, NT, HEADS, VW])
        O = sb("attended", [P, NT, D])
        wo = sb("wo", [P, KT, D])
        with ExitStack() as tmpA:
            sba = lambda n, shape, dt=F32: core.sb(n, shape, dt, tmpA)
            Q = sba("q_all", [P, HEADS, S])
            Qb = sba("q_all_bf16", [QROWS, HEADS, S], BF16)
            K = sba("k_head", [P, 2, S])
            Kb = sba("k_head_bf16", [QROWS, 2, S], BF16)
            kT = sba("k_features", [P, KT, S])
            kTb = sba("k_features_bf16", [P, KT, S], BF16)
            with ExitStack() as tmp2:
                sb2 = lambda n, shape, dt=F32: core.sb(n, shape, dt, tmp2)
                w1 = sb2("w_latents", [P, KT, 3 * LAT])
                w1r = sb2("w_kr_rotated", [P, KT, RD])
                wq = sb2("w_q", [LAT, HEADS, QROWS])
                wqr = sb2("w_q_rotated", [LAT, HEADS, RD])
                wk, wv = sb2("w_ku", [LAT, D]), sb2("w_vu", [LAT, D])
                cos, sin = sb2("cos", [RD, S]), sb2("sin", [RD, S])
                L = sb2("latents", [LAT, 2, S])
                t1 = O[0:RD].rearrange("p (a t) n -> p a (t n)", a=2)
                t2 = sb2("by_sin", [RD, 2, S])
                loaded, rot, made = sem("loaded"), sem("rotated_w"), sem("made")
                l_in, l_out = sem("l_in"), sem("l_out")
                q_in, c_done, s_done, q_done, qn_done, qb_done = (sem(n) for n in
                    ("q_in", "by_cos", "by_sin", "q_rope", "q_plain", "q_bf16"))
                kr_ready, kfeat, kf_out, v_in, v_out = sem("kr_ready"), sem("kf_in"), sem("kf_out"), sem("v_in"), sem("v_out")
                krep, q_zeroed = sem("kr_copies"), sem("q_rows_zeroed")
                pair = lambda b: psum[:, 2 * b:2 * b + 2, :].rearrange("p a n -> p (a n)")
                with nc.Block() as block:
                    @block.sync
                    def _(sp):
                        sp.dma_start(w1[:], d["w1"].rearrange("(k p) n -> p k n", p=P)).then_inc(loaded, 16)
                        sp.dma_start(wq[:].rearrange("p h n -> p (h n)"), d["wq"]).then_inc(loaded, 16)
                        sp.dma_start(wk[:], d["wku"]).then_inc(loaded, 16)
                        sp.dma_start(wv[:], d["wvu"]).then_inc(loaded, 16)
                        sp.dma_start(cos[:], d["cos"]).then_inc(loaded, 16)
                        sp.dma_start(sin[:], d["sin"]).then_inc(loaded, 16)
                        sp.dma_start(wo[:], d["wo"].rearrange("(k p) n -> p k n", p=P)).then_inc(loaded, 16)
                        sp.wait_ge(loaded, 16 * 7)

                    @block.gpsimd
                    def _(pool):
                        pool.memset(V[:], 0.0).then_inc(made, 1)
                        pool.wait_ge(made, 1)
                        pool.memset(V[:, :, :, HD:HD + 1], 1.0).then_inc(made, 1)
                        pool.wait_ge(made, 2)
                        pool.memset(K[64:96, :, :], 0.0).then_inc(made, 1)
                        pool.wait_ge(made, 3)
                        pool.memset(K[SHIFT:SHIFT + 1, :, :], 1.0).then_inc(made, 1)
                        for n in range(1 + HEADS):
                            pool.wait_ge(c_done, n + 1)
                            pool.wait_ge(s_done, n + 1)
                            if n == 0:
                                pool.tensor_tensor(K[0:RD, 0, :], t1[:, 0, :], t2[:, 0, :], ALU.add).then_inc(q_done, 1)
                            else:
                                pool.tensor_tensor(Q[0:RD, n - 1, :], t1[:, n % 2, :], t2[:, n % 2, :],
                                                   ALU.add).then_inc(q_done, 1)

                    @block.tensor
                    def _(pe):
                        pe.wait_ge(rot, 3)
                        for n, wsl in enumerate((w1[:, :, 0:LAT], w1[:, :, LAT:2 * LAT], w1[:, :, 2 * LAT:], w1r[:, :, :])):
                            for half in range(NH2):
                                for k in range(KT):
                                    last = pe.matmul(psum[0:LAT, 2 * n + half, :], wsl[:, k, :],
                                                     XNT[:, k, half * HALF:(half + 1) * HALF],
                                                     start=(k == 0), stop=(k == KT - 1))
                            last.then_inc(l_in, 1)
                        pe.wait_ge(l_out, 2)
                        for f in range(KT):
                            for half in range(NH2):
                                last = pe.matmul(psum[:, 2 * f + half, :], wk[:, f * P:(f + 1) * P],
                                                 L[:, 1, half * HALF:(half + 1) * HALF], start=True, stop=True)
                            last.then_inc(kfeat, 1)
                        for t in range(NT):
                            pe.wait_ge(kf_out, 4)
                            if t >= 2:
                                pe.wait_ge(v_out, t - 1)
                            pe.matmul(psum[:, t % 2, 0:D], L[:, 1, t * P:(t + 1) * P], wv[:], start=True,
                                      stop=True).then_inc(v_in, 1)
                        for h in range(HEADS):
                            b = 2 * (h % 2)
                            if h == 0:
                                pe.wait_ge(v_out, NT)
                                pe.wait_ge(c_done, 1)
                                pe.wait_ge(s_done, 1)
                            if h >= 2:
                                pe.wait_ge(c_done, h)
                                pe.wait_ge(s_done, h)
                                pe.wait_ge(qn_done, h - 1)
                            for half in range(NH2):
                                pe.matmul(psum[0:QROWS, 2 * b + half, :], wq[:, h, :], L[:, 0, half * HALF:(half + 1) * HALF],
                                          start=True, stop=True)
                            for half in range(NH2):
                                last = pe.matmul(psum[0:RD, 2 * b + 2 + half, :], wqr[:, h, :],
                                                 L[:, 0, half * HALF:(half + 1) * HALF], start=True, stop=True)
                            last.then_inc(q_in, 1)

                    @block.scalar
                    def _(act):
                        for n in range(2):
                            act.wait_ge(l_in, n + 1)
                            act.activation(L[:, n, :], pair(n)[0:LAT], ACT.Copy).then_inc(l_out, 1)
                        for f in range(KT):
                            act.wait_ge(kfeat, f + 1)
                            act.activation(kT[:, f, :], pair(f), ACT.Copy).then_inc(kf_out, 1)
                            act.activation(kTb[:, f, :], pair(f), ACT.Copy).then_inc(kf_out, 1)
                        act.wait_ge(made, 2)
                        for t in range(NT):
                            act.wait_ge(v_in, t + 1)
                            act.activation(V[:, t, :, 0:HD], psum[:, t % 2, 0:D].rearrange("p (h d) -> p h d", d=HD),
                                           ACT.Copy).then_inc(v_out, 1)
                        act.wait_ge(q_done, 1)
                        act.activation(K[0:RD, 1, :], K[0:RD, 0, :], ACT.Copy).then_inc(krep, 1)
                        for b in range(2):
                            act.activation(Kb[0:RD, b, :], K[0:RD, 0, :], ACT.Copy).then_inc(krep, 1)
                        act.wait_ge(q_zeroed, 1)
                        for h in range(HEADS + 1):
                            if h < HEADS:
                                b = 2 * (h % 2)
                                act.wait_ge(q_in, h + 1)
                                act.activation(Q[NOPE:QROWS, h, :], pair(b)[NOPE:QROWS], ACT.Copy).then_inc(qn_done, 1)
                            if h >= 1:
                                act.wait_ge(q_done, h + 1)
                                act.wait_ge(qn_done, h)
                                act.activation(Qb[:, h - 1, :], Q[0:QROWS, h - 1, :], ACT.Copy).then_inc(qb_done, 1)

                    @block.vector
                    def _(dve):
                        dve.wait_ge(loaded, 16 * 7)
                        hf = RD // 2
                        kr = w1[:, :, 2 * LAT:]
                        dve.tensor_scalar(w1r[:, :, 0:hf], kr[:, :, hf:], -1.0, None, ALU.mult).then_inc(rot, 1)
                        dve.tensor_copy(w1r[:, :, hf:], kr[:, :, 0:hf])
                        dve.tensor_scalar(wqr[:, :, 0:hf], wq[:, :, hf:RD], -1.0, None, ALU.mult).then_inc(rot, 1)
                        dve.tensor_copy(wqr[:, :, hf:], wq[:, :, 0:hf]).then_inc(rot, 1)
                        dve.memset(Q[64:96, :, :], 0.0).then_inc(q_zeroed, 1)
                        for n in range(1 + HEADS):
                            if n == 0:
                                dve.wait_ge(l_in, 4)
                                p, r = pair(2)[0:RD], pair(3)[0:RD]
                            else:
                                dve.wait_ge(q_in, n)
                                b = 2 * ((n - 1) % 2)
                                p, r = pair(b)[0:RD], pair(b + 1)[0:RD]
                            if n >= 2:
                                dve.wait_ge(q_done, n - 1)
                            dve.tensor_tensor(t1[:, n % 2, :], p, cos[:], ALU.mult).then_inc(c_done, 1)
                            dve.tensor_tensor(t2[:, n % 2, :], r, sin[:], ALU.mult).then_inc(s_done, 1)

            with ExitStack() as tmp2:
                sb2 = lambda n, shape, dt=F32: core.sb(n, shape, dt, tmp2)
                idb = sb2("identity_bf16", [P, P], BF16)
                mQ, mK = sb2("mask_by_query", [P, P], BF16), sb2("mask_by_key", [P, P], BF16)
                setup = sem("masks")
                k_in, kb_in = [sem("k_in_even"), sem("k_in_odd")], [sem("kb_in_even"), sem("kb_in_odd")]
                with nc.Block() as block:
                    @block.gpsimd
                    def _(pool):
                        pool.memset(mQ[:], 0.0).then_inc(setup, 1)
                        pool.wait_ge(setup, 1)
                        pool.memset(mK[:], 0.0).then_inc(setup, 1)
                        pool.wait_ge(setup, 2)
                        pool.affine_select(out=mQ[:], in_=mQ[:], compare_op=ALU.is_ge, fill=NEG, base=0,
                                           pattern=[[-1, P]], channel_multiplier=1).then_inc(setup, 1)
                        pool.wait_ge(setup, 3)
                        pool.affine_select(out=mK[:], in_=mK[:], compare_op=ALU.is_ge, fill=NEG, base=0,
                                           pattern=[[1, P]], channel_multiplier=-1).then_inc(setup, 1)
                        pool.wait_ge(setup, 4)
                        pool.tensor_copy(idb[:], ident[:]).then_inc(setup, 1)

                class HeadKeys:

                    @staticmethod
                    def keys(sp, h):
                        sp.dma_start(K[NOPE:QROWS, h % 2, :], kT[(h % 8) * HD:(h % 8 + 1) * HD, h // 8, :]
                                     ).then_inc(k_in[h % 2], 16)

                    @staticmethod
                    def keys_bf16(sp, h):
                        sp.dma_start(Kb[NOPE:QROWS, h % 2, :], kTb[(h % 8) * HD:(h % 8 + 1) * HD, h // 8, :]
                                     ).then_inc(kb_in[h % 2], 16)

                    @staticmethod
                    def first(sp):
                        for h in range(AHEAD):
                            HeadKeys.keys_bf16(sp, h)
                        for h in range(2):
                            HeadKeys.keys(sp, h)

                    @staticmethod
                    def load(sp, h, m_ready, per_head, s_ready):
                        if h + AHEAD < HEADS:
                            sp.wait_ge(m_ready, (h + 1) * per_head)
                            HeadKeys.keys_bf16(sp, h + 2)
                        if 1 <= h < HEADS - 1:
                            sp.wait_ge(s_ready, NT * h)
                            HeadKeys.keys(sp, h + 1)

                    @staticmethod
                    def wait_max(pe, h):
                        pe.wait_ge(kb_in[h % 2], 16 * (h // 2 + 1))

                    @staticmethod
                    def wait_keys(pe, h):
                        pe.wait_ge(k_in[h % 2], 16 * (h // 2 + 1))

                attention_heads(nc, core, tag, True, V, O,
                                q_max=lambda h, a, b: Qb[:, h, a:b], k_max=lambda h, a, b: Kb[:, h % 2, a:b],
                                keys=lambda h, c: K[0:SHIFT + 1, h % 2, c * P:(c + 1) * P],
                                queries=lambda h, a, b: Q[0:SHIFT + 1, h, a:b],
                                shift_row=lambda h: Q[SHIFT:SHIFT + 1, h, :], exp_kw=lambda c: {"scale": SC},
                                shift_dt=F32, masks=(idb[:], mQ[:], mK[:]), head_loads=HeadKeys)

        project_out(nc, core, tag, O, wo, None)


def store_output(nc, core, out_dram):
    stored = core.stored
    with nc.Block() as block:
        @block.sync
        def _(sp):
            sp.dma_start(out_dram.rearrange("(t p) d -> p t d", p=P), core.X[:]).then_inc(stored, 16)
            sp.wait_ge(stored, 16)


def build(nc, a, out):
    with ExitStack() as ctx:
        core = Core(nc, ctx)
        load_inputs(nc, core, a["x"])
        if STAGES >= 1:
            norm_stage(nc, core, "n1")
            attention16(nc, core, "aa", a["a_wq"], a["a_wk"], a["a_wv"], a["a_wo"],
                        {"bqk": a["a_bqk"], "bv": a["a_bv"], "bo": a["a_bo"]},
                        {"justice": a["a_justice"], "order": a["a_order"]}, a["pos"])
            core.layer_done()
        if STAGES >= 2:
            ternary_scope = ExitStack()
            ternary = ternary_weights(nc, core, ternary_scope, a["f_up"], a["f_gate"], a["f_down"])
            norm_stage(nc, core, "n2")
            ternary_ffn(nc, core, "f0", ternary)
            core.layer_done()
        if STAGES >= 3:
            norm_stage(nc, core, "n3")
            gated_delta(nc, core, "gd", {k[2:]: a[k] for k in a if k.startswith("g_")})
            core.layer_done()
        if STAGES >= 4:
            norm_stage(nc, core, "n4")
            ternary_ffn(nc, core, "f1", ternary)
            ternary_scope.close()
            core.layer_done()
        if STAGES >= 5:
            norm_stage(nc, core, "n5")
            attention16(nc, core, "ac", a["c_wq"], a["c_wk"], a["c_wv"], a["c_wo"], {"bo": a["c_bo"]}, None, None)
            core.layer_done()
        if STAGES >= 6:
            routed_layer(nc, core, "r0", {k[2:]: a[k] for k in a if k.startswith("r_")})
            core.layer_done()
        if STAGES >= 7:
            norm_stage(nc, core, "n7")
            latent_attention(nc, core, "la", {k[2:]: a[k] for k in a if k.startswith("m_")})
            core.layer_done()
        if STAGES >= 8:
            routed_layer(nc, core, "r1", {k[2:]: a[k] for k in a if k.startswith("r_")})
        store_output(nc, core, out)


def lay_out(inputs):
    c = np.ascontiguousarray
    i = {k: np.asarray(v) for k, v in inputs.items()}
    a = {
        "x": c(i["L0_attn_a_hidden_states"][0]),
        "a_wq": c(i["L0_attn_a_Wq"].T), "a_wk": c(i["L0_attn_a_Wk"].T), "a_wv": c(i["L0_attn_a_Wv"].T),
        "a_wo": c(i["L0_attn_a_Wo"].T),
        "a_bqk": c(np.concatenate([i["L0_attn_a_bq"].reshape(KT, P).T, i["L0_attn_a_bk"].reshape(KT, P).T], axis=1)),
        "a_bv": c(i["L0_attn_a_bv"]),
        "a_bo": c(i["L0_attn_a_bo"]),
        "a_justice": c(i["L0_attn_a_justice_gate"]), "a_order": c(i["L0_attn_a_order_gate"]),
        "pos": c((np.arange(S, dtype=np.float32) / S).reshape(NT, P).T),
        "f_up": c(i["L0_ffn_W_up"].T), "f_gate": c(i["L0_ffn_W_gate"].T), "f_down": c(i["L0_ffn_W_down"].T),
    }
    cat = np.concatenate
    b = {k[len("L0_attn_b_"):]: v for k, v in i.items() if k.startswith("L0_attn_b_")}
    conv = cat([b["conv_wq"], b["conv_wk"], b["conv_wv"]], axis=0)
    a.update({
        "g_wqkv": c(cat([b["Wq"], b["Wk"], b["Wv"]], axis=1)),
        "g_wgab": c(cat([b["Wg"], b["Wa"], b["Wb"]], axis=1)),
        "g_conv": c(conv.reshape(NF, P, TAPS).transpose(1, 0, 2).reshape(P, NF * TAPS)),
        "g_wo": c(b["Wo"]), "g_nw": c(b["norm_weight"]), "g_dt": c(b["dt_bias"]), "g_alog": c(b["A_log"]),
        "g_masks": level_masks(),
        "g_own": c(np.repeat(np.repeat(np.eye(4, dtype=np.float32), GK, axis=0), GV, axis=1)),
    })
    w = i["L1_attn_a_Wqkv"].reshape(HEADS, 3, HD, D)
    a.update({
        "c_wq": c(w[:, 0].reshape(D, D).T), "c_wk": c(w[:, 1].reshape(D, D).T), "c_wv": c(w[:, 2].reshape(D, D).T),
        "c_wo": c(i["L1_attn_a_Wproj"].T), "c_bo": c(i["L1_attn_a_bproj"]),
    })
    r = {k[len("L1_ffn_"):]: v for k, v in i.items() if k.startswith("L1_ffn_")}
    a.update({
        "r_gate": c(r["gate_w"].T), "r_up": c(r["w_up"].T), "r_gt": c(r["w_gate"].T), "r_down": c(r["w_down"].T),
        "r_upA": c(r["up_A"].reshape(P, D).T), "r_gtA": c(r["gate_A"].reshape(P, D).T),
        "r_upB": c(r["up_B"].transpose(0, 2, 1).reshape(P, DH)), "r_gtB": c(r["gate_B"].transpose(0, 2, 1).reshape(P, DH)),
        "r_dnA": c(r["down_A"].reshape(P, DH).T), "r_dnB": c(r["down_B"].transpose(0, 2, 1).reshape(P, D)),
        "r_expert": c(np.broadcast_to((np.arange(P) // RANK).astype(np.float32), (P, P))),
    })
    m = {k[len("L1_attn_b_"):]: v for k, v in i.items() if k.startswith("L1_attn_b_")}
    cos, sin = rope_tables()
    a.update({
        "m_w1": c(cat([m["Wqd"], m["Wkvd"], m["Wkr"]], axis=1)),
        "m_wq": c(cat([m["Wqr"].reshape(LAT, HEADS, RD), m["Wqu"].reshape(LAT, HEADS, HD)], axis=2).reshape(LAT, -1)),
        "m_wku": c(m["Wku"]), "m_wvu": c(m["Wvu"]), "m_wo": c(m["Wo"]), "m_cos": cos, "m_sin": sin,
    })
    return a


def rope_tables():
    freqs = 1.0 / 10000.0 ** (np.arange(0, RD, 2, dtype=np.float32) / RD)
    ang = np.outer(np.arange(S, dtype=np.float32), freqs)
    return (np.ascontiguousarray(np.tile(np.cos(ang), (1, 2)).T.astype(np.float32)),
            np.ascontiguousarray(np.tile(np.sin(ang), (1, 2)).T.astype(np.float32)))


def level_masks():
    row, col = np.arange(P)[:, None], np.arange(P)[None, :]
    below = [((row >> (n + 1)) == (col >> (n + 1))) & ((row >> n) > (col >> n)) for n in range(LEVELS)]
    both = [[m.astype(np.uint32) for m in below], [m.T.astype(np.uint32) for m in below]]
    return np.ascontiguousarray(np.stack([np.stack(x) for x in both]).transpose(2, 0, 1, 3).reshape(P, -1))


def kernel(**inputs):
    import concourse.bacc as bacc
    from concourse.bass_utils import run_bass_kernel_spmd

    nc = bacc.Bacc("TRN2", target_bir_lowering=False, num_devices=1)
    arrays = lay_out(inputs)
    aps = {n: nc.dram_tensor(f"in_{n}", v.shape, mybir.dt.from_np(v.dtype), kind="ExternalInput").ap()
           for n, v in arrays.items()}
    out = nc.dram_tensor("out", (S, D), F32, kind="ExternalOutput").ap()
    build(nc, aps, out)
    r = run_bass_kernel_spmd(nc, [{f"in_{n}": v for n, v in arrays.items()}], core_ids=[0])
    return r.results[0]["out"].reshape(1, S, D)
```

```python
from contextlib import ExitStack

import numpy as np

import concourse.bass as bass
from concourse import mybir

F32 = mybir.dt.float32
BF16 = mybir.dt.bfloat16
U32 = mybir.dt.uint32
ALU = mybir.AluOpType
ACT = mybir.ActivationFunctionType
AX = mybir.AxisListType

P = 128
S = 1024
D = 256
NT = S // P
KT = D // P
HALF = 512
NH2 = S // HALF
HEADS = 16
HD = D // HEADS
LN_EPS = 1e-5


class Core:

    def __init__(self, nc, ctx):
        self.nc, self.ctx, self.n, self.sems = nc, ctx, 0, []
        self.X = self.sb("x_tokens", [P, NT, D], F32)
        self.XNT = self.sb("xn_features", [P, KT, S], F32)
        self.ident = self.sb("identity", [P, P], F32)
        self.ones = self.sb("ones_row", [1, P], F32)
        self.ones_sq = self.sb("ones_square", [P, P], F32)
        self.stats = self.sb("bn_stats", [P, NT, 6], F32)
        self.stored = nc.alloc_semaphore("stored")
        self.psum = self.ps("psum", [P, 8, HALF], F32)

    def sb(self, name, shape, dt, ctx=None):
        self.n += 1
        return (ctx or self.ctx).enter_context(self.nc.sbuf_tensor(f"{name}_{self.n}", shape, dt))

    def ps(self, name, shape, dt):
        return self.ctx.enter_context(self.nc.psum_tensor(name, shape, dt))

    def sem(self, name):
        self.n += 1
        self.sems.append(self.nc.alloc_semaphore(f"{name}_{self.n}"))
        return self.sems[-1]

    def tile_stats(self, dve, t, written):
        dve.wait_ge(written, t + 1)
        dve.bn_stats(self.stats[:, t, :], self.X[:, t, :])

    def layer_done(self):
        self.nc.clear_and_free_semaphores(self.sems)
        self.sems = []
        self.nc.all_engine_barrier()


def load_inputs(nc, core, x_dram):
    X, ident = core.X, core.ident
    x_loaded, zeroed, made = core.sem("x_loaded"), core.sem("ident_zeroed"), core.sem("consts_made")
    with nc.Block() as block:
        @block.sync
        def _(sp):
            sp.dma_start(X[:], x_dram.rearrange("(t p) d -> p t d", p=P)).then_inc(x_loaded, 16)
            sp.wait_ge(x_loaded, 16)

        @block.vector
        def _(dve):
            dve.wait_ge(x_loaded, 16)
            for t in range(NT):
                dve.bn_stats(core.stats[:, t, :], X[:, t, :])

        @block.gpsimd
        def _(pool):
            pool.memset(ident[:], 0.0).then_inc(zeroed, 1)
            pool.memset(core.ones[:], 1.0).then_inc(made, 1)
            pool.memset(core.ones_sq[:], 1.0).then_inc(made, 1)
            pool.wait_ge(zeroed, 1)
            pool.affine_select(out=ident[:], in_=ident[:], compare_op=ALU.not_equal, fill=1.0, base=0,
                               pattern=[[-1, P]], channel_multiplier=1).then_inc(made, 1)


def norm_stage(nc, core, tag, loads=None, room=None):
    X, XNT, ident, psum = core.X, core.XNT, core.ident, core.psum
    mv_done, var_done, shift_done = (core.sem(tag + n) for n in ("_mean_var", "_var_eps", "_shift"))
    std_done, rstd_done, xn_even, xn_odd = (core.sem(tag + n) for n in ("_std", "_rstd", "_xn_even", "_xn_odd"))
    turned, taken = core.sem(tag + "_transposed"), core.sem(tag + "_taken")
    with ExitStack() as tmp:
        mv = core.sb("mean_var", [P, NT, 2], F32, tmp)
        ve = core.sb("var_eps", [P, NT], F32, tmp)
        std = core.sb("std", [P, NT], F32, tmp)
        rstd = core.sb("rstd", [P, NT], F32, tmp)
        shift = core.sb("minus_mean_rstd", [P, NT], F32, tmp)
        xn = core.sb("xn", [P, NT, D], F32, tmp) if room is None else room
        with nc.Block() as block:
            if loads is not None:
                @block.sync
                def _(sp):
                    loads(sp)

            @block.vector
            def _(dve):
                for t in range(NT):
                    dve.bn_aggr(mv[:, t, :], core.stats[:, t, :]).then_inc(mv_done, 1)
                dve.wait_ge(mv_done, NT)
                dve.tensor_scalar(ve[:], mv[:, :, 1], LN_EPS, None, ALU.add).then_inc(var_done, 1)
                dve.wait_ge(std_done, 1)
                dve.reciprocal(rstd[:], std[:]).then_inc(rstd_done, 1)
                dve.wait_ge(rstd_done, 1)
                dve.scalar_tensor_tensor(shift[:], mv[:, :, 0], -1.0, rstd[:], ALU.mult, ALU.mult).then_inc(shift_done, 1)
                for t in range(0, NT, 2):
                    dve.tensor_scalar(xn[:, t, :], X[:, t, :], mv[:, t, 0:1], rstd[:, t:t + 1],
                                      ALU.subtract, ALU.mult).then_inc(xn_even, 1)
                for half in range(NH2):
                    dve.wait_ge(turned, 2 * half + 2)
                    dve.tensor_copy(XNT[:, 1, half * HALF:(half + 1) * HALF],
                                    psum[:, 2 * half + 1, :]).then_inc(taken, 1)

            @block.scalar
            def _(act):
                act.wait_ge(var_done, 1)
                act.activation(std[:], ve[:], ACT.Sqrt).then_inc(std_done, 1)
                act.wait_ge(shift_done, 1)
                for t in range(1, NT, 2):
                    act.activation(xn[:, t, :], X[:, t, :], ACT.Identity, bias=shift[:, t:t + 1],
                                   scale=rstd[:, t:t + 1]).then_inc(xn_odd, 1)
                for half in range(NH2):
                    act.wait_ge(turned, 2 * half + 1)
                    act.activation(XNT[:, 0, half * HALF:(half + 1) * HALF], psum[:, 2 * half, :],
                                   ACT.Copy).then_inc(taken, 1)

            @block.tensor
            def _(pe):
                for half in range(NH2):
                    for f in range(KT):
                        for i in range(4):
                            t = 4 * half + i
                            pe.wait_ge((xn_even, xn_odd)[t % 2], t // 2 + 1)
                            last = pe.transpose(psum[:, 2 * half + f, i * P:(i + 1) * P],
                                                xn[:, t, f * P:(f + 1) * P], ident[:])
                        last.then_inc(turned, 1)


DE = 1024
NE = DE // P
TERNARY_EPS = 1e-8


def ternary_weights(nc, core, scope, wup_d, wgate_d, wdown_d):
    scale = core.sb("ternary_scales", [P, 3], F32, scope)
    ups = core.sb("w_up_signs", [P, KT, DE], BF16, scope)
    gates = core.sb("w_gate_signs", [P, KT, DE], BF16, scope)
    downs = core.sb("w_down_signs", [P, NE, D], BF16, scope)
    flat = [ups[:].rearrange("p k n -> p (k n)"), gates[:].rearrange("p k n -> p (k n)"),
            downs[:].rearrange("p k n -> p (k n)")]
    N = KT * DE
    loaded = [core.sem(f"ternary_w{i}_loaded") for i in range(3)]
    absum, total, scaled, halves, low = (core.sem("ternary_" + n) for n in
                                         ("abs_summed", "total", "scaled", "halved", "low_side"))
    done = core.sem("ternary_signs")
    with ExitStack() as tmp:
        w = [core.sb(f"w{i}", [P, N], F32, tmp) for i in range(3)]
        b = core.sb("low_side", [P, N], F32, tmp)
        part = core.sb("abs_sums", [P, 3], F32, tmp)
        h = core.sb("half_scales", [P, 2, 3], F32, tmp)
        def loads(sp):
            for i, (d, k) in enumerate(((wup_d, KT), (wgate_d, KT), (wdown_d, NE))):
                sp.dma_start(w[i][:].rearrange("p (k n) -> p k n", k=k),
                             d.rearrange("(k p) n -> p k n", p=P)).then_inc(loaded[i], 16)

        norm_stage(nc, core, "n2", loads)
        with nc.Block() as block:
            @block.tensor
            def _(pe):
                pe.wait_ge(absum, 3)
                pe.matmul(core.psum[:, 0, 0:3], core.ones_sq[:], part[:], start=True, stop=True).then_inc(total, 1)

            @block.vector
            def _(dve):
                for i in range(3):
                    dve.wait_ge(loaded[i], 16)
                    dve.tensor_reduce(part[:, i:i + 1], w[i][:], AX.X, ALU.add,
                                      apply_absolute_value=True).then_inc(absum, 1)
                dve.wait_ge(total, 1)
                dve.tensor_scalar(scale[:], core.psum[:, 0, 0:3], 1.0 / (DE * D), TERNARY_EPS,
                                  ALU.mult, ALU.add).then_inc(scaled, 1)
                dve.wait_ge(scaled, 1)
                dve.tensor_scalar(h[:, 0, :], scale[:], 0.5, None, ALU.mult).then_inc(halves, 1)
                dve.tensor_scalar(h[:, 1, :], scale[:], -0.5, None, ALU.mult).then_inc(halves, 1)
                dve.wait_ge(halves, 2)
                for i in range(3):
                    if i:
                        dve.wait_ge(done, i)
                    dve.tensor_scalar(b[:], w[i][:], h[:, 1, i:i + 1], None, ALU.is_lt).then_inc(low, 1)
                    dve.wait_ge(low, i + 1)
                    dve.scalar_tensor_tensor(flat[i], w[i][:], h[:, 0, i:i + 1], b[:], ALU.is_gt,
                                             ALU.subtract).then_inc(done, 1)
    return scale, ups, gates, downs


def ternary_ffn(nc, core, tag, weights):
    scale, ups, gates, downs = weights
    X, XNT, psum = core.X, core.XNT, core.psum
    sem = lambda n: core.sem(tag + n)
    x_high, x_rest, x_mid, x_low = (sem("_x_" + n) for n in ("high", "rest", "middle", "low"))
    h_high, h_rest, h_mid, h_low = (sem("_h_" + n) for n in ("high", "rest", "middle", "low"))
    proj, act_done, hid, down, added = (sem(n) for n in ("_projected", "_silu", "_hidden", "_down", "_added"))
    with ExitStack() as tmp:
        XP = core.sb("xn_parts", [P, 3, KT, S], BF16, tmp)
        xr = core.sb("xn_rest", [P, KT, S], F32, tmp)
        HP = core.sb("hidden_parts", [P, 3, NE, S], BF16, tmp)
        h32 = core.sb("hidden", [P, 2, HALF], F32, tmp)
        hr = core.sb("hidden_rest", [P, 2, HALF], F32, tmp)
        sil = core.sb("silu_up", [P, 2, HALF], F32, tmp)
        cols = lambda half: slice(half * HALF, (half + 1) * HALF)
        units = [(e, half) for half in range(NH2) for e in range(NE)]
        with nc.Block() as block:
            @block.tensor
            def _(pe):
                for u, (e, half) in enumerate(units):
                    b = u % 2
                    if e == 0:
                        pe.wait_ge(x_low, KT * (half + 1))
                    if u >= 2:
                        pe.wait_ge(hid, u - 1)
                    for j, w in enumerate((ups, gates)):
                        for part in range(3):
                            for k in range(KT):
                                last = pe.matmul(psum[:, 2 * b + j, :], w[:, k, e * P:(e + 1) * P],
                                                 XP[:, part, k, cols(half)],
                                                 start=(part == 0 and k == 0), stop=(part == 2 and k == KT - 1))
                        last.then_inc(proj, 1)
                for t in range(NT):
                    pe.wait_ge(h_low, NE * (t // 4 + 1))
                    if t >= 4:
                        pe.wait_ge(added, t - 3)
                    for e in range(NE):
                        for part in range(3):
                            last = pe.matmul(psum[:, 4 + t % 4, 0:D], HP[:, part, e, t * P:(t + 1) * P], downs[:, e, :],
                                             start=(e == 0 and part == 0), stop=(e == NE - 1 and part == 2))
                    last.then_inc(down, 1)

            @block.scalar
            def _(act):
                for half in range(NH2):
                    for k in range(KT):
                        act.activation(XP[:, 0, k, cols(half)], XNT[:, k, cols(half)], ACT.Copy).then_inc(x_high, 1)
                    for k in range(KT):
                        act.wait_ge(x_rest, half * KT + k + 1)
                        act.activation(XP[:, 1, k, cols(half)], xr[:, k, cols(half)], ACT.Copy).then_inc(x_mid, 1)
                for u in range(len(units) + 2):
                    if u < len(units):
                        act.wait_ge(proj, 2 * u + 1)
                        if u >= 2:
                            act.wait_ge(hid, u - 1)
                        act.activation(sil[:, u % 2, :], psum[:, 2 * (u % 2), :], ACT.Silu,
                                       scale=scale[:, 0:1]).then_inc(act_done, 1)
                    if 1 <= u <= len(units):
                        e, half = units[u - 1]
                        act.wait_ge(hid, u)
                        act.activation(HP[:, 0, e, cols(half)], h32[:, (u - 1) % 2, :], ACT.Copy).then_inc(h_high, 1)
                    if u >= 2:
                        e, half = units[u - 2]
                        act.wait_ge(h_rest, u - 1)
                        act.activation(HP[:, 1, e, cols(half)], hr[:, u % 2, :], ACT.Copy).then_inc(h_mid, 1)

            @block.vector
            def _(dve):
                for half in range(NH2):
                    for k in range(KT):
                        dve.wait_ge(x_high, half * KT + k + 1)
                        dve.tensor_tensor(xr[:, k, cols(half)], XNT[:, k, cols(half)], XP[:, 0, k, cols(half)],
                                          ALU.subtract).then_inc(x_rest, 1)
                    for k in range(KT):
                        dve.wait_ge(x_mid, half * KT + k + 1)
                        dve.tensor_tensor(XP[:, 2, k, cols(half)], xr[:, k, cols(half)], XP[:, 1, k, cols(half)],
                                          ALU.subtract).then_inc(x_low, 1)
                for u in range(len(units) + 2):
                    if u < len(units):
                        dve.wait_ge(proj, 2 * u + 2)
                        dve.wait_ge(act_done, u + 1)
                        if u >= 2:
                            dve.wait_ge(h_high, u - 1)
                            dve.wait_ge(h_rest, u - 1)
                        dve.scalar_tensor_tensor(h32[:, u % 2, :], psum[:, 2 * (u % 2) + 1, :],
                                                 scale[:, 1:2], sil[:, u % 2, :], ALU.mult, ALU.mult).then_inc(hid, 1)
                    if 1 <= u <= len(units):
                        e, half = units[u - 1]
                        dve.wait_ge(h_high, u)
                        if u >= 3:
                            dve.wait_ge(h_low, u - 2)
                        dve.tensor_tensor(hr[:, (u - 1) % 2, :], h32[:, (u - 1) % 2, :], HP[:, 0, e, cols(half)],
                                          ALU.subtract).then_inc(h_rest, 1)
                    if u >= 2:
                        e, half = units[u - 2]
                        dve.wait_ge(h_mid, u - 1)
                        dve.tensor_tensor(HP[:, 2, e, cols(half)], hr[:, u % 2, :], HP[:, 1, e, cols(half)],
                                          ALU.subtract).then_inc(h_low, 1)
                for t in range(NT):
                    dve.wait_ge(down, t + 1)
                    dve.scalar_tensor_tensor(X[:, t, :], psum[:, 4 + t % 4, 0:D], scale[:, 2:3], X[:, t, :],
                                             ALU.mult, ALU.add).then_inc(added, 1)
                    core.tile_stats(dve, t, added)


VW = 32
AHEAD = 2


def attention_heads(nc, core, tag, causal, V, O, q_max, k_max, keys, queries, shift_row, exp_kw,
                    shift_dt, masks=None, head_loads=None):
    psum, ident = core.psum, core.ident
    sem = lambda n: core.sem(f"{tag}_{n}")
    PB = 4
    SB, MB, PVB, TB = 0, 4, 6, 7
    end = lambda qt: (qt + 1) * P if causal else S
    pieces = lambda qt: [(a, min(a + HALF, end(qt))) for a in range(0, end(qt), HALF)]
    count = [len(pieces(qt)) for qt in range(NT)]
    per_head = sum(count)
    start = [sum(count[:qt]) for qt in range(NT)]
    q_from = lambda c: c * P if causal else 0
    with ExitStack() as tmp:
        sb = lambda n, shape, dt=F32: core.sb(n, shape, dt, tmp)
        mx = sb("row_max_pieces", [P, 2, NT, NH2])
        nm = sb("minus_max", [P, 2, NT])
        nmT = sb("minus_max_rows", [NT, 2, P], shift_dt)
        pr = sb("probs", [P, PB, S])
        oT = sb("out_features", [P, 2, D])
        rc = sb("reciprocals", [P, 2, 2, 4])
        m_ready, m_piece, m_done = sem("max_scores"), sem("max_pieces"), sem("minus_max")
        mt_ready, mt_done, shift_in = sem("max_transposed"), sem("max_row"), sem("shift_row")
        s_ready, e_done, pv_ready = sem("scores"), sem("exp"), sem("values_summed")
        o_kept, o_turned, r_done, o_done = sem("out_kept"), sem("out_transposed"), sem("recip"), sem("out_done")
        with nc.Block() as block:
            @block.tensor
            def _(pe):
                def max_scores(h, qt):
                    if qt == 0 and head_loads:
                        head_loads.wait_max(pe, h)
                    for i, (a, b) in enumerate(pieces(qt)):
                        n = h * per_head + start[qt] + i
                        if n >= 2:
                            pe.wait_ge(m_piece, n - 1)
                        own = causal and i == count[qt] - 1
                        last = pe.matmul(psum[:, MB + n % 2, 0:b - a], q_max(h, qt * P, (qt + 1) * P), k_max(h, a, b),
                                         start=True, stop=not own)
                        if own:
                            last = pe.matmul(psum[:, MB + n % 2, b - a - P:b - a], masks[0], masks[1],
                                             start=False, stop=True)
                        last.then_inc(m_ready, 1)

                def turn_max(h):
                    pe.wait_ge(m_done, h + 1)
                    if h >= 1:
                        pe.wait_ge(mt_done, h)
                    if h >= 3:
                        pe.wait_ge(o_done, h - 2)
                    pe.transpose(psum[0:NT, TB, 2 * P:3 * P], nm[:, h % 2, :], ident[:]).then_inc(mt_ready, 1)

                def key_scores(h, c):
                    n = h * NT + c
                    if c == 0:
                        pe.wait_ge(shift_in, 16 * (h + 1))
                        if head_loads:
                            head_loads.wait_keys(pe, h)
                    if n >= 2:
                        pe.wait_ge(e_done, n - 1)
                    for half in range(q_from(c) // HALF, NH2):
                        a = max(q_from(c), half * HALF)
                        o = psum[:, SB + 2 * (n % 2) + half, a - half * HALF:]
                        own = causal and a == q_from(c)
                        last = pe.matmul(o, keys(h, c), queries(h, a, (half + 1) * HALF), start=True, stop=not own)
                        if own:
                            last = pe.matmul(o[:, 0:P], masks[0], masks[2], start=False, stop=True)
                    last.then_inc(s_ready, 1)

                def values(n):
                    h, c = n // NT, n % NT
                    pe.wait_ge(e_done, n + 1)
                    if c == 0 and h >= 1:
                        pe.wait_ge(o_kept, h)
                    for g in range(q_from(c) // D, 4):
                        a = max(q_from(c), g * D)
                        last = pe.matmul(psum[32 * g:32 * g + VW, PVB, a - g * D:D], V[:, c, h, :],
                                         pr[:, n % PB, a:(g + 1) * D], start=(c == 0),
                                         stop=(c == (2 * g + 1 if causal else NT - 1)))
                    last.then_inc(pv_ready, 1)

                def turn_out(h):
                    pe.wait_ge(o_kept, h + 1)
                    if h >= 1:
                        pe.wait_ge(o_done, h)
                    pe.wait_ge(mt_done, min(h + 3, HEADS))
                    for b in range(2):
                        last = pe.transpose(psum[:, TB, b * P:(b + 1) * P], oT[:, h % 2, b * P:(b + 1) * P], ident[:])
                    last.then_inc(o_turned, 1)

                for h in range(AHEAD):
                    for qt in range(NT):
                        max_scores(h, qt)
                        if h == 1 and qt == 2:
                            turn_max(0)
                for h in range(HEADS):
                    for c in range(NT):
                        n = h * NT + c
                        key_scores(h, c)
                        if h + AHEAD < HEADS:
                            max_scores(h + AHEAD, c)
                        if c == 2 and h + 1 < HEADS:
                            turn_max(h + 1)
                        if c == 4 and h >= 1:
                            turn_out(h - 1)
                        if n >= 1:
                            values(n - 1)
                values(HEADS * NT - 1)
                turn_out(HEADS - 1)

            @block.vector
            def _(dve):
                def row_max(h, qt):
                    for i, (a, b) in enumerate(pieces(qt)):
                        n = h * per_head + start[qt] + i
                        dve.wait_ge(m_ready, n + 1)
                        dve.reduce_max(mx[:, h % 2, qt, i:i + 1], psum[:, MB + n % 2, 0:b - a], AX.X
                                       ).then_inc(m_piece, 1)

                def minus_max(h):
                    dve.wait_ge(m_piece, (h + 1) * per_head)
                    if h >= 2:
                        dve.wait_ge(mt_ready, h - 1)
                    dve.tensor_reduce(nm[:, h % 2, :], mx[:, h % 2, :, :], AX.X, ALU.max, negate=True).then_inc(m_done, 1)

                def finish(h):
                    dve.wait_ge(o_turned, h + 1)
                    t4 = psum[:, TB, 0:D].rearrange("p (b g d) -> p b g d", b=2, g=4)
                    dve.reciprocal(rc[:, h % 2, :, :], t4[:, :, :, HD]).then_inc(r_done, 1)
                    dve.wait_ge(r_done, h + 1)
                    for b in range(2):
                        last = dve.tensor_tensor(
                            O[:].rearrange("p (g b) n -> p b g n", b=2)[:, b, :, h * HD:(h + 1) * HD],
                            t4[:, b, :, 0:HD], rc[:, h % 2, b, :].unsqueeze(2).broadcast_to([P, 4, HD]), ALU.mult)
                    last.then_inc(o_done, 1)

                if causal:
                    for b in range(2):
                        dve.memset(mx[:, b, 0:NT // 2, 1:2], -3e38)
                for h in range(AHEAD):
                    for qt in range(NT):
                        row_max(h, qt)
                    minus_max(h)
                for h in range(HEADS):
                    for c in range(NT):
                        if h + AHEAD < HEADS:
                            row_max(h + AHEAD, c)
                        if c == 4 and h >= 1:
                            finish(h - 1)
                    if h + AHEAD < HEADS:
                        minus_max(h + AHEAD)
                finish(HEADS - 1)

            @block.sync
            def _(sp):
                if head_loads:
                    head_loads.first(sp)
                for h in range(HEADS):
                    sp.wait_ge(mt_done, h + 1)
                    sp.dma_start(shift_row(h).rearrange("a (t p) -> a t p", t=NT), nmT[:, h % 2, :]).then_inc(shift_in, 16)
                    if head_loads:
                        head_loads.load(sp, h, m_ready, per_head, s_ready)

            @block.scalar
            def _(act):
                def keep_out(h):
                    act.wait_ge(pv_ready, (h + 1) * NT)
                    if h >= 2:
                        act.wait_ge(o_turned, h - 1)
                    act.activation(oT[:, h % 2, :], psum[:, PVB, 0:D], ACT.Copy).then_inc(o_kept, 1)

                def max_row(h):
                    act.wait_ge(mt_ready, h + 1)
                    if h >= 2:
                        act.wait_ge(shift_in, 16 * (h - 1))
                    act.activation(nmT[:, h % 2, :], psum[0:NT, TB, 2 * P:3 * P], ACT.Copy).then_inc(mt_done, 1)

                max_row(0)
                for h in range(HEADS):
                    for c in range(NT):
                        n = h * NT + c
                        act.wait_ge(s_ready, n + 1)
                        if n >= PB:
                            act.wait_ge(pv_ready, n - PB + 1)
                        act.activation(pr[:, n % PB, q_from(c):],
                                       psum[:, SB + 2 * (n % 2):SB + 2 * (n % 2) + 2, :].rearrange("p a n -> p (a n)")[:, q_from(c):],
                                       ACT.Exp, **exp_kw(c)).then_inc(e_done, 1)
                        if c == 0 and h >= 1:
                            keep_out(h - 1)
                        if c == 2 and h + 1 < HEADS:
                            max_row(h + 1)
                keep_out(HEADS - 1)


PARTS = 6
K_PARTS = (0, 1, 2, 0, 1, 0)
Q_PARTS = (0, 0, 0, 1, 1, 2)
SHIFT_ROW = PARTS * HD
KROWS = SHIFT_ROW + 1


def attention16(nc, core, tag, wq_d, wk_d, wv_d, wo_d, biases, gates, pos_d):
    X, XNT, psum, ident = core.X, core.XNT, core.psum, core.ident
    sem = lambda n: core.sem(f"{tag}_{n}")
    scratch = nc.dram_tensor(f"{tag}_parts", (4, 3, P, S), BF16, kind="Internal").ap()
    with ExitStack() as tmp:
        sb = lambda n, shape, dt=F32: core.sb(n, shape, dt, tmp)
        KS = sb("k_stack", [P, HEADS, S], BF16)
        QS = sb("q_stack", [P, HEADS, S], BF16)
        V = sb("v_ones", [P, NT, HEADS, VW])
        O = sb("attended", [P, NT, D])
        wo = sb("wo", [P, KT, D])
        bo = sb("bo", [1, D])
        esc = sb("exp_scale", [P, 1])
        ebias = sb("exp_bias", [P, NT])
        with ExitStack() as tmp2:
            sb2 = lambda n, shape, dt=F32: core.sb(n, shape, dt, tmp2)
            wq, wk, wv = sb2("wq", [P, KT, D]), sb2("wk", [P, KT, D]), sb2("wv", [P, KT, D])
            bqk = sb2("bias_qk", [P, 2, KT])
            bv = sb2("bias_v", [1, D])
            g3 = sb2("gates", [P, 2])
            pos = sb2("positions", [P, NT])
            full = sb2("qk_full", [P, 2, S])
            parts = sb2("qk_parts", [P, 4, 3, S], BF16)
            rest = sb2("qk_rest", [P, 2, S])
            loaded, made = sem("loaded"), sem("ones_made")
            qk_ready, full_done = sem("qk_projected"), sem("qk_full")
            hi, r1, mid, lo = (sem(n) for n in ("high", "rest", "middle", "low"))
            stacked = [sem("stacked_first_half"), sem("stacked_second_half")]
            written = [sem(f"parts_written_{u}") for u in range(4)]
            ORDER = (0, 2, 1, 3)
            v_ready, v_done, zeroed = sem("v_projected"), sem("v_kept"), sem("v_zeroed")
            esc_done = sem("exp_scale")
            def loads(sp):
                for w, w_d in ((wq, wq_d), (wk, wk_d), (wv, wv_d), (wo, wo_d)):
                    sp.dma_start(w[:], w_d.rearrange("(k p) n -> p k n", p=P)).then_inc(loaded, 16)
                sp.dma_start(bo[:], biases["bo"].rearrange("(a n) -> a n", a=1)).then_inc(loaded, 16)
                if gates is not None:
                    sp.dma_start(bqk[:].rearrange("p w k -> p (w k)"), biases["bqk"]).then_inc(loaded, 16)
                    sp.dma_start(bv[:], biases["bv"].rearrange("(a n) -> a n", a=1)).then_inc(loaded, 16)
                    for i, name in enumerate(("justice", "order")):
                        sp.dma_start(g3[:, i:i + 1], gates[name].rearrange("(a n) -> a n", a=1).broadcast_to([P, 1])
                                     ).then_inc(loaded, 16)
                    sp.dma_start(pos[:], pos_d).then_inc(loaded, 16)

            norm_stage(nc, core, tag + "n", loads)
            with nc.Block() as block:
                @block.sync
                def _(sp):
                    for n, u in enumerate(ORDER):
                        which, f = u // 2, u % 2
                        for part, ready in enumerate((hi, mid, lo)):
                            sp.wait_ge(ready, n + 1)
                            sp.dma_start(scratch[u, part], parts[:, u, part, :]).then_inc(written[u], 16)
                        if n % 2:
                            for uu in ORDER[n - 1:n + 1]:
                                sp.wait_ge(written[uu], 16 * 3)
                                w_, f_ = uu // 2, uu % 2
                                for j, part in enumerate((Q_PARTS, K_PARTS)[w_]):
                                    sp.dma_start((QS, KS)[w_][j * HD:(j + 1) * HD, 8 * f_:8 * f_ + 8, :],
                                                 scratch[uu, part].rearrange("(h d) t -> d h t", d=HD)
                                                 ).then_inc(stacked[f_], 16)

                nload = 5 + (5 if gates is not None else 0)

                @block.tensor
                def _(pe):
                    pe.wait_ge(loaded, 16 * nload)
                    for n, u in enumerate(ORDER):
                        which, f = u // 2, u % 2
                        w = (wq, wk)[which]
                        for half in range(NH2):
                            if n >= 2:
                                pe.wait_ge(full_done, 2 * (n - 2) + half + 1)
                            for k in range(KT):
                                last = pe.matmul(psum[:, 2 * (n % 2) + half, :], w[:, k, f * P:(f + 1) * P],
                                                 XNT[:, k, half * HALF:(half + 1) * HALF],
                                                 start=(k == 0), stop=(k == KT - 1))
                            last.then_inc(qk_ready, 1)
                    for t in range(NT):
                        if t >= 2:
                            pe.wait_ge(v_done, t - 1)
                        for k in range(KT):
                            last = pe.matmul(psum[:, 4 + t % 2, 0:D], XNT[:, k, t * P:(t + 1) * P], wv[:, k, :],
                                             start=(k == 0), stop=(k == KT - 1 and gates is None))
                        if gates is not None:
                            last = pe.matmul(psum[:, 4 + t % 2, 0:D], core.ones[:], bv[:], start=False, stop=True)
                        last.then_inc(v_ready, 1)

                @block.scalar
                def _(act):
                    if gates is not None:
                        act.wait_ge(loaded, 16 * nload)
                        act.activation(g3[:], g3[:], ACT.Sigmoid).then_inc(esc_done, 1)
                    for n, u in enumerate(ORDER):
                        which, f = u // 2, u % 2
                        for half in range(NH2):
                            act.wait_ge(qk_ready, 2 * n + half + 1)
                            if n >= 2:
                                act.wait_ge(r1, n - 1)
                                act.wait_ge(hi, n - 1)
                            act.activation(full[:, n % 2, half * HALF:(half + 1) * HALF],
                                           psum[:, 2 * (n % 2) + half, :], ACT.Identity,
                                           bias=bqk[:, which, f:f + 1] if gates is not None else 0.0
                                           ).then_inc(full_done, 1)
                        act.wait_ge(full_done, 2 * n + 2)
                        act.activation(parts[:, u, 0, :], full[:, n % 2, :], ACT.Copy).then_inc(hi, 1)
                        act.wait_ge(r1, n + 1)
                        act.activation(parts[:, u, 1, :], rest[:, n % 2, :], ACT.Copy).then_inc(mid, 1)

                @block.vector
                def _(dve):
                    if gates is not None:
                        dve.wait_ge(esc_done, 1)
                        dve.tensor_scalar(esc[:], g3[:, 0:1], -0.1 / HD ** 0.5, 1.0 / HD ** 0.5,
                                          ALU.mult, ALU.add).then_inc(esc_done, 1)
                        dve.tensor_scalar(ebias[:], pos[:], g3[:, 1:2], 0.05, ALU.mult, ALU.mult).then_inc(esc_done, 1)
                    else:
                        dve.memset(esc[:], 1.0 / HD ** 0.5).then_inc(esc_done, 1)
                        dve.memset(ebias[:], 0.0).then_inc(esc_done, 1)
                    for n, u in enumerate(ORDER):
                        dve.wait_ge(hi, n + 1)
                        if n >= 2:
                            dve.wait_ge(lo, n - 1)
                            dve.wait_ge(mid, n - 1)
                        dve.tensor_tensor(rest[:, n % 2, :], full[:, n % 2, :], parts[:, u, 0, :],
                                          ALU.subtract).then_inc(r1, 1)
                        dve.wait_ge(mid, n + 1)
                        dve.tensor_tensor(parts[:, u, 2, :], rest[:, n % 2, :], parts[:, u, 1, :],
                                          ALU.subtract).then_inc(lo, 1)
                    dve.wait_ge(zeroed, 3)
                    for t in range(NT):
                        dve.wait_ge(v_ready, t + 1)
                        dve.tensor_copy(V[:, t, :, 0:HD],
                                        psum[:, 4 + t % 2, 0:D].rearrange("p (h d) -> p h d", d=HD)).then_inc(v_done, 1)

                @block.gpsimd
                def _(pool):
                    pool.memset(V[:], 0.0).then_inc(zeroed, 1)
                    pool.wait_ge(zeroed, 1)
                    pool.memset(V[:, :, :, HD:HD + 1], 1.0).then_inc(zeroed, 1)
                    pool.wait_ge(zeroed, 2)
                    pool.memset(KS[SHIFT_ROW:KROWS, :, :], 1.0).then_inc(zeroed, 1)

        class Stacks:
            wait_keys = first = load = staticmethod(lambda *x: None)

            @staticmethod
            def wait_max(pe, h):
                if h % (HEADS // 2) == 0:
                    pe.wait_ge(stacked[h // (HEADS // 2)], 16 * 2 * PARTS)

        attention_heads(nc, core, tag, False, V, O,
                        q_max=lambda h, a, b: QS[0:SHIFT_ROW, h, a:b], k_max=lambda h, a, b: KS[0:SHIFT_ROW, h, a:b],
                        keys=lambda h, c: KS[0:KROWS, h, c * P:(c + 1) * P],
                        queries=lambda h, a, b: QS[0:KROWS, h, a:b], shift_row=lambda h: QS[SHIFT_ROW:KROWS, h, :],
                        exp_kw=lambda c: {"bias": ebias[:, c:c + 1], "scale": esc[:]}, shift_dt=BF16,
                        head_loads=Stacks)
        project_out(nc, core, tag, O, wo, bo)


def project_out(nc, core, tag, O, wo, bo, tiles=KT, OT=None):
    X, psum, ident = core.X, core.psum, core.ident
    turned, kept, ready, added = (core.sem(f"{tag}_{n}") for n in ("o_turned", "o_features", "proj", "added"))
    with ExitStack() as tmp:
        OT = core.sb("attended_features", [P, tiles, S], F32, tmp) if OT is None else OT
        with nc.Block() as block:
            @block.tensor
            def _(pe):
                for n in range(NH2 * tiles):
                    half, f = n // tiles, n % tiles
                    if n >= 4:
                        pe.wait_ge(kept, n - 3)
                    for i in range(4):
                        t = 4 * half + i
                        last = pe.transpose(psum[:, n % 4, i * P:(i + 1) * P], O[:, t, f * P:(f + 1) * P], ident[:])
                    last.then_inc(turned, 1)
                for t in range(NT):
                    pe.wait_ge(kept, tiles * (t // 4 + 1))
                    if t >= 4:
                        pe.wait_ge(added, t - 3)
                    for k in range(tiles):
                        last = pe.matmul(psum[:, 4 + t % 4, 0:D], OT[:, k, t * P:(t + 1) * P], wo[:, k, :],
                                         start=(k == 0), stop=(k == tiles - 1 and bo is None))
                    if bo is not None:
                        last = pe.matmul(psum[:, 4 + t % 4, 0:D], core.ones[:], bo[:], start=False, stop=True)
                    last.then_inc(ready, 1)

            @block.scalar
            def _(act):
                for n in range(NH2 * tiles):
                    half, f = n // tiles, n % tiles
                    act.wait_ge(turned, n + 1)
                    act.activation(OT[:, f, half * HALF:(half + 1) * HALF], psum[:, n % 4, :],
                                   ACT.Copy).then_inc(kept, 1)

            @block.vector
            def _(dve):
                for t in range(NT):
                    dve.wait_ge(ready, t + 1)
                    dve.tensor_tensor(X[:, t, :], psum[:, 4 + t % 4, 0:D], X[:, t, :], ALU.add).then_inc(added, 1)
                    core.tile_stats(dve, t, added)



GH, GK, GV = 6, 32, 64
QKW, VWD = GH * GK, GH * GV
FW = 2 * QKW + VWD
NF = FW // P
TAPS = 4
T32 = 32
NG = 2
GCH = GH * (S // P) // NG
NBT = 4
CB = GH * (S // P) // NBT
RMS_EPS = 1e-5


def gated_delta(nc, core, tag, d):
    X, XNT, psum, ident = core.X, core.XNT, core.psum, core.ident
    sem = lambda n: core.sem(f"{tag}_{n}")
    with ExitStack() as tmp:
        sb = lambda n, shape, dt=F32: core.sb(n, shape, dt, tmp)
        SG = sb("silu_gate", [P, NT, VWD])
        KBE = sb("k_beta_eg", [P, NT, GH, GK])
        KD = sb("k_decayed", [P, NT, GH, GK])
        BV = sb("beta_v", [P, NT, GH, GV])
        ETH = sb("exp_total_by_row", [P, 2, NT])
        G = sb("g_sums", [P, NT, GH])
        g = sb("g", [P, NT, GH])
        wo = sb("delta_wo", [P, 3, D])
        nw = sb("norm_weight", [P, GV])
        tri = sb("upper_ones", [P, P])
        QET = sb("qe_features", [P, 2, S])
        wload = sem("wo_loaded")
        with ExitStack() as mid_scope:
            sbm = lambda n, shape, dt=F32: core.sb(n, shape, dt, mid_scope)
            PT = sbm("p_by_key", [P, GH * NT, P])
            EA = sbm("e_then_minus_a", [P, GH * NT, P])
            BLOCKS = 4 * GCH
            MA = sbm("minus_a_blocks", [BLOCKS, NG, T32, T32])
            TB = sbm("t_blocks", [BLOCKS, NG, T32, T32])
            outer = sbm("outer_products", [BLOCKS, NG, (T32 // 2) ** 2])
            a_scratch = nc.dram_tensor("gd_a_blocks", (NG, 4, GCH, T32, T32), F32, kind="Internal").ap()
            t_scratch = nc.dram_tensor("gd_t_blocks", (NG, 2, 4, GCH, T32, T32), F32, kind="Internal").ap()
            group = lambda q: slice(q * T32, (q + 1) * T32)
            chunks_of = lambda n: slice(n * GCH, (n + 1) * GCH)
            a_written = [sem(f"a_blocks_written_{n}") for n in range(NG)]
            a_loaded = [sem(f"a_blocks_loaded_{n}") for n in range(NG)]
            t_written = [sem(f"t_blocks_written_{n}") for n in range(NG)]
            t_eye, swept = sem("t_set_to_identity"), [sem(f"swept_{n}") for n in range(NG)]

            EARLY = 18

            def substitute(eng, n, first, end):
                step = swept[n]
                eng.wait_ge(t_eye, 16 * NG)
                eng.wait_ge(a_loaded[n], 16)
                for i in range(first, min(end, T32 - 1)):
                    rows, cols = T32 - 1 - i, i + 1
                    prod = outer[:, n, 0:rows * cols].rearrange("p (t j) -> p t j", j=cols)
                    if i:
                        eng.wait_ge(step, 2 * i)
                    eng.tensor_tensor(prod, MA[:, n, i, i + 1:].unsqueeze(2).broadcast_to([BLOCKS, rows, cols]),
                                      TB[:, n, i, 0:cols].unsqueeze(1).broadcast_to([BLOCKS, rows, cols]),
                                      ALU.mult).then_inc(step, 1)
                    eng.wait_ge(step, 2 * i + 1)
                    eng.tensor_tensor(TB[:, n, i + 1:, 0:cols], TB[:, n, i + 1:, 0:cols], prod,
                                      ALU.add).then_inc(step, 1)
                if end == T32:
                    eng.wait_ge(step, 2 * (T32 - 1))
                    eng.tensor_copy(MA[:, n], TB[:, n].rearrange("p t j -> p j t")).then_inc(step, 1)

            def load_a_blocks(sp, n):
                for q in range(4):
                    sp.dma_start(a_scratch[n, q].rearrange("c j t -> j c t"), EA[group(q), chunks_of(n), group(q)]
                                 ).then_inc(a_written[n], 16)
                sp.wait_ge(a_written[n], 64)
                sp.dma_start(MA[:, n].rearrange("p j t -> p (j t)"), a_scratch[n].rearrange("q c j t -> (q c) (j t)")
                             ).then_inc(a_loaded[n], 16)

            def store_t_blocks(sp, n):
                sp.wait_ge(swept[n], 2 * T32 - 1)
                for i, o in enumerate((MA, TB)):
                    sp.dma_start(t_scratch[n, i].rearrange("q c j t -> (q c) (j t)"),
                                 o[:, n].rearrange("p j t -> p (j t)")).then_inc(t_written[n], 16)

            norm_scope = ExitStack()
            sbn = lambda n, shape, dt=F32: core.sb(n, shape, dt, norm_scope)
            KN, KB = sbn("k_normed", [P, NT, GH, GK]), sbn("k_beta", [P, NT, GH, GK])
            QN, QE = sbn("q_normed", [P, NT, GH, GK]), sbn("q_eg", [P, NT, GH, GK])
            with ExitStack() as tmp2:
                sb2 = lambda n, shape, dt=F32: core.sb(n, shape, dt, tmp2)
                YT = sb2("conv_tokens", [P, NT, FW])
                AB = sb2("ab", [P, NT, 2 * GH])
                dtb, alog = sb2("dt_bias", [P, GH]), sb2("a_log", [P, GH])
                head_loads = sem("dt_alog_loaded")
                with ExitStack() as tmp3:
                    sb3 = lambda n, shape, dt=F32: core.sb(n, shape, dt, tmp3)
                    flat = EA[:].rearrange("p c n -> p (c n)")
                    GW = VWD + 2 * GH
                    wqkv = flat[:, 0:KT * FW].rearrange("p (k n) -> p k n", k=KT)
                    wgab = flat[:, KT * FW:KT * (FW + GW)].rearrange("p (k n) -> p k n", k=KT)
                    cw = sb3("conv_w", [P, NF, TAPS])
                    Y = PT[:].rearrange("p (f a) n -> p f (a n)", f=NF)
                    loaded, proj, tapped, conv = sem("w_loaded"), sem("proj"), sem("tap"), sem("conv")
                    silu, turned, kept = sem("silu"), sem("turned"), sem("kept")
                    gate_in, gate_out, ab_out = sem("gate_in"), sem("gate_out"), sem("ab_out")
                    tri_made = sem("tri")

                    def loads(sp):
                        for k in range(KT):
                            sp.dma_start(wqkv[:, k, :], d["wqkv"][k * P:(k + 1) * P, :]).then_inc(loaded, 16)
                            sp.dma_start(wgab[:, k, :], d["wgab"][k * P:(k + 1) * P, :]).then_inc(loaded, 16)
                        sp.dma_start(cw[:].rearrange("p f t -> p (f t)"), d["conv"]).then_inc(loaded, 16)
                        sp.dma_start(wo[:], d["wo"].rearrange("(k p) n -> p k n", p=P)).then_inc(wload, 16)
                        sp.dma_start(nw[:], d["nw"].rearrange("(a n) -> a n", a=1).broadcast_to([P, GV])
                                     ).then_inc(wload, 16)
                        sp.dma_start(dtb[:], d["dt"].rearrange("(a n) -> a n", a=1).broadcast_to([P, GH])
                                     ).then_inc(head_loads, 16)
                        sp.dma_start(alog[:], d["alog"].rearrange("(a n) -> a n", a=1).broadcast_to([P, GH])
                                     ).then_inc(head_loads, 16)

                    norm_stage(nc, core, tag + "n", loads, room=BV[:].rearrange("p t h c -> p (t h c)")[:, 0:NT * D]
                               .rearrange("p (t n) -> p t n", t=NT))
                    with nc.Block() as block:
                        @block.sync
                        def _(sp):
                            sp.wait_ge(wload, 32)
                            sp.wait_ge(head_loads, 32)

                        @block.gpsimd
                        def _(pool):
                            pool.affine_select(out=tri[:], in_=core.ones_sq[:], compare_op=ALU.is_ge, fill=0.0,
                                               base=0, pattern=[[1, P]], channel_multiplier=-1).then_inc(tri_made, 1)

                        @block.tensor
                        def _(pe):
                            pe.wait_ge(loaded, 16 * 5)

                            def project(f):
                                if f >= 2:
                                    pe.wait_ge(conv, TAPS - 1 + (TAPS - 1) * (f - 2))
                                for half in range(NH2):
                                    for k in range(KT):
                                        last = pe.matmul(psum[:, 2 * (f % 2) + half, :],
                                                         wqkv[:, k, f * P:(f + 1) * P],
                                                         XNT[:, k, half * HALF:(half + 1) * HALF],
                                                         start=(k == 0), stop=(k == KT - 1))
                                last.then_inc(proj, 1)

                            def turn(f):
                                pe.wait_ge(silu, f + 1)
                                for half in range(NH2):
                                    n = 2 * f + half
                                    if n >= 2:
                                        pe.wait_ge(kept, n - 1)
                                    for i in range(4):
                                        t = 4 * half + i
                                        last = pe.transpose(psum[:, 4 + n % 2, i * P:(i + 1) * P],
                                                            Y[:, f, t * P:(t + 1) * P], ident[:])
                                    last.then_inc(turned, 1)

                            def gates(t):
                                if t >= 2:
                                    pe.wait_ge(gate_out, t - 1)
                                    pe.wait_ge(ab_out, t - 1)
                                for k in range(KT):
                                    last = pe.matmul(psum[:, 6 + t % 2, 0:VWD + 2 * GH], XNT[:, k, t * P:(t + 1) * P],
                                                     wgab[:, k, :], start=(k == 0), stop=(k == KT - 1))
                                last.then_inc(gate_in, 1)

                            for f in range(NF + 1):
                                if f < NF:
                                    project(f)
                                if f >= 1:
                                    turn(f - 1)
                                gates(f)
                            for t in range(NF + 1, NT):
                                gates(t)

                        @block.scalar
                        def _(act):
                            def gate(t):
                                act.wait_ge(gate_in, t + 1)
                                act.activation(SG[:, t, :], psum[:, 6 + t % 2, 0:VWD], ACT.Silu).then_inc(gate_out, 1)

                            act.wait_ge(loaded, 16 * 5)
                            for f in range(NF + 1):
                                if f < NF:
                                    act.wait_ge(proj, f + 1)
                                    act.activation(Y[:, f, :], psum[:, 2 * (f % 2):2 * (f % 2) + 2, :
                                                                    ].rearrange("p a n -> p (a n)"),
                                                   ACT.Copy, scale=cw[:, f, TAPS - 1:TAPS]).then_inc(tapped, 1)
                                if f >= 1:
                                    act.wait_ge(conv, (TAPS - 1) * f)
                                    act.activation(Y[:, f - 1, :], Y[:, f - 1, :], ACT.Silu).then_inc(silu, 1)
                                    for half in range(NH2):
                                        n = 2 * (f - 1) + half
                                        act.wait_ge(turned, n + 1)
                                        act.activation(YT[:, 4 * half:4 * half + 4, (f - 1) * P:f * P],
                                                       psum[:, 4 + n % 2, :].rearrange("p (t n) -> p t n", t=4),
                                                       ACT.Copy).then_inc(kept, 1)
                                gate(f)
                            for t in range(NF + 1, NT):
                                gate(t)

                        @block.vector
                        def _(dve):
                            def keep_ab(t):
                                dve.wait_ge(gate_in, t + 1)
                                dve.wait_ge(gate_out, t + 1)
                                dve.tensor_copy(AB[:, t, :], psum[:, 6 + t % 2, VWD:VWD + 2 * GH]).then_inc(ab_out, 1)

                            for f in range(NF):
                                dve.wait_ge(tapped, f + 1)
                                src = psum[:, 2 * (f % 2):2 * (f % 2) + 2, :].rearrange("p a n -> p (a n)")
                                for i in range(1, TAPS):
                                    if i > 1:
                                        dve.wait_ge(conv, (TAPS - 1) * f + i - 1)
                                    dve.scalar_tensor_tensor(Y[:, f, i:], src[:, 0:S - i],
                                                             cw[:, f, TAPS - 1 - i:TAPS - i], Y[:, f, i:],
                                                             ALU.mult, ALU.add).then_inc(conv, 1)
                                if f >= 1:
                                    keep_ab(f - 1)
                            for t in range(NF - 1, NT):
                                keep_ab(t)

                with ExitStack() as tmp3:
                    sb3 = lambda n, shape, dt=F32: core.sb(n, shape, dt, tmp3)
                    x, ax, e, u, lnu, du, one = (sb3(n, [P, NT, GH]) for n in
                                                 ("a_in", "a_abs", "e_neg", "e_plus_1", "ln", "u_minus_1", "is_one"))
                    eb, beta = sb3("exp_minus_b", [P, NT, GH]), sb3("beta", [P, NT, GH])
                    ea = sb3("exp_a_log", [P, GH])
                    eG, eT, eD, dd = (sb3(n, [P, NT, GH]) for n in ("exp_G", "exp_total", "exp_rest", "rest"))
                    sq = PT[:].rearrange("p c n -> p (c n)")[:, 0:NT * 2 * QKW].rearrange("p (t n) -> p t n", t=NT)
                    ss, r = sb3("square_sums", [P, NT, 2 * GH]), sb3("inverse_norms", [P, NT, 2 * GH])
                    fk = EA[:].rearrange("p c n -> p (c n)")[:, 0:5 * NT * GH].rearrange("p (a t h) -> p a t h", a=5, t=NT)
                    ch, aux, from_act, from_pe = sem("chain"), sem("to_act"), sem("from_act"), sem("from_pe")
                    to_pe, sq_done = sem("to_pe"), sem("sq_done")
                    with nc.Block() as block:
                        @block.tensor
                        def _(pe):
                            pe.wait_ge(to_pe, 1)
                            gf = g[:].rearrange("p t h -> p (t h)")
                            pe.matmul(psum[:, 0, 0:NT * GH], tri[:], gf, start=True, stop=True).then_inc(from_pe, 1)
                            pe.matmul(psum[:, 1, 0:NT * GH], core.ones_sq[:], gf, start=True, stop=True).then_inc(from_pe, 1)

                        @block.scalar
                        def _(act):
                            act.activation(ea[:], alog[:], ACT.Exp).then_inc(from_act, 1)
                            act.activation(eb[:], AB[:, :, GH:], ACT.Exp, scale=-1.0).then_inc(from_act, 1)
                            act.wait_ge(aux, 1)
                            act.activation(e[:], ax[:], ACT.Exp, scale=-1.0).then_inc(from_act, 1)
                            act.wait_ge(aux, 2)
                            act.activation(lnu[:], u[:], ACT.Ln).then_inc(from_act, 1)
                            act.wait_ge(aux, 3)
                            act.activation(eG[:], G[:], ACT.Exp).then_inc(from_act, 1)
                            act.activation(eT[:], psum[:, 1, 0:NT * GH].rearrange("p (t h) -> p t h", h=GH),
                                           ACT.Exp).then_inc(from_act, 1)
                            act.activation(eD[:], dd[:], ACT.Exp).then_inc(from_act, 1)
                            act.wait_ge(sq_done, 1)
                            act.activation(ss[:], ss[:], ACT.Sqrt).then_inc(from_act, 1)

                        @block.vector
                        def _(dve):
                            n = [0]

                            def link(i):
                                n[0] += 1
                                i.then_inc(ch, 1)
                                dve.wait_ge(ch, n[0])

                            link(dve.tensor_tensor(x[:], AB[:, :, 0:GH], dtb[:].unsqueeze(1).broadcast_to([P, NT, GH]), ALU.add))
                            dve.scalar_tensor_tensor(ax[:], x[:], -1.0, x[:], ALU.mult, ALU.max).then_inc(aux, 1)
                            qk = YT[:, :, 0:2 * QKW]
                            link(dve.tensor_tensor(sq[:], qk, qk, ALU.mult))
                            dve.reduce_sum(ss[:].rearrange("p t h -> p (t h)"),
                                           sq[:].rearrange("p t (h c) -> p (t h) c", c=GK), AX.X).then_inc(sq_done, 1)
                            dve.wait_ge(from_act, 3)
                            dve.tensor_scalar(u[:], e[:], 1.0, None, ALU.add).then_inc(aux, 1)
                            dve.wait_ge(aux, 2)
                            link(dve.tensor_scalar(du[:], u[:], 1.0, None, ALU.subtract))
                            link(dve.tensor_scalar(one[:], du[:], 0.0, None, ALU.is_equal))
                            link(dve.tensor_tensor(du[:], du[:], one[:], ALU.add))
                            link(dve.reciprocal(du[:], du[:]))
                            link(dve.tensor_tensor(du[:], du[:], e[:], ALU.mult))
                            link(dve.tensor_tensor(one[:], one[:], e[:], ALU.mult))
                            dve.wait_ge(from_act, 4)
                            link(dve.tensor_tensor(lnu[:], lnu[:], du[:], ALU.mult))
                            link(dve.tensor_tensor(lnu[:], lnu[:], one[:], ALU.add))
                            link(dve.scalar_tensor_tensor(x[:], x[:], 0.0, lnu[:], ALU.max, ALU.add))
                            dve.scalar_tensor_tensor(g[:], x[:], -1.0, ea[:].unsqueeze(1).broadcast_to([P, NT, GH]),
                                                     ALU.mult, ALU.mult).then_inc(to_pe, 1)
                            link(dve.tensor_scalar(eb[:], eb[:], 1.0, None, ALU.add))
                            link(dve.reciprocal(beta[:], eb[:]))
                            dve.wait_ge(from_pe, 2)
                            link(dve.tensor_copy(G[:], psum[:, 0, 0:NT * GH].rearrange("p (t h) -> p t h", h=GH)))
                            dve.tensor_tensor(dd[:], psum[:, 1, 0:NT * GH].rearrange("p (t h) -> p t h", h=GH), G[:],
                                              ALU.subtract).then_inc(aux, 1)
                            dve.wait_ge(from_act, 8)
                            link(dve.reciprocal(r[:], ss[:]))
                            for h in range(GH):
                                rows = slice(32 * (h % 4), 32 * (h % 4) + 32)
                                link(dve.tensor_copy(ETH[rows, h // 4, :], eT[rows, :, h]))
                            rq, rk = r[:, :, 0:GH], r[:, :, GH:]
                            link(dve.tensor_scalar(fk[:, 0], rq, GK ** -0.5, None, ALU.mult))
                            link(dve.tensor_tensor(fk[:, 1], fk[:, 0], eG[:], ALU.mult))
                            link(dve.tensor_tensor(fk[:, 2], rk, beta[:], ALU.mult))
                            link(dve.tensor_tensor(fk[:, 3], fk[:, 2], eG[:], ALU.mult))
                            link(dve.tensor_tensor(fk[:, 4], rk, eD[:], ALU.mult))
                            q, k = YT[:, :, 0:QKW], YT[:, :, QKW:2 * QKW]
                            for out, src, f in ((QN, q, fk[:, 0]), (QE, q, fk[:, 1]), (KN, k, rk), (KB, k, fk[:, 2]),
                                                (KBE, k, fk[:, 3]), (KD, k, fk[:, 4])):
                                for t in range(NT):
                                    dve.tensor_tensor(out[:, t], src[:, t, :].rearrange("p (h c) -> p h c", c=GK),
                                                      f[:, t, :].unsqueeze(2).broadcast_to([P, GH, GK]), ALU.mult)
                            for t in range(NT):
                                last = dve.tensor_tensor(BV[:, t], YT[:, t, 2 * QKW:].rearrange("p (h c) -> p h c", c=GV),
                                                         beta[:, t, :].unsqueeze(2).broadcast_to([P, GH, GV]), ALU.mult)

            with ExitStack() as tmp2:
                sb2 = lambda n, shape, dt=F32: core.sb(n, shape, dt, tmp2)
                KNT, KBT, QNT = (sb2(n, [P, 2, S]) for n in ("kn_features", "kb_features", "qn_features"))
                GT = sb2("g_sums_rows", [NT * GH, P])
                g_scratch = nc.dram_tensor("gd_g_sums", (NT * GH, P), F32, kind="Internal").ap()
                turned, kept = sem("qk_turned"), sem("qk_kept")
                gt_in, gt_kept, g_stored = sem("g_rows_in"), sem("g_rows_kept"), sem("g_rows_stored")
                g_spread = [sem(f"g_rows_of_head_{h}") for h in range(GH)]
                e_sub, e_exp, e_done = sem("e_sub"), sem("e_exp"), sem("e_done")
                p_in, p_done, a_in, a_done = sem("p_in"), sem("p_done"), sem("a_in"), sem("a_done")
                units = [(o, i, f, half) for f in range(2) for o, i in ((KNT, KN), (KBT, KB), (QNT, QN))
                         for half in range(NH2)]
                FIRST = len(units) // 2
                units += [(QET, QE, f, half) for f in range(2) for half in range(NH2)]
                NB = GH * 2
                with nc.Block() as block:
                    @block.sync
                    def _(sp):
                        sp.wait_ge(gt_kept, 1)
                        sp.dma_start(g_scratch, GT[:]).then_inc(g_stored, 16)
                        sp.wait_ge(g_stored, 16)
                        for h in range(GH):
                            sp.dma_start(EA[:, h * NT:(h + 1) * NT, :],
                                         g_scratch.rearrange("(a t h) n -> a h t n", a=1, h=GH)[:, h].broadcast_to([P, NT, P])
                                         ).then_inc(g_spread[h], 16)
                        for n in range(NG):
                            sp.dma_start(TB[:, n].rearrange("p t j -> p (t j)"),
                                         d["eye"].rearrange("(a n) -> a n", a=1).broadcast_to([BLOCKS, T32 * T32])
                                         ).then_inc(t_eye, 16)
                        sp.wait_ge(a_done, NB // NG)
                        load_a_blocks(sp, 0)

                    @block.gpsimd
                    def _(pool):
                        substitute(pool, 0, 0, EARLY)

                    @block.tensor
                    def _(pe):
                        def turn(n):
                            o, i, f, half = units[n]
                            w = P if f == 0 else QKW - P
                            if n >= 2:
                                pe.wait_ge(kept, n - 1)
                            for j in range(4):
                                t = 4 * half + j
                                last = pe.transpose(psum[0:w, n % 2, j * P:(j + 1) * P],
                                                    i[:, t].rearrange("p h c -> p (h c)")[:, f * P:f * P + w], ident[:])
                            last.then_inc(turned, 1)

                        pe.transpose(psum[0:NT * GH, 2, 0:P], G[:].rearrange("p t h -> p (t h)"), ident[:]).then_inc(gt_in, 1)
                        for n in range(FIRST):
                            turn(n)
                        for b in range(NB):
                            h, half = b // 2, b % 2
                            rows = slice(32 * (h % 4), 32 * (h % 4) + 32)
                            pe.wait_ge(kept, FIRST if h < 4 else 2 * FIRST)
                            for o, used, ready, by in ((4, p_done, p_in, QNT), (6, a_done, a_in, KBT)):
                                if b >= 2:
                                    pe.wait_ge(used, b - 1)
                                for j in range(4):
                                    cols = slice((4 * half + j) * P, (4 * half + j + 1) * P)
                                    last = pe.matmul(psum[:, o + b % 2, j * P:(j + 1) * P], KNT[rows, h // 4, cols],
                                                     by[rows, h // 4, cols], start=True, stop=True)
                                last.then_inc(ready, 1)
                            if FIRST + b < len(units):
                                turn(FIRST + b)

                    @block.scalar
                    def _(act):
                        def keep(n):
                            o, i, f, half = units[n]
                            w = P if f == 0 else QKW - P
                            act.wait_ge(turned, n + 1)
                            act.activation(o[0:w, f, half * HALF:(half + 1) * HALF], psum[0:w, n % 2, :],
                                           ACT.Copy).then_inc(kept, 1)

                        act.wait_ge(gt_in, 1)
                        act.activation(GT[:], psum[0:NT * GH, 2, 0:P], ACT.Copy).then_inc(gt_kept, 1)
                        for n in range(FIRST):
                            keep(n)
                        for b in range(NB):
                            blk = slice(4 * b, 4 * b + 4)
                            act.wait_ge(e_sub, b + 1)
                            act.activation(EA[:, blk], EA[:, blk], ACT.Exp).then_inc(e_exp, 1)
                            if FIRST + b < len(units):
                                keep(FIRST + b)

                    @block.vector
                    def _(dve):
                        for b in range(NB + 1):
                            if b < NB:
                                h, half = b // 2, b % 2
                                dve.wait_ge(g_spread[h], 16)
                                for j in range(4):
                                    last = dve.tensor_scalar(EA[:, 4 * b + j], EA[:, 4 * b + j],
                                                             G[:, 4 * half + j, h:h + 1], 0.0, ALU.subtract, ALU.min)
                                last.then_inc(e_sub, 1)
                            if b >= 1:
                                c = b - 1
                                blk = slice(4 * c, 4 * c + 4)
                                dve.wait_ge(e_exp, c + 1)
                                dve.tensor_tensor(EA[:, blk], EA[:, blk], tri[:].unsqueeze(1).broadcast_to([P, 4, P]),
                                                  ALU.mult).then_inc(e_done, 1)
                                dve.wait_ge(e_done, c + 1)
                                dve.wait_ge(p_in, c + 1)
                                dve.tensor_tensor(PT[:, blk], psum[:, 4 + c % 2, :].rearrange("p (t n) -> p t n", t=4),
                                                  EA[:, blk], ALU.mult).then_inc(p_done, 1)
                                dve.wait_ge(p_done, c + 1)
                                dve.wait_ge(a_in, c + 1)
                                dve.scalar_tensor_tensor(EA[:, blk], psum[:, 6 + c % 2, :].rearrange("p (t n) -> p t n", t=4),
                                                         -1.0, EA[:, blk], ALU.mult, ALU.mult).then_inc(a_done, 1)

            norm_scope.close()

            TT = core.sb("t_inverse_transposed", [P, GH * NT, P], F32, mid_scope)
            nWT = core.sb("minus_w_features", [P, 2, S], F32, mid_scope)
            with ExitStack() as tmp2:
                sb2 = lambda n, shape, dt=F32: core.sb(n, shape, dt, tmp2)
                T64 = sb2("t_first_half", [P, GH * NT, P // 2])
                X32 = sb2("a_times_t", [P, NBT, CB, T32])
                zeroed = sem("zeroed")
                placed = [sem(f"t_blocks_placed_{n}") for n in range(NG)]
                x_in, x_kept, y_in, w_in, w_kept = (sem(n) for n in ("x_in", "x_kept", "y_in", "w_in", "w_kept"))
                x64_in, x64_kept, y64_in, y64_kept = (sem(n) for n in ("x64_in", "x64_kept", "y64_in", "y64_kept"))
                joined = sem("off_blocks_joined")
                chunks = lambda b: range(b * CB, (b + 1) * CB)
                blk = lambda b: slice(b * CB, (b + 1) * CB)
                bank = lambda b, i: psum[:, 2 * (b % BANKS) + i, 0:CB * T32].rearrange("p (c n) -> p c n", n=T32)
                half_bank = lambda b: psum[:, 2 * (b % BANKS):2 * (b % BANKS) + 2, :].rearrange("p a (c n) -> p (a c) n", n=P // 2)[:, 0:CB]
                lo, hi = slice(0, P // 2), slice(P // 2, P)
                BANKS = 3
                UB = CB // 4
                with nc.Block() as block:
                    @block.sync
                    def _(sp):
                        load_a_blocks(sp, 1)
                        for n in range(NG):
                            store_t_blocks(sp, n)
                            sp.wait_ge(t_written[n], 32)
                            for q in range(4):
                                sp.dma_start(TT[group(q), chunks_of(n), group(q)],
                                             t_scratch[n, 0, q].rearrange("c j t -> j c t")).then_inc(placed[n], 16)
                            for q in range(3):
                                sp.dma_start(T64[group(q), chunks_of(n), group(q % 2)],
                                             t_scratch[n, 1, q].rearrange("c t j -> t c j")).then_inc(placed[n], 16)

                    @block.gpsimd
                    def _(pool):
                        substitute(pool, 0, EARLY, T32)

                    @block.tensor
                    def _(pe):
                        def w_features(b):
                            pe.wait_ge(y64_kept, b + 1)
                            for u in range(UB * b, UB * (b + 1)):
                                h, half = u // 2, u % 2
                                rows = slice(32 * (h % 4), 32 * (h % 4) + 32)
                                if u >= 2:
                                    pe.wait_ge(w_kept, u - 1)
                                for j in range(4):
                                    t = 4 * half + j
                                    last = pe.matmul(psum[rows, 6 + u % 2, j * P:(j + 1) * P], KBE[:, t, h, :],
                                                     TT[:, h * NT + t, :], start=True, stop=True)
                                last.then_inc(w_in, 1)

                        def x32(b):
                            pe.wait_ge(placed[((b + 1) * CB - 1) // GCH], 16 * 7)
                            if b >= BANKS:
                                pe.wait_ge(y64_kept, b - BANKS + 1)
                            for i, c in enumerate(chunks(b)):
                                for q in (0, 2):
                                    last = pe.matmul(bank(b, 0)[group(q + 1), i], EA[group(q), c, group(q + 1)],
                                                     T64[group(q), c, 0:T32], start=True, stop=True)
                            last.then_inc(x_in, 1)

                        def y32(b):
                            pe.wait_ge(x_kept, 2 * (b + 1))
                            for i, c in enumerate(chunks(b)):
                                pe.matmul(bank(b, 0)[group(1), i], TT[group(1), c, group(1)], X32[group(1), b, i],
                                          start=True, stop=True)
                            for i, c in enumerate(chunks(b)):
                                for q in (1, 3):
                                    last = pe.matmul(bank(b, 1)[group(q - 1), i], X32[group(q), b, i],
                                                     TT[group(q), c, group(q)], start=True, stop=True)
                            last.then_inc(y_in, 1)

                        def x64(b):
                            pe.wait_ge(zeroed, 4)
                            pe.wait_ge(joined, 3 * (b + 1))
                            for i, c in enumerate(chunks(b)):
                                last = pe.matmul(half_bank(b)[hi, i], EA[lo, c, hi], T64[lo, c], start=True, stop=True)
                            last.then_inc(x64_in, 1)

                        def y64(b):
                            pe.wait_ge(x64_kept, b + 1)
                            for i, c in enumerate(chunks(b)):
                                last = pe.matmul(half_bank(b)[lo, i], T64[hi, c], TT[hi, c, hi], start=True, stop=True)
                            last.then_inc(y64_in, 1)

                        for b in range(NBT + 2):
                            if b < NBT:
                                x32(b)
                            if 1 <= b <= NBT:
                                x64(b - 1)
                            if b < NBT:
                                y32(b)
                            if 1 <= b <= NBT:
                                y64(b - 1)
                            if b >= 2:
                                w_features(b - 2)

                    @block.scalar
                    def _(act):
                        def keep_w(b):
                            for u in range(UB * b, UB * (b + 1)):
                                h, half = u // 2, u % 2
                                rows = slice(32 * (h % 4), 32 * (h % 4) + 32)
                                act.wait_ge(w_in, u + 1)
                                act.activation(nWT[rows, h // 4, half * HALF:(half + 1) * HALF],
                                               psum[rows, 6 + u % 2, :], ACT.Copy, scale=-1.0).then_inc(w_kept, 1)

                        for o in (TT[hi, :, lo], TT[group(1), :, group(0)], TT[group(3), :, group(2)],
                                  T64[group(0), :, group(1)]):
                            rows, _, n = o.shape
                            act.activation(o, core.ones_sq[P - rows:, 0:n].unsqueeze(1).broadcast_to([rows, GH * NT, n]),
                                           ACT.Copy, scale=0.0).then_inc(zeroed, 1)
                        for b in range(NBT + 2):
                            if b < NBT:
                                act.wait_ge(x_in, b + 1)
                                for q in (1, 3):
                                    act.activation(X32[group(q), b], bank(b, 0)[group(q)], ACT.Copy).then_inc(x_kept, 1)
                            if 1 <= b <= NBT:
                                act.wait_ge(x64_in, b)
                                act.activation(T64[hi, blk(b - 1)], half_bank(b - 1)[hi], ACT.Copy).then_inc(x64_kept, 1)
                            if b >= 2:
                                keep_w(b - 2)

                    @block.vector
                    def _(dve):
                        substitute(dve, 1, 0, T32)
                        for b in range(NBT + 1):
                            if b < NBT:
                                dve.wait_ge(y_in, b + 1)
                                dve.tensor_copy(T64[group(1), blk(b), group(0)], bank(b, 0)[group(1)]).then_inc(joined, 1)
                                for q in (0, 2):
                                    dve.tensor_copy(TT[group(q), blk(b), group(q + 1)],
                                                    bank(b, 1)[group(q)]).then_inc(joined, 1)
                            if b >= 1:
                                dve.wait_ge(y64_in, b)
                                dve.tensor_copy(TT[lo, blk(b - 1), hi], half_bank(b - 1)[lo]).then_inc(y64_kept, 1)

            O = core.sb("delta_out", [P, NT, VWD], F32, mid_scope)
            with ExitStack() as tmp2:
                sb2 = lambda n, shape, dt=F32: core.sb(n, shape, dt, tmp2)
                St = sb2("state", [P, 2, GV])
                SD = EA[:].rearrange("p c n -> p (c n)")[:, 0:16 * GV].rearrange("p (a f h n) -> p a f h n", a=2, f=2, h=4)
                own = sb2("own_block", [P, 4, GV])
                U = sb2("u", [P, 2, VWD])
                s0, u_in, u_kept, s_in, s_done, o_in, o_kept = (sem(n) for n in
                    ("state_zeroed", "u_in", "u_kept", "s_in", "s_done", "o_in", "o_kept"))
                blocked, own_in = sem("state_blocked"), sem("own_loaded")
                WID = ((P, 4), (QKW - P, 2))
                with nc.Block() as block:
                    @block.sync
                    def _(sp):
                        sp.dma_start(own[:].rearrange("p a n -> p (a n)"), d["own"]).then_inc(own_in, 16)

                    @block.tensor
                    def _(pe):
                        def by_state(o, lhsT, t):
                            for f, (w, nh) in enumerate(WID):
                                last = pe.matmul(o[:, f * 4 * GV:(f * 4 + nh) * GV], lhsT[0:w, f, t * P:(t + 1) * P],
                                                 SD[0:w, t % 2, f, 0:nh, :].rearrange("p a n -> p (a n)"),
                                                 start=False, stop=(f == 1), skip_group_check=True)
                            return last

                        def u_from_v(t):
                            if t >= 2:
                                pe.wait_ge(u_kept, t - 1)
                            for h in range(GH):
                                pe.matmul(psum[:, t % 2, h * GV:(h + 1) * GV], TT[:, h * NT + t, :], BV[:, t, h, :],
                                          start=(h == 0), stop=False, skip_group_check=True)

                        u_from_v(0)
                        for t in range(NT):
                            pe.wait_ge(blocked, 2 * t + 2)
                            by_state(psum[:, t % 2, 0:VWD], nWT, t).then_inc(u_in, 1)
                            if t + 1 < NT:
                                u_from_v(t + 1)
                            pe.wait_ge(u_kept, t + 1)
                            for h in range(GH):
                                rows = slice(32 * (h % 4), 32 * (h % 4) + 32)
                                last = pe.matmul(psum[rows, 4 + t % 2, (h // 4) * GV:(h // 4 + 1) * GV], KD[:, t, h, :],
                                                 U[:, t % 2, h * GV:(h + 1) * GV], start=True, stop=True)
                            last.then_inc(s_in, 1)
                            if t >= 2:
                                pe.wait_ge(o_kept, t - 1)
                            for h in range(GH):
                                pe.matmul(psum[:, 2 + t % 2, h * GV:(h + 1) * GV], PT[:, h * NT + t, :],
                                          U[:, t % 2, h * GV:(h + 1) * GV], start=(h == 0), stop=False,
                                          skip_group_check=True)
                            by_state(psum[:, 2 + t % 2, 0:VWD], QET, t).then_inc(o_in, 1)

                    @block.vector
                    def _(dve):
                        dve.memset(St[:], 0.0).then_inc(s0, 1)
                        dve.memset(SD[:], 0.0).then_inc(blocked, 2)
                        dve.wait_ge(s0, 1)
                        dve.wait_ge(own_in, 16)
                        dve.wait_ge(blocked, 2)
                        for t in range(NT):
                            dve.wait_ge(u_in, t + 1)
                            if t >= 2:
                                dve.wait_ge(s_in, t - 1)
                                dve.wait_ge(o_in, t - 1)
                            dve.tensor_copy(U[:, t % 2, :], psum[:, t % 2, 0:VWD]).then_inc(u_kept, 1)
                            dve.wait_ge(s_in, t + 1)
                            if t >= 1:
                                dve.wait_ge(blocked, 2 * t + 2)
                            for f, (w, nh) in enumerate(WID):
                                dve.scalar_tensor_tensor(St[0:w, f, :], St[0:w, f, :], ETH[0:w, f, t:t + 1],
                                                         psum[0:w, 4 + t % 2, f * GV:(f + 1) * GV],
                                                         ALU.mult, ALU.add).then_inc(s_done, 1)
                            if t >= 1:
                                dve.wait_ge(o_in, t)
                            dve.wait_ge(s_done, 2 * t + 2)
                            for f, (w, nh) in enumerate(WID):
                                dve.tensor_tensor(SD[0:w, (t + 1) % 2, f, 0:nh, :], St[0:w, f, :].unsqueeze(1).broadcast_to([w, nh, GV]),
                                                  own[0:w, 0:nh, :], ALU.mult).then_inc(blocked, 1)

                    @block.scalar
                    def _(act):
                        for t in range(NT):
                            act.wait_ge(o_in, t + 1)
                            act.activation(O[:, t, :], psum[:, 2 + t % 2, 0:VWD], ACT.Copy).then_inc(o_kept, 1)

            with ExitStack() as tmp2:
                sb2 = lambda n, shape, dt=F32: core.sb(n, shape, dt, tmp2)
                sq = EA[:].rearrange("p c n -> p (c n)")[:, 0:NT * VWD].rearrange("p (t n) -> p t n", t=NT)
                ms, rr = sb2("o_mean_squares", [P, NT * GH]), sb2("o_inverse_rms", [P, NT * GH])
                ch, sw, to_act, from_act = sem("norm_chain"), sem("gate_weighted"), sem("rms_in"), sem("rms_out")
                with nc.Block() as block:
                    @block.gpsimd
                    def _(pool):
                        for t in range(NT):
                            pool.tensor_tensor(SG[:, t].rearrange("p (h c) -> p h c", c=GV),
                                               SG[:, t].rearrange("p (h c) -> p h c", c=GV),
                                               nw[:].unsqueeze(1).broadcast_to([P, GH, GV]), ALU.mult).then_inc(sw, 1)

                    @block.scalar
                    def _(act):
                        act.wait_ge(to_act, 1)
                        act.activation(ms[:], ms[:], ACT.Sqrt).then_inc(from_act, 1)

                    @block.vector
                    def _(dve):
                        n = [0]

                        def link(i):
                            n[0] += 1
                            i.then_inc(ch, 1)
                            dve.wait_ge(ch, n[0])

                        link(dve.tensor_tensor(sq[:], O[:], O[:], ALU.mult))
                        link(dve.reduce_sum(ms[:], sq[:].rearrange("p t (h c) -> p (t h) c", c=GV), AX.X))
                        dve.tensor_scalar(ms[:], ms[:], 1.0 / GV, RMS_EPS, ALU.mult, ALU.add).then_inc(to_act, 1)
                        dve.wait_ge(from_act, 1)
                        link(dve.reciprocal(rr[:], ms[:]))
                        link(dve.tensor_tensor(O[:].rearrange("p t (h c) -> p (t h) c", c=GV),
                                               O[:].rearrange("p t (h c) -> p (t h) c", c=GV),
                                               rr[:].unsqueeze(2).broadcast_to([P, NT * GH, GV]), ALU.mult))
                        dve.wait_ge(sw, NT)
                        dve.tensor_tensor(O[:], O[:], SG[:], ALU.mult)

            project_out(nc, core, tag, O, wo, None, tiles=3,
                        OT=PT[:].rearrange("p c n -> p (c n)")[:, 0:3 * S].rearrange("p (f n) -> p f n", f=3))



NX = 8
RANK = 16
TOPK = 2
DH = 704
ALPHA = 2.0
FT = [(f * P, min(P, DH - f * P)) for f in range(-(-DH // P))]
NFT = len(FT)


def routed_weights(nc, core, d, scope):
    w = {
        "gate": core.sb("router", [P, KT, NX], F32, scope),
        "up": core.sb("w_up", [P, KT, DH], F32, scope), "gt": core.sb("w_gate", [P, KT, DH], F32, scope),
        "upA": core.sb("up_a", [P, KT, P], F32, scope), "gtA": core.sb("gate_a", [P, KT, P], F32, scope),
        "upB": core.sb("up_b", [P, DH], F32, scope), "gtB": core.sb("gate_b", [P, DH], F32, scope),
        "down": core.sb("w_down", [P, NFT, D], F32, scope), "dnA": core.sb("down_a", [P, NFT, P], F32, scope),
        "dnB": core.sb("down_b", [P, D], F32, scope), "expert": core.sb("expert_of_column", [P, P], F32, scope),
    }
    router_loaded, loaded = core.sem("router_loaded"), core.sem("routed_w_loaded")
    full = (NFT - 1) * P

    def loads(sp):
        sp.dma_start(w["gate"][:], d["gate"].rearrange("(k p) n -> p k n", p=P)).then_inc(router_loaded, 16)
        sp.dma_start(w["expert"][:], d["expert"]).then_inc(router_loaded, 16)
        for name in ("upA", "gtA", "up", "gt"):
            sp.dma_start(w[name][:], d[name].rearrange("(k p) n -> p k n", p=P)).then_inc(loaded, 16)
        for name in ("upB", "gtB", "dnB"):
            sp.dma_start(w[name][:], d[name]).then_inc(loaded, 16)
        for name in ("down", "dnA"):
            sp.dma_start(w[name][:, 0:NFT - 1, :], d[name][0:full, :].rearrange("(k p) n -> p k n", p=P)
                         ).then_inc(loaded, 16)
            sp.dma_start(w[name][0:DH - full, NFT - 1, :], d[name][full:DH, :]).then_inc(loaded, 16)

    return w, loads, router_loaded, loaded, 16 * (4 + 3 + 2 * 2)


def routed_layer(nc, core, tag, d):
    with ExitStack() as scope:
        w, loads, router_loaded, loaded, count = routed_weights(nc, core, d, scope)
        norm_stage(nc, core, tag + "n", loads)
        routed_ffn(nc, core, tag, w, router_loaded, loaded, count)


def routed_ffn(nc, core, tag, w, router_loaded, loaded, all_loaded):
    X, XNT, psum, ident = core.X, core.XNT, core.psum, core.ident
    sem = lambda n: core.sem(f"{tag}_{n}")
    with ExitStack() as tmp:
        sb = lambda n, shape, dt=F32: core.sb(n, shape, dt, tmp)
        MASK = sb("expert_mask", [P, TOPK, S])
        CB = sb("weight_rows", [P, TOPK, S])
        H = sb("slot_hidden", [P, TOPK, NFT, S])
        MX = sb("mixed_hidden", [P, NFT, S])
        DL = sb("lora_down", [P, S])
        with ExitStack() as tmp2:
            sb2 = lambda n, shape, dt=F32: core.sb(n, shape, dt, tmp2)
            LG, m8 = sb2("logits", [P, NT, NX]), sb2("sorted", [P, NT, 8])
            ix, ixf = sb2("indices", [P, NT, 8], U32), sb2("indices_f", [P, NT, TOPK])
            pm, gm, ps_, rs = (sb2(n, [P, TOPK]) for n in ("part_max", "all_max", "part_sum", "inv_sum"))
            ev, cw = sb2("exp_top", [P, NT, TOPK]), sb2("weights", [P, NT, TOPK])
            mk = sb2("wide_rows", [P, 2, TOPK, NT, P])
            lg_in, lg_out, top, idx, ch = sem("logits"), sem("logits_kept"), sem("top"), sem("index"), sem("chain")
            pmax, gmax, dif, ex, tot, tot_in = sem("part_max"), sem("all_max"), sem("dif"), sem("exp"), sem("part_sum"), sem("total")
            wide, turned, kept = sem("wide"), sem("turned"), sem("kept")
            tot_read = sem("total_read")
            Z = sb2("lora_in", [P, 2, TOPK, S])
            sil, gc = sb2("silu", [P, 2, HALF]), sb2("gate_weighted", [P, 2, HALF])
            MD = sb2("mask_differences", [P, S])
            z_in, z_done, up_in, silu, gated, hid, mixed = (sem(n) for n in
                ("z_in", "z_done", "up_in", "silu", "gated", "hidden", "mixed"))
            mask_diff = sem("mask_difference")
            pairs = [(half, f) for half in range(NH2) for f in range(NFT)]
            NP, BUF = len(pairs), 3
            steps = [(0, 0)] + [s for p in range(1, NP) for s in ((p, 0), (p - 1, 1))] + [(NP - 1, 1)]
            at = {s: i for i, s in enumerate(steps)}
            with nc.Block() as block:
                @block.tensor
                def _(pe):
                    def lora_in(half):
                        for j, wa in enumerate(("upA", "gtA")):
                            if half:
                                pe.wait_ge(z_done, TOPK * (j + 1))
                            for k in range(KT):
                                last = pe.matmul(psum[:, 2 * BUF + j, :], w[wa][:, k, :],
                                                 XNT[:, k, half * HALF:(half + 1) * HALF],
                                                 start=(k == 0), stop=(k == KT - 1))
                            last.then_inc(z_in, 1)

                    def base(p):
                        half, f = pairs[p]
                        a, n = FT[f]
                        for j, wb in enumerate(("up", "gt")):
                            for kk in range(KT):
                                pe.matmul(psum[0:n, 2 * (p % BUF) + j, :], w[wb][:, kk, a:a + n],
                                          XNT[:, kk, half * HALF:(half + 1) * HALF], start=(kk == 0), stop=False,
                                          skip_group_check=True)

                    pe.wait_ge(router_loaded, 32)
                    for t in range(NT):
                        for k in range(KT):
                            last = pe.matmul(psum[:, 5, t * NX:(t + 1) * NX], XNT[:, k, t * P:(t + 1) * P],
                                             w["gate"][:, k, :], start=(k == 0), stop=(k == KT - 1))
                    last.then_inc(lg_in, 1)
                    pe.wait_ge(loaded, all_loaded)
                    lora_in(0)
                    base(0)
                    pe.wait_ge(tot, 1)
                    pe.matmul(psum[:, 5, P:P + TOPK], core.ones_sq[:], ps_[:], start=True, stop=True).then_inc(tot_in, 1)
                    base(1)
                    pe.wait_ge(tot_read, 1)
                    n = 0
                    for kind in range(2):
                        pe.wait_ge(wide, kind + 1)
                        for k in range(TOPK):
                            for half in range(NH2):
                                if n >= 2:
                                    pe.wait_ge(kept, n - 1)
                                for j in range(4):
                                    last = pe.transpose(psum[:, 4 + n % 2, j * P:(j + 1) * P],
                                                        mk[:, kind, k, 4 * half + j, :], ident[:])
                                last.then_inc(turned, 1)
                                n += 1

                    for p, k in steps:
                        half, f = pairs[p]
                        a, n = FT[f]
                        cols = slice(half * HALF, (half + 1) * HALF)
                        if (p, k) == (1, 0):
                            lora_in(1)
                        if (p, k) == (2, 0):
                            pe.wait_ge(kept, 2 * TOPK * NH2)
                        if k == 0 and p >= BUF:
                            pe.wait_ge(silu, at[p - BUF, 1] + 1)
                            pe.wait_ge(gated, at[p - BUF, 1] + 1)
                        if k == 0 and p >= 2:
                            base(p)
                        if k == 0 and f == 0:
                            pe.wait_ge(z_done, 2 * TOPK * (half + 1))
                        if k == 1:
                            pe.wait_ge(silu, at[p, 0] + 1)
                            pe.wait_ge(gated, at[p, 0] + 1)
                        for j, wl in enumerate(("upB", "gtB")):
                            pe.matmul(psum[0:n, 2 * (p % BUF) + j, :], w[wl][:, a:a + n], Z[:, j, k, cols],
                                      start=False, stop=True, skip_group_check=True).then_inc(up_in, 1)

                @block.gpsimd
                def _(pool):
                    pool.wait_ge(pmax, 1)
                    pool.partition_all_reduce(gm[:], pm[:], P, bass.bass_isa.ReduceOp.max).then_inc(gmax, 1)

                    for p, (half, f) in enumerate(pairs):
                        n = FT[f][1]
                        cols = slice(half * HALF, (half + 1) * HALF)
                        pool.wait_ge(hid, at[p, 1] + 1)
                        pool.tensor_tensor(MX[0:n, f, cols], H[0:n, 0, f, cols], H[0:n, 1, f, cols],
                                           ALU.add).then_inc(mixed, 1)

                @block.scalar
                def _(act):
                    act.wait_ge(dif, 1)
                    act.activation(ev[:], ev[:], ACT.Exp).then_inc(ex, 1)
                    n = 0
                    for o in (MASK, CB):
                        for k in range(TOPK):
                            for half in range(NH2):
                                act.wait_ge(turned, n + 1)
                                act.activation(o[:, k, half * HALF:(half + 1) * HALF], psum[:, 4 + n % 2, :],
                                               ACT.Copy).then_inc(kept, 1)
                                n += 1

                    for i, (p, k) in enumerate(steps):
                        n = FT[pairs[p][1]][1]
                        act.wait_ge(up_in, 2 * i + 1)
                        if i >= 2:
                            act.wait_ge(hid, i - 1)
                        act.activation(sil[0:n, i % 2, :], psum[0:n, 2 * (p % BUF), :], ACT.Silu).then_inc(silu, 1)

                @block.vector
                def _(dve):
                    c = [0]

                    def link(i):
                        c[0] += 1
                        i.then_inc(ch, 1)
                        dve.wait_ge(ch, c[0])

                    dve.wait_ge(lg_in, 1)
                    dve.tensor_copy(LG[:].rearrange("p t n -> p (t n)"), psum[:, 5, 0:NT * NX]).then_inc(lg_out, 1)
                    dve.wait_ge(lg_out, 1)
                    for t in range(NT):
                        dve.max(m8[:, t, :], LG[:, t, :]).then_inc(top, 1)
                    dve.wait_ge(top, NT)
                    dve.reduce_max(pm[:], m8[:, :, 0:TOPK].rearrange("p t k -> p k t"), AX.X).then_inc(pmax, 1)
                    for t in range(NT):
                        dve.max_index(ix[:, t, :], m8[:, t, :], LG[:, t, :]).then_inc(idx, 1)
                    dve.wait_ge(idx, NT)
                    link(dve.tensor_copy(ixf[:], ix[:, :, 0:TOPK]))
                    for k in range(TOPK):
                        for t in range(NT):
                            last = dve.tensor_scalar(mk[:, 0, k, t, :], w["expert"][:], ixf[:, t, k:k + 1], ALPHA,
                                                     ALU.is_equal, ALU.mult)
                    last.then_inc(wide, 1)
                    dve.wait_ge(gmax, 1)
                    dve.tensor_tensor(ev[:], m8[:, :, 0:TOPK], gm[:].unsqueeze(1).broadcast_to([P, NT, TOPK]),
                                      ALU.subtract).then_inc(dif, 1)
                    dve.wait_ge(ex, 1)
                    dve.reduce_sum(ps_[:], ev[:].rearrange("p t k -> p k t"), AX.X).then_inc(tot, 1)
                    dve.wait_ge(tot_in, 1)
                    dve.reciprocal(rs[:], psum[:, 5, P:P + TOPK]).then_inc(tot_read, 1)
                    dve.wait_ge(tot_read, 1)
                    link(dve.tensor_tensor(cw[:], ev[:], rs[:].unsqueeze(1).broadcast_to([P, NT, TOPK]), ALU.mult))
                    for k in range(TOPK):
                        for t in range(NT):
                            last = dve.tensor_scalar(mk[:, 1, k, t, :], core.ones_sq[:], cw[:, t, k:k + 1], None, ALU.mult)
                    last.then_inc(wide, 1)

                    def lora_masked(half):
                        cols = slice(half * HALF, (half + 1) * HALF)
                        for j in range(2):
                            dve.wait_ge(z_in, 2 * half + j + 1)
                            for k, m in enumerate((MASK[:, 0, cols], MD[:, cols])):
                                dve.tensor_tensor(Z[:, j, k, cols], psum[:, 2 * BUF + j, :], m, ALU.mult
                                                  ).then_inc(z_done, 1)

                    dve.wait_ge(kept, TOPK * NH2)
                    dve.tensor_tensor(MD[:], MASK[:, 1, :], MASK[:, 0, :], ALU.subtract).then_inc(mask_diff, 1)
                    dve.wait_ge(mask_diff, 1)
                    lora_masked(0)
                    dve.wait_ge(kept, 2 * TOPK * NH2)
                    for i, (p, k) in enumerate(steps):
                        half, f = pairs[p]
                        n = FT[f][1]
                        cols = slice(half * HALF, (half + 1) * HALF)
                        dve.wait_ge(up_in, 2 * i + 2)
                        dve.tensor_tensor(gc[0:n, i % 2, :], psum[0:n, 2 * (p % BUF) + 1, :], CB[0:n, k, cols],
                                          ALU.mult).then_inc(gated, 1)
                        dve.wait_ge(gated, i + 1)
                        dve.wait_ge(silu, i + 1)
                        dve.tensor_tensor(H[0:n, k, f, cols], gc[0:n, i % 2, :], sil[0:n, i % 2, :],
                                          ALU.mult).then_inc(hid, 1)
                        if i == 0:
                            lora_masked(1)

        with ExitStack() as tmp2:
            d1 = core.sb("lora_down_second", [P, S], F32, tmp2)
            d_in, d_part, d_done, out_in, added = sem("d_in"), sem("d_part"), sem("d_done"), sem("out_in"), sem("added")
            with nc.Block() as block:
                @block.tensor
                def _(pe):
                    for half in range(NH2):
                        for k in range(TOPK):
                            for f, (a, n) in enumerate(FT):
                                last = pe.matmul(psum[:, 2 * half + k, :], w["dnA"][0:n, f, :],
                                                 H[0:n, k, f, half * HALF:(half + 1) * HALF],
                                                 start=(f == 0), stop=(f == NFT - 1))
                            last.then_inc(d_in, 1)
                    for t in range(NT):
                        if t >= 4:
                            pe.wait_ge(added, t - 3)
                        for f, (a, n) in enumerate(FT):
                            pe.matmul(psum[:, 4 + t % 4, 0:D], MX[0:n, f, t * P:(t + 1) * P], w["down"][0:n, f, :],
                                      start=(f == 0), stop=False)
                        pe.wait_ge(d_done, t // 4 + 1)
                        pe.matmul(psum[:, 4 + t % 4, 0:D], DL[:, t * P:(t + 1) * P], w["dnB"][:],
                                  start=False, stop=True).then_inc(out_in, 1)

                @block.vector
                def _(dve):
                    for half in range(NH2):
                        cols = slice(half * HALF, (half + 1) * HALF)
                        for k, o in enumerate((DL, d1)):
                            dve.wait_ge(d_in, 2 * half + k + 1)
                            dve.tensor_tensor(o[:, cols], psum[:, 2 * half + k, :], MASK[:, k, cols],
                                              ALU.mult).then_inc(d_part, 1)
                        dve.wait_ge(d_part, 2 * half + 2)
                        dve.tensor_tensor(DL[:, cols], DL[:, cols], d1[:, cols], ALU.add).then_inc(d_done, 1)
                    for t in range(NT):
                        dve.wait_ge(out_in, t + 1)
                        dve.tensor_tensor(X[:, t, :], psum[:, 4 + t % 4, 0:D], X[:, t, :], ALU.add).then_inc(added, 1)
                        core.tile_stats(dve, t, added)


LAT, RD = 64, 64
NOPE = LAT
QROWS = RD + HD
SHIFT = 96
NEG = -1e30


def latent_attention(nc, core, tag, d):
    X, XNT, psum, ident = core.X, core.XNT, core.psum, core.ident
    sem = lambda n: core.sem(f"{tag}_{n}")
    SC = float(1.0 / np.sqrt(np.float32(HD + RD)))
    with ExitStack() as tmp:
        sb = lambda n, shape, dt=F32: core.sb(n, shape, dt, tmp)
        V = sb("v_ones", [P, NT, HEADS, VW])
        O = sb("attended", [P, NT, D])
        wo = sb("wo", [P, KT, D])
        with ExitStack() as tmpA:
            sba = lambda n, shape, dt=F32: core.sb(n, shape, dt, tmpA)
            Q = sba("q_all", [P, HEADS, S])
            Qb = sba("q_all_bf16", [QROWS, HEADS, S], BF16)
            K = sba("k_head", [P, 2, S])
            Kb = sba("k_head_bf16", [QROWS, 2, S], BF16)
            kT = sba("k_features", [P, KT, S])
            kTb = sba("k_features_bf16", [P, KT, S], BF16)
            idb = sba("identity_bf16", [P, P], BF16)
            mQ, mK = sba("mask_by_query", [P, P], BF16), sba("mask_by_key", [P, P], BF16)
            with ExitStack() as tmp2:
                sb2 = lambda n, shape, dt=F32: core.sb(n, shape, dt, tmp2)
                w1 = sb2("w_latents", [P, KT, 3 * LAT + RD])
                wq = sb2("w_q_rotary", [LAT, HEADS, 2 * RD])
                wplain = sb2("w_plain", [P, D])
                wv = sb2("w_vu", [P, D])
                cs = sb2("cos_over_sin", [2 * RD, S])
                L = sb2("latents", [2 * LAT, S])
                qT, qTb = sb2("q_features", [P, KT, S]), sb2("q_features_bf16", [P, KT, S], BF16)
                t = sb2("by_cos_over_by_sin", [2 * RD, 2, S])
                moved = O[0:RD].rearrange("p (a t) n -> p a (t n)", a=2)
                loaded, rot, made, masks_made = sem("loaded"), sem("rotated_w"), sem("made"), sem("masks_made")
                l_in, l_out, unit_in, by_cs, shifted = (sem(n) for n in ("l_in", "l_out", "unit_in", "by_cos_sin", "by_sin_moved"))
                added = [sem("rotary_even"), sem("rotary_odd")]
                misc_in, misc_act, misc_dve, cast = (sem(n) for n in ("misc_in", "misc_act", "misc_dve", "cast"))
                q_plain, q_zeroed = sem("q_plain_rows"), sem("q_zero_rows")
                pair = lambda b: psum[:, 2 * b:2 * b + 2, :].rearrange("p a n -> p (a n)")
                cols = lambda half: slice(half * HALF, (half + 1) * HALF)

                def loads(sp):
                    sp.dma_start(w1[:, :, 0:3 * LAT], d["w1"].rearrange("(k p) n -> p k n", p=P)).then_inc(loaded, 16)
                    sp.dma_start(wq[:, :, 0:RD], d["wqr"].rearrange("p (h n) -> p h n", n=RD)).then_inc(loaded, 16)
                    sp.dma_start(wplain[0:LAT], d["wqu"]).then_inc(loaded, 16)
                    sp.dma_start(wplain[LAT:], d["wku"]).then_inc(loaded, 16)
                    sp.dma_start(wv[LAT:], d["wvu"]).then_inc(loaded, 16)
                    sp.dma_start(cs[:], d["cs"]).then_inc(loaded, 16)
                    sp.dma_start(wo[:], d["wo"].rearrange("(k p) n -> p k n", p=P)).then_inc(loaded, 16)

                    sp.dma_start(Q[QROWS:SHIFT], d["zeros"].rearrange("(a b n) -> a b n", a=1, b=1).broadcast_to(
                        [SHIFT - QROWS, HEADS, S])).then_inc(q_zeroed, 16)

                LOADS = 7
                norm_stage(nc, core, tag + "n", loads, room=K[:].rearrange("p a (t n) -> p (a t) n", n=D))

                UNITS = 1 + HEADS
                FEATS = 2 * KT
                MISC = FEATS + NT
                unit_bank = lambda n: 1 + n % 2
                misc_bank = lambda m: 3 * (m % 2)
                with nc.Block() as block:
                    @block.tensor
                    def _(pe):
                        def unit(n):
                            if n >= 2:
                                pe.wait_ge(by_cs, n - 1)
                            for half in range(NH2):
                                o = psum[:, 2 * unit_bank(n) + half, :]
                                if n == 0:
                                    for k in range(KT):
                                        last = pe.matmul(o, w1[:, k, 2 * LAT:], XNT[:, k, cols(half)],
                                                         start=(k == 0), stop=(k == KT - 1))
                                else:
                                    last = pe.matmul(o, wq[:, n - 1, :], L[0:LAT, cols(half)], start=True, stop=True)
                            last.then_inc(unit_in, 1)

                        def misc(m):
                            if m >= 2:
                                pe.wait_ge(misc_dve, m - 1)
                                pe.wait_ge(misc_act, min(m - 1, FEATS))
                            if m < FEATS:
                                f, rows = m % KT, (slice(LAT, P), slice(0, LAT))[m // KT]
                                for half in range(NH2):
                                    last = pe.matmul(psum[:, 2 * misc_bank(m) + half, :], wplain[rows, f * P:(f + 1) * P],
                                                     L[rows, cols(half)], start=True, stop=True)
                            else:
                                i = m - FEATS
                                last = pe.matmul(psum[:, 2 * misc_bank(m), 0:D], L[LAT:, i * P:(i + 1) * P], wv[LAT:],
                                                 start=True, stop=True)
                            last.then_inc(misc_in, 1)

                        pe.wait_ge(loaded, 16 * LOADS)
                        for half in range(NH2):
                            for k in range(KT):
                                last = pe.matmul(psum[:, half, :], w1[:, k, 0:2 * LAT], XNT[:, k, cols(half)],
                                                 start=(k == 0), stop=(k == KT - 1))
                        last.then_inc(l_in, 1)
                        pe.wait_ge(rot, 4)
                        for n in range(UNITS):
                            unit(n)
                            if n == 0:
                                pe.wait_ge(l_out, 1)
                            if n < MISC:
                                misc(n)

                    @block.scalar
                    def _(act):
                        act.wait_ge(l_in, 1)
                        act.activation(L[:], pair(0), ACT.Copy).then_inc(l_out, 1)
                        for n in range(UNITS + 1):
                            if n < UNITS:
                                act.wait_ge(by_cs, n + 1)
                                if n >= 2:
                                    act.wait_ge(added[n % 2], (n - 2) // 2 + 1)
                                act.activation(moved[:, n % 2, :], t[RD:, n % 2, :], ACT.Copy).then_inc(shifted, 1)
                            if n < FEATS:
                                act.wait_ge(misc_in, n + 1)
                                act.activation((kT, qT)[n // KT][:, n % KT, :], pair(misc_bank(n)),
                                               ACT.Copy).then_inc(misc_act, 1)
                            if n == 1:
                                act.wait_ge(added[0], 1)
                                act.activation(K[0:RD, 1, :], K[0:RD, 0, :], ACT.Copy).then_inc(cast, 1)
                                for b in range(2):
                                    act.activation(Kb[0:RD, b, :], K[0:RD, 0, :], ACT.Copy).then_inc(cast, 1)
                            if n >= 2:
                                act.wait_ge(added[(n - 1) % 2], (n - 1) // 2 + 1)
                                act.activation(Qb[0:RD, n - 2, :], Q[0:RD, n - 2, :], ACT.Copy).then_inc(cast, 1)

                    def add_halves(eng, n):
                        eng.wait_ge(shifted, n + 1)
                        eng.wait_ge(by_cs, n + 1)
                        o = K[0:RD, 0, :] if n == 0 else Q[0:RD, n - 1, :]
                        eng.tensor_tensor(o, t[0:RD, n % 2, :], moved[:, n % 2, :], ALU.add).then_inc(added[n % 2], 1)

                    @block.vector
                    def _(dve):
                        dve.memset(V[:], 0.0).then_inc(made, 1)
                        dve.wait_ge(made, 1)
                        dve.memset(V[:, :, :, HD:HD + 1], 1.0).then_inc(made, 1)
                        dve.memset(K[NOPE:SHIFT, :, :], 0.0).then_inc(made, 1)
                        dve.memset(K[SHIFT:SHIFT + 1, :, :], 1.0).then_inc(made, 1)
                        dve.wait_ge(loaded, 16 * LOADS)
                        hf = RD // 2
                        kr, krr = w1[:, :, 2 * LAT:2 * LAT + RD], w1[:, :, 2 * LAT + RD:]
                        dve.tensor_scalar(krr[:, :, 0:hf], kr[:, :, hf:], -1.0, None, ALU.mult).then_inc(rot, 1)
                        dve.tensor_copy(krr[:, :, hf:], kr[:, :, 0:hf]).then_inc(rot, 1)
                        dve.tensor_scalar(wq[:, :, RD:RD + hf], wq[:, :, hf:RD], -1.0, None, ALU.mult).then_inc(rot, 1)
                        dve.tensor_copy(wq[:, :, RD + hf:], wq[:, :, 0:hf]).then_inc(rot, 1)
                        dve.wait_ge(made, 4)
                        for n in range(UNITS + 1):
                            if n < UNITS:
                                dve.wait_ge(unit_in, n + 1)
                                if n >= 2:
                                    dve.wait_ge(added[n % 2], (n - 2) // 2 + 1)
                                dve.tensor_tensor(t[:, n % 2, :], pair(unit_bank(n)), cs[:], ALU.mult).then_inc(by_cs, 1)
                            if n < MISC:
                                dve.wait_ge(misc_in, n + 1)
                                if n < FEATS:
                                    dve.wait_ge(misc_act, n + 1)
                                    dve.tensor_copy((kTb, qTb)[n // KT][:, n % KT, :],
                                                    (kT, qT)[n // KT][:, n % KT, :]).then_inc(misc_dve, 1)
                                else:
                                    dve.tensor_copy(V[:, n - FEATS, :, 0:HD], psum[:, 2 * misc_bank(n), 0:D].rearrange(
                                        "p (h d) -> p h d", d=HD)).then_inc(misc_dve, 1)
                            if n >= 1 and n % 2:
                                add_halves(dve, n - 1)

                    @block.gpsimd
                    def _(pool):
                        pool.memset(mQ[:], 0.0).then_inc(masks_made, 1)
                        pool.wait_ge(masks_made, 1)
                        pool.memset(mK[:], 0.0).then_inc(masks_made, 1)
                        pool.wait_ge(masks_made, 2)
                        pool.affine_select(out=mQ[:], in_=mQ[:], compare_op=ALU.is_ge, fill=NEG, base=0,
                                           pattern=[[-1, P]], channel_multiplier=1).then_inc(masks_made, 1)
                        pool.wait_ge(masks_made, 3)
                        pool.affine_select(out=mK[:], in_=mK[:], compare_op=ALU.is_ge, fill=NEG, base=0,
                                           pattern=[[1, P]], channel_multiplier=-1).then_inc(masks_made, 1)
                        pool.wait_ge(masks_made, 4)
                        pool.tensor_copy(idb[:], ident[:]).then_inc(masks_made, 1)
                        for n in range(1, UNITS, 2):
                            add_halves(pool, n)

                    @block.sync
                    def _(sp):
                        sp.wait_ge(misc_act, FEATS)
                        sp.wait_ge(misc_dve, FEATS)
                        for h in range(HEADS):
                            for o, f in ((Q, qT), (Qb, qTb)):
                                sp.dma_start(o[NOPE:QROWS, h, :], f[(h % 8) * HD:(h % 8 + 1) * HD, h // 8, :]
                                             ).then_inc(q_plain, 16)
                        sp.wait_ge(q_plain, 2 * HEADS * 16)
                        sp.wait_ge(q_zeroed, 16)

            with ExitStack() as tmp2:
                k_in, kb_in = [sem("k_in_even"), sem("k_in_odd")], [sem("kb_in_even"), sem("kb_in_odd")]

                class HeadKeys:

                    @staticmethod
                    def keys(sp, h):
                        sp.dma_start(K[NOPE:QROWS, h % 2, :], kT[(h % 8) * HD:(h % 8 + 1) * HD, h // 8, :]
                                     ).then_inc(k_in[h % 2], 16)

                    @staticmethod
                    def keys_bf16(sp, h):
                        sp.dma_start(Kb[NOPE:QROWS, h % 2, :], kTb[(h % 8) * HD:(h % 8 + 1) * HD, h // 8, :]
                                     ).then_inc(kb_in[h % 2], 16)

                    @staticmethod
                    def first(sp):
                        for h in range(AHEAD):
                            HeadKeys.keys_bf16(sp, h)
                        for h in range(2):
                            HeadKeys.keys(sp, h)

                    @staticmethod
                    def load(sp, h, m_ready, per_head, s_ready):
                        if h + AHEAD < HEADS:
                            sp.wait_ge(m_ready, (h + 1) * per_head)
                            HeadKeys.keys_bf16(sp, h + 2)
                        if 1 <= h < HEADS - 1:
                            sp.wait_ge(s_ready, NT * h)
                            HeadKeys.keys(sp, h + 1)

                    @staticmethod
                    def wait_max(pe, h):
                        pe.wait_ge(kb_in[h % 2], 16 * (h // 2 + 1))

                    @staticmethod
                    def wait_keys(pe, h):
                        pe.wait_ge(k_in[h % 2], 16 * (h // 2 + 1))

                attention_heads(nc, core, tag, True, V, O,
                                q_max=lambda h, a, b: Qb[:, h, a:b], k_max=lambda h, a, b: Kb[:, h % 2, a:b],
                                keys=lambda h, c: K[0:SHIFT + 1, h % 2, c * P:(c + 1) * P],
                                queries=lambda h, a, b: Q[0:SHIFT + 1, h, a:b],
                                shift_row=lambda h: Q[SHIFT:SHIFT + 1, h, :], exp_kw=lambda c: {"scale": SC},
                                shift_dt=F32, masks=(idb[:], mQ[:], mK[:]), head_loads=HeadKeys)

        project_out(nc, core, tag, O, wo, None)


def store_output(nc, core, out_dram):
    stored = core.stored
    with nc.Block() as block:
        @block.sync
        def _(sp):
            sp.dma_start(out_dram.rearrange("(t p) d -> p t d", p=P), core.X[:]).then_inc(stored, 16)
            sp.wait_ge(stored, 16)


def build(nc, a, out):
    with ExitStack() as ctx:
        core = Core(nc, ctx)
        load_inputs(nc, core, a["x"])
        attention16(nc, core, "aa", a["a_wq"], a["a_wk"], a["a_wv"], a["a_wo"],
                    {"bqk": a["a_bqk"], "bv": a["a_bv"], "bo": a["a_bo"]},
                    {"justice": a["a_justice"], "order": a["a_order"]}, a["pos"])
        core.layer_done()
        ternary_scope = ExitStack()
        ternary = ternary_weights(nc, core, ternary_scope, a["f_up"], a["f_gate"], a["f_down"])
        ternary_ffn(nc, core, "f0", ternary)
        core.layer_done()
        gated_delta(nc, core, "gd", {k[2:]: a[k] for k in a if k.startswith("g_")})
        core.layer_done()
        norm_stage(nc, core, "n4")
        ternary_ffn(nc, core, "f1", ternary)
        ternary_scope.close()
        core.layer_done()
        attention16(nc, core, "ac", a["c_wq"], a["c_wk"], a["c_wv"], a["c_wo"], {"bo": a["c_bo"]}, None, None)
        core.layer_done()
        routed_layer(nc, core, "r0", {k[2:]: a[k] for k in a if k.startswith("r_")})
        core.layer_done()
        latent_attention(nc, core, "la", {k[2:]: a[k] for k in a if k.startswith("m_")})
        core.layer_done()
        routed_layer(nc, core, "r1", {k[2:]: a[k] for k in a if k.startswith("r_")})
        store_output(nc, core, out)


def lay_out(inputs):
    c = np.ascontiguousarray
    i = {k: np.asarray(v) for k, v in inputs.items()}
    a = {
        "x": c(i["L0_attn_a_hidden_states"][0]),
        "a_wq": c(i["L0_attn_a_Wq"].T), "a_wk": c(i["L0_attn_a_Wk"].T), "a_wv": c(i["L0_attn_a_Wv"].T),
        "a_wo": c(i["L0_attn_a_Wo"].T),
        "a_bqk": c(np.concatenate([i["L0_attn_a_bq"].reshape(KT, P).T, i["L0_attn_a_bk"].reshape(KT, P).T], axis=1)),
        "a_bv": c(i["L0_attn_a_bv"]),
        "a_bo": c(i["L0_attn_a_bo"]),
        "a_justice": c(i["L0_attn_a_justice_gate"]), "a_order": c(i["L0_attn_a_order_gate"]),
        "pos": c((np.arange(S, dtype=np.float32) / S).reshape(NT, P).T),
        "f_up": c(i["L0_ffn_W_up"].T), "f_gate": c(i["L0_ffn_W_gate"].T), "f_down": c(i["L0_ffn_W_down"].T),
    }
    cat = np.concatenate
    b = {k[len("L0_attn_b_"):]: v for k, v in i.items() if k.startswith("L0_attn_b_")}
    conv = cat([b["conv_wq"], b["conv_wk"], b["conv_wv"]], axis=0)
    a.update({
        "g_wqkv": c(cat([b["Wq"], b["Wk"], b["Wv"]], axis=1)),
        "g_wgab": c(cat([b["Wg"], b["Wa"], b["Wb"]], axis=1)),
        "g_conv": c(conv.reshape(NF, P, TAPS).transpose(1, 0, 2).reshape(P, NF * TAPS)),
        "g_wo": c(b["Wo"]), "g_nw": c(b["norm_weight"]), "g_dt": c(b["dt_bias"]), "g_alog": c(b["A_log"]),
        "g_eye": c(np.eye(T32, dtype=np.float32).reshape(-1)),
        "g_own": c(np.repeat(np.repeat(np.eye(4, dtype=np.float32), GK, axis=0), GV, axis=1)),
    })
    w = i["L1_attn_a_Wqkv"].reshape(HEADS, 3, HD, D)
    a.update({
        "c_wq": c(w[:, 0].reshape(D, D).T), "c_wk": c(w[:, 1].reshape(D, D).T), "c_wv": c(w[:, 2].reshape(D, D).T),
        "c_wo": c(i["L1_attn_a_Wproj"].T), "c_bo": c(i["L1_attn_a_bproj"]),
    })
    r = {k[len("L1_ffn_"):]: v for k, v in i.items() if k.startswith("L1_ffn_")}
    a.update({
        "r_gate": c(r["gate_w"].T), "r_up": c(r["w_up"].T), "r_gt": c(r["w_gate"].T), "r_down": c(r["w_down"].T),
        "r_upA": c(r["up_A"].reshape(P, D).T), "r_gtA": c(r["gate_A"].reshape(P, D).T),
        "r_upB": c(r["up_B"].transpose(0, 2, 1).reshape(P, DH)), "r_gtB": c(r["gate_B"].transpose(0, 2, 1).reshape(P, DH)),
        "r_dnA": c(r["down_A"].reshape(P, DH).T), "r_dnB": c(r["down_B"].transpose(0, 2, 1).reshape(P, D)),
        "r_expert": c(np.broadcast_to((np.arange(P) // RANK).astype(np.float32), (P, P))),
    })
    m = {k[len("L1_attn_b_"):]: v for k, v in i.items() if k.startswith("L1_attn_b_")}
    a.update({
        "m_w1": c(cat([m["Wqd"], m["Wkvd"], m["Wkr"]], axis=1)), "m_wqr": c(m["Wqr"]), "m_wqu": c(m["Wqu"]),
        "m_wku": c(m["Wku"]), "m_wvu": c(m["Wvu"]), "m_wo": c(m["Wo"]), "m_cs": rope_tables(), "m_zeros": np.zeros(S, np.float32),
    })
    return a


def rope_tables():
    freqs = 1.0 / 10000.0 ** (np.arange(0, RD, 2, dtype=np.float32) / RD)
    ang = np.tile(np.outer(np.arange(S, dtype=np.float32), freqs), (1, 2)).T
    return np.ascontiguousarray(np.concatenate([np.cos(ang), np.sin(ang)]).astype(np.float32))


def kernel(**inputs):
    import concourse.bacc as bacc
    from concourse.bass_utils import run_bass_kernel_spmd

    nc = bacc.Bacc("TRN2", target_bir_lowering=False, num_devices=1)
    arrays = lay_out(inputs)
    aps = {n: nc.dram_tensor(f"in_{n}", v.shape, mybir.dt.from_np(v.dtype), kind="ExternalInput").ap()
           for n, v in arrays.items()}
    out = nc.dram_tensor("out", (S, D), F32, kind="ExternalOutput").ap()
    build(nc, aps, out)
    r = run_bass_kernel_spmd(nc, [{f"in_{n}": v for n, v in arrays.items()}], core_ids=[0])
    return r.results[0]["out"].reshape(1, S, D)
```
